# Optimizing a Trainium2 kernel written in Bass

```python
import numpy as np
import jax
import jax.numpy as jnp

def _softmax(x, axis=-1):
    return jax.nn.softmax(x, axis=axis)

def _gelu(x):
    return jax.nn.gelu(x, approximate=True)

def _silu(x):
    return jax.nn.silu(x)

def _sigmoid(x):
    return jax.nn.sigmoid(x)

def _layernorm(x, axis=-1, eps=1e-05):
    m = jnp.mean(x, axis=axis, keepdims=True)
    v = jnp.var(x, axis=axis, keepdims=True)
    return (x - m) / jnp.sqrt(v + eps)

def _scatter_add(tgt, idx, src, axis=0):
    return tgt.at[idx].add(src)

def _segment_sum(src, seg, n):
    return jax.ops.segment_sum(src, seg, n)
kernel_name = 'mk_gnn_preln_d4_gnn_r32_f25be0'

def setup_inputs(seed: int=0):
    np.random.seed(seed)
    _w = jnp.asarray

    def _rec_inputs():
        import jax
        import jax.numpy as jnp
        _gk = jax.random.key(seed)
        x = -0.0005121 + 1.001 * jax.random.normal(jax.random.fold_in(_gk, 1), (50000, 64), jnp.float32)
        src = jax.random.randint(jax.random.fold_in(_gk, 2), (50000,), 0, 50000, jnp.int32)
        dst = jax.random.randint(jax.random.fold_in(_gk, 3), (50000,), 0, 50000, jnp.int32)
        _o = jnp.argsort(dst, stable=True)
        src = src[_o]
        dst = dst[_o]
        edge_attr_64 = 0.000156602 + 1.00005 * jax.random.normal(jax.random.fold_in(_gk, 12), (50000, 64), jnp.float32)
        return (x, src, dst, edge_attr_64)
    x, src, dst, edge_attr_64 = _rec_inputs()

    def _L0_gnn_setup():
        import jax, jax.numpy as jnp
        import numpy as np
        N_NODES = 50000
        N_EDGES = 25000
        D_IN = 64
        D_HID = 64
        D_OUT = 64
        key = jax.random.key(seed)
        ks = jax.random.split(key, 9)
        x = jax.random.normal(ks[0], (N_NODES, D_IN), dtype=jnp.float32)
        src = jax.random.randint(ks[1], (N_EDGES,), 0, N_NODES, dtype=jnp.int64)
        dst = jax.random.randint(ks[2], (N_EDGES,), 0, N_NODES, dtype=jnp.int64)
        s0 = 1.0 / np.sqrt(D_IN)
        s1 = 1.0 / np.sqrt(D_HID)
        W_self0 = jax.random.normal(ks[3], (D_IN, D_HID), dtype=jnp.float32) * s0
        W_neigh0 = jax.random.normal(ks[4], (D_IN, D_HID), dtype=jnp.float32) * s0
        b0 = jnp.zeros((D_HID,), dtype=jnp.float32)
        W_self1 = jax.random.normal(ks[5], (D_HID, D_OUT), dtype=jnp.float32) * s1
        W_neigh1 = jax.random.normal(ks[6], (D_HID, D_OUT), dtype=jnp.float32) * s1
        b1 = jnp.zeros((D_OUT,), dtype=jnp.float32)
        return {'x': x, 'src': src, 'dst': dst, 'W_self0': W_self0, 'W_neigh0': W_neigh0, 'b0': b0, 'W_self1': W_self1, 'W_neigh1': W_neigh1, 'b1': b1}
    _L0_gnn_all = _L0_gnn_setup()
    _L0_gnn_in = {k: v for k, v in _L0_gnn_all.items() if k in ('W_self0', 'W_neigh0', 'b0', 'W_self1', 'W_neigh1', 'b1')}
    del _L0_gnn_all

    def _L1_gnn_setup():
        import jax, jax.numpy as jnp
        import numpy as np
        N, E, D, H, C = (50000, 25000, 64, 2, 64)

        def _transformer_conv(x, src, dst, wq, bq, wk, bk, wv, bv, ws, bs):
            n = x.shape[0]
            q = (x @ wq + bq).reshape(n, H, C)
            k = (x @ wk + bk).reshape(n, H, C)
            v = (x @ wv + bv).reshape(n, H, C)
            qi = q[dst]
            kj = k[src]
            vj = v[src]
            alpha = jnp.einsum('ehc,ehc->eh', qi, kj) / jnp.sqrt(jnp.asarray(C, x.dtype))
            amax = jax.ops.segment_max(alpha, dst, num_segments=n)
            amax = jnp.where(jnp.isfinite(amax), amax, 0.0)
            ex = jnp.exp(alpha - amax[dst])
            denom = jax.ops.segment_sum(ex, dst, num_segments=n)
            a = ex / (denom[dst] + 1e-16)
            out = jax.ops.segment_sum(a[:, :, None] * vj, dst, num_segments=n)
            out = out.mean(axis=1)
            return out + x @ ws + bs
        key = jax.random.key(seed)
        ks = jax.random.split(key, 20)
        x = jax.random.normal(ks[0], (N, D), dtype=jnp.float32)
        edge_index = jax.random.randint(ks[1], (2, E), 0, N, dtype=jnp.int64)
        s = 1.0 / np.sqrt(D)

        def lin(k, din, dout):
            return jax.random.uniform(k, (din, dout), jnp.float32, -s, s)
        inp = {'x': x, 'edge_index': edge_index}
        i = 2
        for l, din in ((1, D), (2, C)):
            for nm, dout in (('wq', H * C), ('wk', H * C), ('wv', H * C), ('ws', C)):
                inp[f'l{l}_{nm}'] = lin(ks[i], din, dout)
                i += 1
                inp[f"l{l}_{nm.replace('w', 'b')}"] = jnp.zeros((dout,), jnp.float32)
        return inp
    _L1_gnn_all = _L1_gnn_setup()
    _L1_gnn_in = {k: v for k, v in _L1_gnn_all.items() if k in ('l1_wq', 'l1_bq', 'l1_wk', 'l1_bk', 'l1_wv', 'l1_bv', 'l1_ws', 'l1_bs', 'l2_wq', 'l2_bq', 'l2_wk', 'l2_bk', 'l2_wv', 'l2_bv', 'l2_ws', 'l2_bs')}
    del _L1_gnn_all

    def _L2_gnn_setup():
        import jax, jax.numpy as jnp
        import numpy as np
        N_NODES = 3125
        N_EDGES = 50000
        N_FEATS = 64
        HID1 = 128
        HID2 = 128

        def _gcn_conv(x, src, dst, norm, W, b, n_nodes):
            h = x @ W.T
            msg = h[src] * norm[:, None]
            out = jax.ops.segment_sum(msg, dst, num_segments=n_nodes)
            return out + b
        key = jax.random.key(seed)
        ks = jax.random.split(key, 8)
        x = jax.random.normal(ks[0], (N_NODES, N_FEATS), dtype=jnp.float32)
        edge_index = jax.random.randint(ks[1], (2, N_EDGES), 0, N_NODES, dtype=jnp.int64)
        W1 = jax.random.normal(ks[2], (HID1, N_FEATS), dtype=jnp.float32) * (1.0 / np.sqrt(N_FEATS))
        b1 = jnp.zeros((HID1,), dtype=jnp.float32)
        W2 = jax.random.normal(ks[3], (HID2, HID1), dtype=jnp.float32) * (1.0 / np.sqrt(HID1))
        b2 = jnp.zeros((HID2,), dtype=jnp.float32)
        W3 = jax.random.normal(ks[4], (N_FEATS, HID2), dtype=jnp.float32) * (1.0 / np.sqrt(HID2))
        b3 = jnp.zeros((N_FEATS,), dtype=jnp.float32)
        return {'x': x, 'edge_index': edge_index, 'W1': W1, 'b1': b1, 'W2': W2, 'b2': b2, 'W3': W3, 'b3': b3}
    _L2_gnn_all = _L2_gnn_setup()
    _L2_gnn_in = {k: v for k, v in _L2_gnn_all.items() if k in ('W1', 'b1', 'W2', 'b2', 'W3', 'b3')}
    del _L2_gnn_all

    def _L3_gnn_setup():
        import jax, jax.numpy as jnp
        import numpy as np
        N_NODES = 50000
        N_EDGES = 31250
        D_NODE = 64
        D_EDGE = 64

        def _layer_norm(x, gamma, beta, eps=1e-05):
            mu = jnp.mean(x, axis=-1, keepdims=True)
            var = jnp.var(x, axis=-1, keepdims=True)
            return (x - mu) * jax.lax.rsqrt(var + eps) * gamma + beta
        key = jax.random.key(seed)
        ks = jax.random.split(key, 12)
        d, de = (D_NODE, D_EDGE)
        din = 2 * d + de
        s = lambda f_in: 1.0 / np.sqrt(f_in)
        return {'node_feat': jax.random.normal(ks[0], (N_NODES, d), jnp.float32), 'edge_src': jax.random.randint(ks[1], (N_EDGES,), 0, N_NODES, jnp.int32), 'edge_dst': jax.random.randint(ks[2], (N_EDGES,), 0, N_NODES, jnp.int32), 'edge_feat': jax.random.normal(ks[3], (N_EDGES, de), jnp.float32), 'W_m1': jax.random.uniform(ks[4], (din, d), jnp.float32, -s(din), s(din)), 'b_m1': jax.random.uniform(ks[5], (d,), jnp.float32, -s(din), s(din)), 'W_m2': jax.random.uniform(ks[6], (d, d), jnp.float32, -s(d), s(d)), 'b_m2': jax.random.uniform(ks[7], (d,), jnp.float32, -s(d), s(d)), 'W_u1': jax.random.uniform(ks[8], (d, d), jnp.float32, -s(d), s(d)), 'b_u1': jax.random.uniform(ks[9], (d,), jnp.float32, -s(d), s(d)), 'W_u2': jax.random.uniform(ks[10], (d, d), jnp.float32, -s(d), s(d)), 'b_u2': jax.random.uniform(ks[11], (d,), jnp.float32, -s(d), s(d)), 'ln_gamma': jnp.ones((d,), jnp.float32), 'ln_beta': jnp.zeros((d,), jnp.float32)}
    _L3_gnn_all = _L3_gnn_setup()
    _L3_gnn_in = {k: v for k, v in _L3_gnn_all.items() if k in ('W_m1', 'b_m1', 'W_m2', 'b_m2', 'W_u1', 'b_u1', 'W_u2', 'b_u2', 'ln_gamma', 'ln_beta')}
    del _L3_gnn_all
    return {'x': x, 'src': src, 'dst': dst, 'edge_attr_64': edge_attr_64, 'L0_gnn_W_self0': _L0_gnn_in['W_self0'], 'L0_gnn_W_neigh0': _L0_gnn_in['W_neigh0'], 'L0_gnn_b0': _L0_gnn_in['b0'], 'L0_gnn_W_self1': _L0_gnn_in['W_self1'], 'L0_gnn_W_neigh1': _L0_gnn_in['W_neigh1'], 'L0_gnn_b1': _L0_gnn_in['b1'], 'L1_gnn_l1_wq': _L1_gnn_in['l1_wq'], 'L1_gnn_l1_bq': _L1_gnn_in['l1_bq'], 'L1_gnn_l1_wk': _L1_gnn_in['l1_wk'], 'L1_gnn_l1_bk': _L1_gnn_in['l1_bk'], 'L1_gnn_l1_wv': _L1_gnn_in['l1_wv'], 'L1_gnn_l1_bv': _L1_gnn_in['l1_bv'], 'L1_gnn_l1_ws': _L1_gnn_in['l1_ws'], 'L1_gnn_l1_bs': _L1_gnn_in['l1_bs'], 'L1_gnn_l2_wq': _L1_gnn_in['l2_wq'], 'L1_gnn_l2_bq': _L1_gnn_in['l2_bq'], 'L1_gnn_l2_wk': _L1_gnn_in['l2_wk'], 'L1_gnn_l2_bk': _L1_gnn_in['l2_bk'], 'L1_gnn_l2_wv': _L1_gnn_in['l2_wv'], 'L1_gnn_l2_bv': _L1_gnn_in['l2_bv'], 'L1_gnn_l2_ws': _L1_gnn_in['l2_ws'], 'L1_gnn_l2_bs': _L1_gnn_in['l2_bs'], 'L2_gnn_W1': _L2_gnn_in['W1'], 'L2_gnn_b1': _L2_gnn_in['b1'], 'L2_gnn_W2': _L2_gnn_in['W2'], 'L2_gnn_b2': _L2_gnn_in['b2'], 'L2_gnn_W3': _L2_gnn_in['W3'], 'L2_gnn_b3': _L2_gnn_in['b3'], 'L3_gnn_W_m1': _L3_gnn_in['W_m1'], 'L3_gnn_b_m1': _L3_gnn_in['b_m1'], 'L3_gnn_W_m2': _L3_gnn_in['W_m2'], 'L3_gnn_b_m2': _L3_gnn_in['b_m2'], 'L3_gnn_W_u1': _L3_gnn_in['W_u1'], 'L3_gnn_b_u1': _L3_gnn_in['b_u1'], 'L3_gnn_W_u2': _L3_gnn_in['W_u2'], 'L3_gnn_b_u2': _L3_gnn_in['b_u2'], 'L3_gnn_ln_gamma': _L3_gnn_in['ln_gamma'], 'L3_gnn_ln_beta': _L3_gnn_in['ln_beta']}

def reference(x, src, dst, edge_attr_64, L0_gnn_W_self0, L0_gnn_W_neigh0, L0_gnn_b0, L0_gnn_W_self1, L0_gnn_W_neigh1, L0_gnn_b1, L1_gnn_l1_wq, L1_gnn_l1_bq, L1_gnn_l1_wk, L1_gnn_l1_bk, L1_gnn_l1_wv, L1_gnn_l1_bv, L1_gnn_l1_ws, L1_gnn_l1_bs, L1_gnn_l2_wq, L1_gnn_l2_bq, L1_gnn_l2_wk, L1_gnn_l2_bk, L1_gnn_l2_wv, L1_gnn_l2_bv, L1_gnn_l2_ws, L1_gnn_l2_bs, L2_gnn_W1, L2_gnn_b1, L2_gnn_W2, L2_gnn_b2, L2_gnn_W3, L2_gnn_b3, L3_gnn_W_m1, L3_gnn_b_m1, L3_gnn_W_m2, L3_gnn_b_m2, L3_gnn_W_u1, L3_gnn_b_u1, L3_gnn_W_u2, L3_gnn_b_u2, L3_gnn_ln_gamma, L3_gnn_ln_beta):
    import jax
    import jax.numpy as jnp

    def _L0_gnn_ref(x, src, dst, W_self0, W_neigh0, b0, W_self1, W_neigh1, b1):
        import jax, jax.numpy as jnp
        import numpy as np
        N_NODES = 50000
        N_EDGES = 25000
        D_IN = 64
        D_HID = 64
        D_OUT = 64
        n = x.shape[0]
        deg = jax.ops.segment_sum(jnp.ones(src.shape[0], dtype=x.dtype), dst, num_segments=n)
        inv_deg = (1.0 / jnp.maximum(deg, 1.0))[:, None]

        def sage_mean(h, W_self, W_neigh, b):
            agg = jax.ops.segment_sum(h[src], dst, num_segments=n)
            neigh = agg * inv_deg
            return h @ W_self + neigh @ W_neigh + b
        h = jax.nn.relu(sage_mean(x, W_self0, W_neigh0, b0))
        h = jax.nn.relu(h)
        h = sage_mean(h, W_self1, W_neigh1, b1)
        return h

    def _L1_gnn_ref(x, edge_index, l1_wq, l1_bq, l1_wk, l1_bk, l1_wv, l1_bv, l1_ws, l1_bs, l2_wq, l2_bq, l2_wk, l2_bk, l2_wv, l2_bv, l2_ws, l2_bs):
        import jax, jax.numpy as jnp
        import numpy as np
        N, E, D, H, C = (50000, 25000, 64, 2, 64)

        def _transformer_conv(x, src, dst, wq, bq, wk, bk, wv, bv, ws, bs):
            n = x.shape[0]
            q = (x @ wq + bq).reshape(n, H, C)
            k = (x @ wk + bk).reshape(n, H, C)
            v = (x @ wv + bv).reshape(n, H, C)
            qi = q[dst]
            kj = k[src]
            vj = v[src]
            alpha = jnp.einsum('ehc,ehc->eh', qi, kj) / jnp.sqrt(jnp.asarray(C, x.dtype))
            amax = jax.ops.segment_max(alpha, dst, num_segments=n)
            amax = jnp.where(jnp.isfinite(amax), amax, 0.0)
            ex = jnp.exp(alpha - amax[dst])
            denom = jax.ops.segment_sum(ex, dst, num_segments=n)
            a = ex / (denom[dst] + 1e-16)
            out = jax.ops.segment_sum(a[:, :, None] * vj, dst, num_segments=n)
            out = out.mean(axis=1)
            return out + x @ ws + bs
        src, dst = (edge_index[0], edge_index[1])
        h = _transformer_conv(x, src, dst, l1_wq, l1_bq, l1_wk, l1_bk, l1_wv, l1_bv, l1_ws, l1_bs)
        h = _transformer_conv(h, src, dst, l2_wq, l2_bq, l2_wk, l2_bk, l2_wv, l2_bv, l2_ws, l2_bs)
        return h

    def _L2_gnn_ref(x, edge_index, W1, b1, W2, b2, W3, b3):
        import jax, jax.numpy as jnp
        import numpy as np
        N_NODES = 3125
        N_EDGES = 50000
        N_FEATS = 64
        HID1 = 128
        HID2 = 128

        def _gcn_conv(x, src, dst, norm, W, b, n_nodes):
            h = x @ W.T
            msg = h[src] * norm[:, None]
            out = jax.ops.segment_sum(msg, dst, num_segments=n_nodes)
            return out + b
        n = x.shape[0]
        loop = jnp.arange(n, dtype=edge_index.dtype)
        src = jnp.concatenate([edge_index[0], loop])
        dst = jnp.concatenate([edge_index[1], loop])
        deg = jax.ops.segment_sum(jnp.ones(dst.shape, dtype=x.dtype), dst, num_segments=n)
        dinv = jnp.where(deg > 0, jax.lax.rsqrt(deg), 0.0)
        norm = dinv[src] * dinv[dst]
        h = jax.nn.relu(_gcn_conv(x, src, dst, norm, W1, b1, n))
        h = jax.nn.relu(_gcn_conv(h, src, dst, norm, W2, b2, n))
        h = _gcn_conv(h, src, dst, norm, W3, b3, n)
        return jax.nn.softmax(h, axis=1)

    def _L3_gnn_ref(node_feat, edge_src, edge_dst, edge_feat, W_m1, b_m1, W_m2, b_m2, W_u1, b_u1, W_u2, b_u2, ln_gamma, ln_beta):
        import jax, jax.numpy as jnp
        import numpy as np
        N_NODES = 50000
        N_EDGES = 31250
        D_NODE = 64
        D_EDGE = 64

        def _layer_norm(x, gamma, beta, eps=1e-05):
            mu = jnp.mean(x, axis=-1, keepdims=True)
            var = jnp.var(x, axis=-1, keepdims=True)
            return (x - mu) * jax.lax.rsqrt(var + eps) * gamma + beta
        msg_input = jnp.concatenate([node_feat[edge_src], node_feat[edge_dst], edge_feat], axis=-1)
        h = jax.nn.silu(msg_input @ W_m1 + b_m1)
        messages = h @ W_m2 + b_m2
        aggregated = jax.ops.segment_sum(messages, edge_dst, num_segments=node_feat.shape[0])
        upd = jax.nn.silu(aggregated @ W_u1 + b_u1) @ W_u2 + b_u2
        return _layer_norm(node_feat + upd, ln_gamma, ln_beta)
    edge_index = jnp.stack([src, dst])
    h = jnp.maximum(_layernorm(x, axis=-1), 0.0)
    x = x + _L0_gnn_ref(h, src, dst, L0_gnn_W_self0, L0_gnn_W_neigh0, L0_gnn_b0, L0_gnn_W_self1, L0_gnn_W_neigh1, L0_gnn_b1)
    h = jnp.maximum(_layernorm(x, axis=-1), 0.0)
    x = x + _L1_gnn_ref(h, edge_index, L1_gnn_l1_wq, L1_gnn_l1_bq, L1_gnn_l1_wk, L1_gnn_l1_bk, L1_gnn_l1_wv, L1_gnn_l1_bv, L1_gnn_l1_ws, L1_gnn_l1_bs, L1_gnn_l2_wq, L1_gnn_l2_bq, L1_gnn_l2_wk, L1_gnn_l2_bk, L1_gnn_l2_wv, L1_gnn_l2_bv, L1_gnn_l2_ws, L1_gnn_l2_bs)
    h = jnp.maximum(_layernorm(x, axis=-1), 0.0)
    x = x + _L2_gnn_ref(h, edge_index, L2_gnn_W1, L2_gnn_b1, L2_gnn_W2, L2_gnn_b2, L2_gnn_W3, L2_gnn_b3)
    h = jnp.maximum(_layernorm(x, axis=-1), 0.0)
    x = x + _L3_gnn_ref(h, src, dst, edge_attr_64, L3_gnn_W_m1, L3_gnn_b_m1, L3_gnn_W_m2, L3_gnn_b_m2, L3_gnn_W_u1, L3_gnn_b_u1, L3_gnn_W_u2, L3_gnn_b_u2, L3_gnn_ln_gamma, L3_gnn_ln_beta)
    return x

_drawn_inputs = setup_inputs


def setup_inputs(seed=0):
    import zlib

    import numpy as np

    out = dict(_drawn_inputs(seed))
    spreads = {'L0_gnn_b0': (0.0, 0.1),
     'L0_gnn_b1': (0.0, 0.1),
     'L1_gnn_l1_bq': (0.0, 2.0),
     'L1_gnn_l1_bk': (0.0, 2.0),
     'L1_gnn_l1_bv': (0.0, 0.289),
     'L1_gnn_l1_bs': (0.0, 0.1),
     'L1_gnn_l2_bq': (0.0, 2.0),
     'L1_gnn_l2_bk': (0.0, 2.0),
     'L1_gnn_l2_bv': (0.0, 0.1),
     'L1_gnn_l2_bs': (0.0, 0.1),
     'L2_gnn_b1': (0.0, 0.8),
     'L2_gnn_b2': (0.0, 2.0),
     'L2_gnn_b3': (0.0, 2.0),
     'L3_gnn_ln_gamma': (1.0, 0.2),
     'L3_gnn_ln_beta': (0.0, 0.1)}
    factors = {'edge_attr_64': 4.231,
     'L1_gnn_l1_wq': 8.0,
     'L1_gnn_l1_wk': 8.0,
     'L1_gnn_l2_wq': 8.0,
     'L1_gnn_l2_wk': 8.0,
     'L2_gnn_W1': 8.0,
     'L2_gnn_W2': 8.0,
     'L2_gnn_W3': 8.0,
     'L3_gnn_W_m1': 2.752,
     'L3_gnn_b_m1': 8.0,
     'L3_gnn_b_m2': 2.841,
     'L3_gnn_b_u1': 3.22}
    for name, (base, spread) in spreads.items():
        noise = np.random.default_rng([zlib.crc32(name.encode()), seed]).standard_normal(out[name].shape)
        drawn = base * np.exp(spread * noise) if base else spread * noise
        out[name] = jnp.asarray(drawn.astype(out[name].dtype))
    for name, factor in factors.items():
        out[name] = (out[name] * factor).astype(out[name].dtype)
    return out
```

```python
import concourse.bass as bass
from concourse import mybir
from contextlib import ExitStack

N = 50000
E = 50000
D = 64
DH = 128
NT = 100
W = 128
T = N // NT
G = 5
GROUPS = T // G
HI, LO = 20, 25
HB = 8
CH = 125
EPAD = 391 * W + W
PADDST = 1 << 20
BIG = 1.0e30
FLOOR = -1.0e29

F32 = mybir.dt.float32
BF16 = mybir.dt.bfloat16
I32 = mybir.dt.int32
ALU = mybir.AluOpType
ACT = mybir.ActivationFunctionType
AX = mybir.AxisListType.X

LN = "red cen sq var ln rstd nrm "
CONV = ("oh he tr_h ht tr_o oht mm_g gt exp_g prod dot tr_a fwd seg sub exp tr_p wm agg den rec state_in state tr ct mm ")
PASS_STAGES = {
    0: LN,
    1: "oh agg deg max rec ev state tr ct mm out",
    2: "oh agg ev state tr ct mm xadd " + LN,
    3: CONV + "out",
    4: CONV + "xadd rsc " + LN,
    5: "oh agg ev state tr ct mm out",
    6: "oh agg ev state tr ct mm relu mm2 out",
    7: "oh agg ev state pre max sub exp den rec prob xadd tr ct mm out " + LN,
    8: "oh tr_h ht tr_o oht mm_y yt tr_e et mm_z abs e1 e2 lsig e3 silu agg ev state tr ct mm "
       "ub uabs u1 u2 ulsig u3 usilu mm2 pre gam bet xadd " + LN,
}
NAMES = sorted({n for v in PASS_STAGES.values() for n in v.split()})
LOADS = {0: "x", 1: "idx hs", 2: "idx hs x", 3: "idx hs flag", 4: "idx hs flag x", 5: "idx hs", 6: "idx hs",
         7: "idx hs x", 8: "idx hs ea x"}
STORES = {0: "a", 1: "a", 2: "a b", 3: "a", 4: "a b", 5: "a", 6: "a", 7: "a b c", 8: "b"}
EDGE_PASSES = range(1, 9)


def rank(table, p, name):
    return sum(name in table[q].split() for q in range(p))


def start(p, name):
    return 2 + (GROUPS + 2 * (name == "oh")) * rank(PASS_STAGES, p, name)


def done(p, name, g, par):
    return g + (start(p, name) + par + 1)


def before(p, name, g, par):
    return g + (start(p, name) + par - 1)


def ended(table, p, name, per):
    return per * (GROUPS // 2) * rank(table, p + 1, name)


def loaded(p, name, g):
    return 8 * g + (8 * GROUPS * rank(LOADS, p, name) + 16)


def gathered_at(p, g):
    return 8 * G * g + (8 * G * GROUPS * (p - 1) + 32 * G)


def gathered_before(p, g):
    return 8 * G * g + (8 * G * GROUPS * (p - 1) + 16 * G)


def stored_before(p, name, g):
    return 8 * g + (8 * GROUPS * rank(STORES, p, name) + 16)


def build(nc, a, out):
    ctx = ExitStack()
    with ctx:
        ctx.enter_context(nc.allow_non_contiguous_dma(reason="short index columns and biases"))

        def sb(name, shape, dt=F32):
            return ctx.enter_context(nc.sbuf_tensor(name, shape, dt))

        def sem(name):
            return ctx.enter_context(nc.semaphore(name))

        def dram(name, shape, dt=F32):
            return nc.dram_tensor(name, shape, dt, kind="Internal").ap()

        srcpad = dram("srcpad", (EPAD // W, W), I32)
        dstpad = dram("dstpad", (EPAD // W, W), I32)
        eapad = dram("eapad", (EPAD, D))
        cnt_d = dram("cnt_d", (T,))
        srow_d = dram("srow_d", (T,), I32)
        flag_d = dram("flag_d", (T, 2, W))
        Ht = {n: dram(f"h{n}", (N, DH if n == 5 else D)) for n in range(9)}
        X1 = dram("x1", (N, D))
        X2 = dram("x2", (N, D))
        X3 = dram("x3", (N, D))
        prime_d = dram("prime_d", (16, 16))

        def tiles_of(table):
            return table.rearrange("(t p) f -> p t f", p=NT)

        iota_i = sb("iota_i", [128, T], I32)
        iota_f = sb("iota_f", [128, T])
        base_f = sb("base_f", [128, T])
        pcol_i = sb("pcol_i", [128, 1], I32)
        tbase_i = sb("tbase_i", [128, T // CH], I32)
        tbase = sb("tbase", [128, T // CH])
        ident = sb("ident", [128, 128])
        tri = sb("tri", [128, 128])
        ones = sb("ones", [128, 128])
        epsc = sb("epsc", [128, 2])
        srcw = sb("srcw", [128, T], I32)
        drel = sb("drel", [128, T + 2 * G])
        deg = sb("deg", [NT, T])
        invdeg = sb("invdeg", [NT, T])
        dinv = sb("dinv", [NT, T])
        hasedge = sb("hasedge", [NT, T])
        maxc_f = sb("maxc_f", [1, GROUPS // 2])
        maxc = sb("maxc", [1, GROUPS // 2], I32)
        srow = sb("srow", [1, T], I32)
        sage_w = [sb(f"sage_w{l}", [128, D]) for l in range(2)]
        brow = {n: sb(f"brow_{n}", [1, G, w]) for n, w in (("s0", D), ("s1", D), ("g1", DH))}
        bias_b = {n: sb(f"bias_{n}", [NT, D]) for n in ("g3", "gamma", "beta")}
        cw = sb("cw", [65, 2, 4, 128])
        cwT = sb("cwT", [64, 2, 2, 2, 65])
        qk = sb("qk", [66, 2, 2, 65])
        vw = sb("vw", [128, 2, D])
        sw = sb("sw", [66, 2, D])
        bvrow = sb("bvrow", [1, 2, 2, D])
        swrow = sb("swrow", [1, 2, D])
        g1w = sb("g1w", [128, D])
        g2w = sb("g2w", [128, 128])
        g3w = sb("g3w", [64, 128])
        g1t = sb("g1t", [64, 128])
        g2t = sb("g2t", [128, 128])
        g3t = sb("g3t", [128, D])
        g2b = sb("g2b", [128, 1])
        m1w = sb("m1w", [65, 3, D])
        m2w = sb("m2w", [65, D])
        m2T = sb("m2T", [64, 65])
        u1w = sb("u1w", [64, D])
        u1b = sb("u1b", [64, 1])
        mu = sb("mu", [65, D])
        u2w = sb("u2w", [65, D])

        nidx = sb("nidx", [128, 2, G], I32)
        m65 = sb("m65", [128, 2, G, 65])
        m128 = sb("m128", [128, 2, G, 128])
        oh = sb("oh", [128, 2, G, NT])
        ohT = sb("ohT", [NT, 2, G * W])
        c128 = sb("c128", [NT, 2, G, 128])
        c65 = sb("c65", [NT, 2, G, 65])
        ctb = sb("ctb", [128, 2, G * NT])
        hs66 = sb("hs66", [NT, 2, G, 66])
        hsb = sb("hsb", [NT, 2, G * 128])
        xres = sb("xres", [NT, 2, G, D])
        w0, w1, w2, w3 = (sb(f"w{k}", [NT, 2, G, D]) for k in range(4))
        w3b = sb("w3b", [NT, 2, G, DH])
        wc = sb("wc", [NT, 2, G, D])
        small = sb("small", [NT, 2, 8, 2 * G])
        hT = sb("hT", [66, 2, G * NT])
        gS = sb("gS", [NT, 2, 2, G * 65])
        pr = sb("pr", [128, 2, 2, G, 65])
        al = sb("al", [128, 2, 2 * G])
        rowm = sb("rowm", [2 * G, 2, 4, W])
        flags = sb("flags", [2 * G, 2, 2, W])
        h6T = sb("h6T", [128, 2, G * NT])
        eT = sb("eT", [64, 2, G * W])
        ea = sb("ea", [128, 2, G, D])
        ysb = sb("ysb", [NT, 2, G * D])
        z1, z2 = (sb(f"z{k}", [128, 2, G * D]) for k in (1, 2))
        sg = sb("sg", [128, 2, G, 65])
        uz, ue = (sb(f"u{k}", [64, 2, G * NT]) for k in "ze")
        usT = sb("usT", [65, 2, G * NT])
        xsrc = sb("xsrc", [128, G], I32)
        xdst = sb("xdst", [128, G], I32)
        xdf = sb("xdf", [128, G])
        xrow = sb("xrow", [2 * G, W], I32)
        xrf = sb("xrf", [2 * G, W])
        xflag = sb("xflag", [2 * G, 2, W])
        xm65 = sb("xm65", [128, G, 65])
        xm128 = sb("xm128", [128, G, 128])
        xoh = sb("xoh", [128, G, NT])
        xt = sb("xt", [NT, G * 130])
        xstate = sb("xstate", [NT, G * 130])
        xea = sb("xea", [128, G, D])
        xcol = sb("xcol", [128, 3, 2 * G])
        xs = sb("xs", [NT, 6, 2 * G])
        fillc = sb("fillc", [128, 2, 16], I32)
        fillz = sb("fillz", [128, 2 * D])
        zb = sb("zb", [128, 128], BF16)
        dlist = sb("dlist", [CH, E // CH], I32)
        dwork = sb("dwork", [CH, E // CH], I32)
        scol_i = sb("scol_i", [CH, T // CH], I32)
        wsrc = sb("wsrc", [CH, T // CH, W], I32)
        wdst = sb("wdst", [CH, T // CH, W], I32)
        drelw = sb("drelw", [CH, T // CH, W])
        wsf = sb("wsf", [CH, T // CH, W])
        flagw = sb("flagw", [CH, T // CH, 2, W])
        hq = [sb(f"hq{k}", [CH, E // CH]) for k in range(4)]
        ohh = sb("ohh", [CH, 2, HB, HI], BF16)
        ohl = sb("ohl", [CH, 2, HB, LO], BF16)
        cnt_s = sb("cnt_s", [HI, LO])
        cntc = sb("cntc", [CH, T // CH])
        crow = sb("crow", [1, T])

        P = ctx.enter_context(nc.psum_tensor("psum_all", [128, 8 * 512], F32))

        def pb(k, cols=512, off=0):
            return P[:, k * 512 + off:k * 512 + off + cols]

        def tiles(x, f):
            return x.rearrange("p (u f) -> p u f", f=f)

        def two_banks(k, rows, cols):
            return P[0:rows, k * 512:(k + 2) * 512].rearrange("p (h c) -> p h c", h=2)[:, :, 0:cols]

        S = {n: sem(f"st_{n}") for n in NAMES}
        L = {n: [sem(f"loaded_{n}{par}") for par in range(2)] for n in ("idx", "hs", "x", "flag", "ea")}
        ST = {n: [sem(f"stored_{n}{par}") for par in range(2)] for n in "abc"}
        gathered = [sem(f"gathered{par}") for par in range(2)]
        s_load = sem("weights_loaded")
        w_pe = sem("weights_pe")
        w_dve = sem("weights_dve")
        s_vrow = sem("mean_bv_moved")
        s_list = sem("edge_list_loaded")
        s_pad = sem("edge_lists_padded")
        s_ea = sem("edge_features_padded")
        s_fill = sem("fill_ready")
        s_sw = sem("small_products")
        pool_c = sem("pool_consts")
        s_dve = sem("dve_setup")
        s_act = sem("act_setup")
        s_pe = sem("pe_setup")
        q_ready = sem("hist_onehots_ready")
        q_used = sem("hist_onehots_used")
        s_cnt = sem("counts_moved")
        s_srow = sem("window_starts_moved")
        s_flag = sem("flags_stored")
        s_win = sem("windows_gathered")
        tables = sem("tables_ready")
        held = sem("held")
        primed = sem("stages_primed")
        x_in = sem("further_inputs")
        x_g = sem("further_gathered")
        baton = {p: sem(f"baton{p}") for p in EDGE_PASSES}

        SELF = {1: Ht[0], 2: Ht[1], 3: Ht[2], 4: Ht[3], 5: Ht[4], 6: Ht[5], 7: Ht[6], 8: Ht[7]}
        TABLE = dict(SELF)
        TABLE[8] = Ht[8]
        XIN = {0: a["x"], 2: a["x"], 4: X1, 7: X2, 8: X3}
        OUTA = {p: Ht[p] for p in range(8)}
        OUTB = {2: X1, 4: X2, 7: X3, 8: out}
        OUTC = {7: Ht[8]}

        def pass_written(eng, p):
            for n in STORES[p].split():
                for par in range(2):
                    eng.wait_ge(ST[n][par], 16 + ended(STORES, p, n, 16))

        def hold(eng):
            eng.sem_inc(held, 1)

        XSTEPS = {1: (1, 11), 2: (0, 8), 3: (7, 39), 4: (7, 39), 5: (0, 8), 6: (0, 8), 7: (0, 8), 8: (0, 18)}

        def further(eng, p, xb, xmaxc, body, prepare=None):
            first, each = XSTEPS[p]
            hold(eng)
            with eng.If(xmaxc > W):
                if prepare is not None:
                    prepare()
                    hold(eng)
                if first:
                    eng.reg_add(xb, xb, first)
                with eng.Fori(W, xmaxc, W) as j:
                    body(j)
                    hold(eng)
                    eng.reg_add(xb, xb, each)

        def at(eng, xb, k):
            return eng.snap(xb, min_val=1, max_val=1 << 30) + k

        block = ctx.enter_context(nc.Block())

        @block.sync
        def _(sp):
            sp.dma_start(dlist[:, :], a["dst"].rearrange("(p t) -> p t", p=CH)).then_inc(s_list, 16)
            for l in range(2):
                sp.dma_start(sage_w[l][0:D, :], a[f"L0_gnn_W_neigh{l}"]).then_inc(s_load, 16)
                sp.dma_start(sage_w[l][D:128, :], a[f"L0_gnn_W_self{l}"]).then_inc(s_load, 16)
                for k, n in enumerate("qkvs"):
                    wide = D if n == "s" else DH
                    sp.dma_start(cw[0:D, l, k, 0:wide], a[f"L1_gnn_l{l + 1}_w{n}"]).then_inc(s_load, 16)
                    sp.dma_start(cw[D:D + 1, l, k, 0:wide],
                                 a[f"L1_gnn_l{l + 1}_b{n}"].rearrange("(o n) -> o n", o=1)).then_inc(s_load, 16)
                for h in range(2):
                    sp.dma_start(vw[h * D:(h + 1) * D, l, :], a[f"L1_gnn_l{l + 1}_wv"][:, h * D:(h + 1) * D])\
                      .then_inc(s_load, 16)
                sp.dma_start(bvrow[0:1, l, :, :], a[f"L1_gnn_l{l + 1}_bv"].rearrange("(o h n) -> o h n", o=1, h=2))\
                  .then_inc(s_load, 16)
            for n, key in (("s0", "L0_gnn_b0"), ("s1", "L0_gnn_b1"), ("g1", "L2_gnn_b1")):
                wide = DH if n == "g1" else D
                sp.dma_start(brow[n][0:1, :, :], a[key].rearrange("(o u n) -> o u n", o=1, u=1)
                             .broadcast_to([1, G, wide])).then_inc(s_load, 16)
            for n, key in (("g3", "L2_gnn_b3"), ("gamma", "L3_gnn_ln_gamma"), ("beta", "L3_gnn_ln_beta")):
                sp.dma_start(bias_b[n][:, :], a[key].rearrange("(o n) -> o n", o=1).broadcast_to([NT, D]))\
                  .then_inc(s_load, 16)
            sp.dma_start(g1w[:, :], a["L2_gnn_W1"]).then_inc(s_load, 16)
            sp.dma_start(g2w[:, :], a["L2_gnn_W2"]).then_inc(s_load, 16)
            sp.dma_start(g3w[:, :], a["L2_gnn_W3"]).then_inc(s_load, 16)
            sp.dma_start(g2b[:, :], a["L2_gnn_b2"].rearrange("(n o) -> n o", o=1)).then_inc(s_load, 16)
            for k in range(3):
                sp.dma_start(m1w[0:D, k, :], a["L3_gnn_W_m1"][k * D:(k + 1) * D, :]).then_inc(s_load, 16)
            sp.dma_start(m1w[D:D + 1, 1, :], a["L3_gnn_b_m1"].rearrange("(o n) -> o n", o=1)).then_inc(s_load, 16)
            sp.dma_start(m2w[0:D, :], a["L3_gnn_W_m2"]).then_inc(s_load, 16)
            sp.dma_start(m2w[D:D + 1, :], a["L3_gnn_b_m2"].rearrange("(o n) -> o n", o=1)).then_inc(s_load, 16)
            sp.dma_start(u1w[:, :], a["L3_gnn_W_u1"]).then_inc(s_load, 16)
            sp.dma_start(u1b[:, :], a["L3_gnn_b_u1"].rearrange("(n o) -> n o", o=1)).then_inc(s_load, 16)
            sp.dma_start(u2w[0:D, :], a["L3_gnn_W_u2"]).then_inc(s_load, 16)
            sp.dma_start(u2w[D:D + 1, :], a["L3_gnn_b_u2"].rearrange("(o n) -> o n", o=1)).then_inc(s_load, 16)
            for pad, lst in ((srcpad, a["src"]), (dstpad, a["dst"])):
                sp.dma_start(pad.rearrange("a b -> (a b)")[0:E].rearrange("(p t) -> p t", p=80),
                             lst.rearrange("(p t) -> p t", p=80)).then_inc(s_pad, 16)
            sp.wait_ge(s_fill, 3)
            for pad, fill in ((srcpad, 0), (dstpad, 1)):
                sp.dma_start(pad.rearrange("a b -> (a b)")[E:EPAD].rearrange("(p t) -> p t", p=16),
                             fillc[0:16, fill, 0:(EPAD - E) // 16]).then_inc(s_pad, 16)
            sp.dma_start(eapad[E:EPAD, :].rearrange("(p t) f -> p (t f)", p=88), fillz[0:88, :]).then_inc(s_pad, 16)
            sp.wait_ge(w_dve, 1)
            sp.dma_start(sw[D + 1:D + 2, :, :], swrow[0:1, :, :]).then_inc(s_vrow, 16)
            sp.wait_ge(s_dve, CNT_DONE)
            sp.dma_start(cnt_d.rearrange("(h l) -> h l", l=LO), cnt_s[:, :]).then_inc(s_cnt, 16)
            sp.wait_ge(s_cnt, 16)
            sp.dma_start(cntc[:, :], cnt_d.rearrange("(c p) -> p c", p=CH)).then_inc(s_cnt, 16)
            sp.dma_start(crow[:, :], cnt_d.rearrange("(o t) -> o t", o=1)).then_inc(s_cnt, 16)
            sp.wait_ge(s_dve, SCOL_DONE)
            sp.dma_start(srow_d.rearrange("(c p) -> p c", p=CH), scol_i[:, :]).then_inc(s_srow, 16)
            sp.wait_ge(s_srow, 16)
            sp.dma_start(srow[:, :], srow_d.rearrange("(o t) -> o t", o=1)).then_inc(s_srow, 16)
            sp.dma_start(eapad[0:E, :].rearrange("(p t) f -> p (t f)", p=80),
                         a["edge_attr_64"].rearrange("(p t) f -> p (t f)", p=80)).then_inc(s_ea, 16)
            sp.wait_ge(s_dve, FLAG_DONE)
            sp.dma_start(flag_d.rearrange("(c p) s w -> p c s w", p=CH), flagw[:, :, :, :]).then_inc(s_flag, 16)
            sp.wait_ge(s_flag, 16)
            sp.wait_ge(s_srow, 32)
            sp.wait_ge(tables, 1)
            sp.wait_ge(primed, 4)

            xin = sp.alloc_register("xin")
            sp.reg_mov(xin, 0)
            xb = sp.alloc_register("xb_sp")
            st = sp.alloc_register("xstart")
            srcflat = srcpad.rearrange("a (b o) -> (a b) o", o=1)
            dstflat = dstpad.rearrange("a (b o) -> (a b) o", o=1)
            for p in range(NPASS):
                if p:
                    pass_written(sp, p - 1)
                    sp.reg_mov(xb, 1)
                    sp.sem_inc(baton[p], 1)
                if p == 8:
                    sp.wait_ge(s_ea, 16)
                names = LOADS[p].split()
                with sp.Fori(0, GROUPS // 2) as i:
                    g = i * 2
                    if p:
                        xmaxc = sp.value_load(maxc[0:1, bass.ds(i, 1)], min_val=0, max_val=E)
                    for par in range(2):
                        if "idx" in names:
                            sp.wait_ge(gathered[par], gathered_before(p, g))
                            sp.dma_start(nidx[:, par, :], srcw[:, bass.ds(g * G + par * G, G)]).then_inc(L["idx"][par], 16)
                    for par in range(2):
                        tile0 = bass.ds(g * G + par * G, G)
                        if "hs" in names:
                            table = tiles_of(SELF[p])[:, tile0, :]
                            reader = {1: "tr", 2: "tr", 3: "tr_h", 4: "tr_h", 5: "agg", 6: "agg", 7: "agg", 8: "pre"}[p]
                            into = {1: c128[:, par, :, D:128], 2: c128[:, par, :, D:128], 3: hs66[:, par, :, 0:D],
                                    4: hs66[:, par, :, 0:D], 5: tiles(hsb[:, par, 0:G * D], D),
                                    6: tiles(hsb[:, par, :], DH), 7: tiles(hsb[:, par, 0:G * D], D),
                                    8: hs66[:, par, :, 0:D]}[p]
                            sp.wait_ge(S[reader], before(p, reader, g, par))
                            sp.dma_start(into, table).then_inc(L["hs"][par], 16)
                        if "flag" in names:
                            sp.wait_ge(S["seg"], before(p, "seg", g, par))
                            for h in range(2):
                                sp.dma_start(flags[h * G:(h + 1) * G, par, :, :], flag_d[tile0, :, :])\
                                  .then_inc(L["flag"][par], 16)
                        if "ea" in names:
                            sp.wait_ge(S["tr_e"], before(p, "tr_e", g, par))
                            hold(sp)
                            for u in range(G):
                                s0 = sp.value_load(srow[0:1, bass.ds(g * G + (par * G + u), 1)], min_val=0, max_val=E)
                                sp.dma_start(ea[:, par, u, :], eapad[bass.ds(s0, W), :]).then_inc(L["ea"][par], 16)
                        if "x" in names:
                            reader = "cen" if p == 0 else "xadd"
                            sp.wait_ge(S[reader], before(p, reader, g, par))
                            sp.dma_start(xres[:, par, :, :], tiles_of(XIN[p])[:, tile0, :]).then_inc(L["x"][par], 16)
                    if p:
                        for par in range(2):
                            def body(j):
                                sp.wait_ge(baton[p], at(sp, xb, 0))
                                hold(sp)
                                loads = 0
                                for u in range(G):
                                    s0 = sp.value_load(srow[0:1, bass.ds(g * G + (par * G + u), 1)], min_val=0, max_val=E)
                                    sp.reg_alu(st, s0 + j, E, ALU.min)
                                    s1 = sp.snap(st, min_val=0, max_val=E)
                                    sp.dma_start(xsrc[:, u:u + 1], srcflat[bass.ds(s1, W), :]).then_inc(x_in, 16)
                                    sp.dma_start(xdst[:, u:u + 1], dstflat[bass.ds(s1, W), :]).then_inc(x_in, 16)
                                    loads += 2
                                    if p in (3, 4):
                                        for h in range(2):
                                            sp.dma_start(xrow[h * G + u:h * G + u + 1, :],
                                                         dstpad.rearrange("(o a) b -> o (a b)", o=1)[:, bass.ds(s1, W)])\
                                              .then_inc(x_in, 16)
                                        loads += 2
                                    if p == 8:
                                        sp.dma_start(xea[:, u, :], eapad[bass.ds(s1, W), :]).then_inc(x_in, 16)
                                        loads += 1
                                sp.reg_add(xin, xin, 16 * loads)
                                sp.wait_ge(x_in, sp.snap(xin, min_val=1, max_val=1 << 30))
                                sp.sem_inc(baton[p], 1)
                            further(sp, p, xb, xmaxc, body)
            pass_written(sp, NPASS - 1)

        @block.gpsimd
        def _(pool):
            k = 0

            def const(ins):
                nonlocal k
                k += 1
                ins.then_inc(pool_c, 1)
                pool.wait_ge(pool_c, k)

            const(nc.gpsimd.memset(fillc[:, 0, :], 0))
            const(nc.gpsimd.memset(fillc[:, 1, :], PADDST))
            const(nc.gpsimd.memset(fillz[:, :], 0.0))
            pool.sem_inc(s_fill, 3)
            const(nc.gpsimd.iota(iota_i[:, :], pattern=[[1, T]], base=0, channel_multiplier=0))
            const(nc.gpsimd.iota(pcol_i[:, :], pattern=[[0, 1]], base=0, channel_multiplier=1))
            const(nc.gpsimd.iota(tbase_i[:, :], pattern=[[NT * CH, T // CH]], base=0, channel_multiplier=NT))
            const(nc.gpsimd.memset(ident[:, :], 0.0))
            const(nc.gpsimd.affine_select(out=ident[:, :], in_=ident[:, :], compare_op=ALU.not_equal, fill=1.0, base=0,
                                          pattern=[[-1, 128]], channel_multiplier=1))
            const(nc.gpsimd.memset(ones[:, :], 1.0))
            const(nc.gpsimd.affine_select(out=tri[:, :], in_=ones[:, :], compare_op=ALU.is_gt, fill=0.0, base=0,
                                          pattern=[[1, 128]], channel_multiplier=-1))
            const(nc.gpsimd.memset(epsc[:, 0:1], 1e-5))
            const(nc.gpsimd.memset(epsc[:, 1:2], 1.0))
            const(nc.gpsimd.memset(zb[:, :], 0.0))
            const(nc.gpsimd.memset(m65[:, :, :, :], 1.0))
            const(nc.gpsimd.memset(xm65[:, :, :], 1.0))
            const(nc.gpsimd.memset(hs66[:, :, :, :], 1.0))
            const(nc.gpsimd.memset(sg[:, :, :, :], 1.0))
            const(nc.gpsimd.memset(usT[:, :, :], 1.0))
            const(nc.gpsimd.memset(qk[:, :, :, :], 0.0))
            const(nc.gpsimd.memset(xflag[:, :, :], -BIG))
            const(nc.gpsimd.memset(flagw[:, :, :, :], -BIG))
            const(nc.gpsimd.memset(drel[:, T:T + 2 * G], 0.0))
            assert k == POOL_CONSTS
            pool.wait_ge(s_pad, 80)
            pool.wait_ge(s_dve, SCOL_DONE)
            for c in range(T // CH):
                for into, pad in ((wsrc, srcpad), (wdst, dstpad)):
                    pool.indirect_dma_start(into[:, c, :], None, pad,
                                            bass.IndirectOffsetOnAxis(ap=scol_i[:, c:c + 1], axis=1)).then_inc(s_win, 16)
            pool.wait_ge(tables, 1)
            for par in range(2):
                for u in range(G):
                    pool.indirect_dma_start(m65[:, par, u, 0:D], None, a["x"],
                                            bass.IndirectOffsetOnAxis(ap=pcol_i[:, 0:1], axis=0)).then_inc(gathered[par], 16)
                pool.wait_ge(gathered[par], 16 * G)
            pool.sem_inc(primed, 1)
            pool.wait_ge(primed, 4)
            xg = pool.alloc_register("xg")
            pool.reg_mov(xg, 0)
            xb = pool.alloc_register("xb_pool")
            for p in range(1, NPASS):
                pass_written(pool, p - 1)
                pool.reg_mov(xb, 1)
                table, width = TABLE[p], (DH if p == 6 else D)
                rows, xrows = (m128, xm128) if p == 6 else (m65, xm65)
                reader = "mm_z" if p == 8 else "wm" if p in (3, 4) else "agg"
                with pool.Fori(0, GROUPS // 2) as i:
                    g = i * 2
                    xmaxc = pool.value_load(maxc[0:1, bass.ds(i, 1)], min_val=0, max_val=E)
                    for par in range(2):
                        pool.wait_ge(L["idx"][par], loaded(p, "idx", g))
                        pool.wait_ge(S[reader], before(p, reader, g, par))
                        hold(pool)
                        for u in range(G):
                            pool.indirect_dma_start(rows[:, par, u, 0:width], None, table,
                                                    bass.IndirectOffsetOnAxis(ap=nidx[:, par, u:u + 1], axis=0))\
                                .then_inc(gathered[par], 16)
                    for par in range(2):
                        def body(j):
                            pool.wait_ge(baton[p], at(pool, xb, 1))
                            hold(pool)
                            for u in range(G):
                                pool.indirect_dma_start(xrows[:, u, 0:width], None, table,
                                                        bass.IndirectOffsetOnAxis(ap=xsrc[:, u:u + 1], axis=0))\
                                    .then_inc(x_g, 16)
                            pool.reg_add(xg, xg, 16 * G)
                            pool.wait_ge(x_g, pool.snap(xg, min_val=1, max_val=1 << 30))
                            pool.sem_inc(baton[p], 1)
                        further(pool, p, xb, xmaxc, body)

        @block.tensor
        def _(pe):
            mm, turn = nc.tensor.matmul, nc.tensor.transpose

            pe.wait_ge(pool_c, POOL_CONSTS)
            mm(pb(0, LO)[0:HI, :], zb[0:CH, 0:HI], zb[0:CH, 0:LO], start=True, stop=False)
            pe.sem_inc(q_used, 2)
            with pe.Fori(0, E // CH // HB // 2) as t2:
                for k in range(2):
                    pe.wait_ge(q_ready, 4 * t2 + (2 * k + 2))
                    for n in range(HB):
                        ins = mm(pb(0, LO)[0:HI, :], ohh[:, k, n, :], ohl[:, k, n, :], start=False, stop=False)
                    ins.then_inc(q_used, 1)
            mm(pb(0, LO)[0:HI, :], zb[0:CH, 0:HI], zb[0:CH, 0:LO], start=False, stop=True).then_inc(s_pe, 1)

            pe.wait_ge(s_load, 16 * N_WEIGHT_LOADS)
            for l in range(2):
                for k in range(2):
                    for h in range(2):
                        turn(pb(6 + l, 65, (k * 2 + h) * 65)[0:D, :], cw[:, l, k, h * D:(h + 1) * D], ident[0:65, 0:65])
            turn(pb(5, 128)[0:D, :], g1w[:, :], ident[:, :])
            turn(pb(5, 128, 128), g2w[:, :], ident[:, :])
            turn(pb(5, D, 256), g3w[:, :], ident[0:D, 0:D])
            turn(pb(5, 65, 320)[0:D, :], m2w[:, :], ident[0:65, 0:65]).then_inc(w_pe, 1)
            pe.wait_ge(w_dve, 7)
            for l in range(2):
                for h in range(2):
                    mm(pb(6, 65, (l * 2 + h) * 65)[0:65, :], cwT[:, l, 0, h, :], cwT[:, l, 1, h, :], start=True, stop=True)
            mm(pb(5, D)[0:65, :], m2T[:, :], u1w[:, :], start=True, stop=True).then_inc(w_pe, 1)

            pe.wait_ge(s_cnt, 48)
            for c in range(T // CH):
                ins = mm(pb(3, 1, c)[0:CH, :], tri[0:CH, 0:CH], cntc[:, c:c + 1], start=True, stop=c == 0)
                for d in range(c):
                    ins = mm(pb(3, 1, c)[0:CH, :], ones[0:CH, 0:CH], cntc[:, d:d + 1], start=False, stop=d == c - 1)
            ins.then_inc(s_pe, 1)
            pe.wait_ge(s_dve, WSF_DONE)
            for c in range(T // CH):
                turn(pb(4, CH, c * CH), wsf[:, c, :], ident[0:CH, 0:CH])
                ins = turn(pb(5, CH, c * CH), drelw[:, c, :], ident[0:CH, 0:CH])
            ins.then_inc(s_pe, 1)
            for n in PE_STAGES.split():
                pe.sem_inc(S[n], 2)
            pe.sem_inc(primed, 1)
            pe.wait_ge(primed, 4)
            pe.wait_ge(w_dve, W_DVE)
            pe.wait_ge(s_vrow, 16)

            xb = pe.alloc_register("xb_pe")

            def turn_onehots(q, onehot):
                for u in range(G):
                    ins = turn(pb(q + 2 + u // 4, W, (u % 4) * W)[0:NT, :], onehot[:, u, :], ident[:, :])
                return ins

            def node_to_edge(q, par):
                for h in range(2):
                    for u in range(G):
                        ins = mm(pb(q + 2 + h, 65, u * 65), ohT[:, par, u * W:(u + 1) * W],
                                 gS[:, par, h, u * 65:(u + 1) * 65], start=True, stop=True)
                return ins

            def weighted_sums(q, par, onehot):
                for h in range(2):
                    for u in range(G):
                        ins = mm(pb(q + 2 + h, 65, u * 65)[0:NT, :], onehot[:, u, :], pr[:, par, h, u, :],
                                 start=True, stop=True)
                return ins

            def turn_rows(q, par, flag_rows):
                turn(pb(q, 2 * G), rowm[:, par, 1, :], ident[0:2 * G, 0:2 * G])
                return turn(pb(q, 2 * G, 16), flag_rows, ident[0:2 * G, 0:2 * G])

            def pick(q, onehot):
                for k in range(2):
                    for h in range(2):
                        for u in range(G):
                            c = h * G + u
                            ins = mm(pb(q, 1, 32 + 16 * k + c)[0:NT, :], onehot[:, u, :], xcol[:, 1 - k, c:c + 1],
                                     start=True, stop=True)
                return ins

            def turn_features(q, e):
                for u in range(G):
                    ins = turn(pb(q + 2 + u // 4, W, (u % 4) * W)[0:D, :], e[:, u, :], ident[:, :])
                return ins

            def messages(q, par, rows):
                for u in range(G):
                    o = pb(q + 1, D, u * D)
                    mm(o, ident[:, :], rows[:, u, 0:D], start=True, stop=False)
                    mm(o, ohT[:, par, u * W:(u + 1) * W], ysb[:, par, u * D:(u + 1) * D], start=False, stop=False)
                    ins = mm(o, eT[:, par, u * W:(u + 1) * W], m1w[0:D, 2, :], start=False, stop=True)
                return ins

            def message_sums(q, par, onehot):
                for u in range(G):
                    ins = mm(pb(q, 65, u * 65)[0:NT, :], onehot[:, u, :], sg[:, par, u, :], start=True, stop=True)
                return ins

            for p in range(1, NPASS):
                pass_written(pe, p - 1)
                pe.reg_mov(xb, 1)
                with pe.Fori(0, GROUPS // 2) as i:
                    g = i * 2
                    xmaxc = pe.value_load(maxc[0:1, bass.ds(i, 1)], min_val=0, max_val=E)

                    def need(name, par):
                        pe.wait_ge(S[name], done(p, name, g, par))

                    def freed(name, par):
                        pe.wait_ge(S[name], before(p, name, g, par))

                    if p in (1, 2, 5, 6, 7):
                        width = {1: 65, 6: DH}.get(p, D)
                        rows, xrows = (m128, xm128) if p == 6 else (m65, xm65)

                        def sums_of(par, onehot, m, add):
                            q = 4 * par
                            for u in range(G):
                                c = u * width
                                ins = mm(pb(q + c // 512, width, c % 512)[0:NT, :], onehot[:, u, :], m[:, u, 0:width],
                                         start=not add, stop=not add or u == G - 1 or (c + width) % 512 == 0)
                            return ins

                        for par in range(2):
                            q = 4 * par
                            need("oh", par)
                            freed("ev", par)
                            if p >= 5:
                                pe.wait_ge(L["hs"][par], loaded(p, "hs", g))
                                for c in range(0, G * width, 512):
                                    cols = min(512, G * width - c)
                                    mm(pb(q + c // 512, cols)[0:NT, :], ident[0:NT, 0:NT], hsb[:, par, c:c + cols],
                                       start=True, stop=False)
                            pe.wait_ge(gathered[par], gathered_at(p, g))
                            sums_of(par, oh[:, par, :, :], rows[:, par, :, :], p >= 5).then_inc(S["agg"], 1)

                            def body(j):
                                pe.wait_ge(baton[p], at(pe, xb, 5))
                                hold(pe)
                                sums_of(par, xoh, xrows, False).then_inc(baton[p], 1)
                            further(pe, p, xb, xmaxc, body)

                    if p in (1, 2):
                        for par in range(2):
                            need("state", par)
                            pe.wait_ge(L["hs"][par], loaded(p, "hs", g))
                            freed("ct", par)
                            for u in range(G):
                                ins = turn(pb(4 * par + 1, NT, u * NT), c128[:, par, u, :], ident[0:NT, 0:NT])
                            ins.then_inc(S["tr"], 1)
                        for par in range(2):
                            need("ct", par)
                            freed("out" if p == 1 else "xadd", par)
                            bias = brow[f"s{p - 1}"][0:1, :, :].rearrange("p u f -> p (u f)")
                            hold(pe)
                            mm(pb(4 * par + 2, G * D)[0:NT, :], ones[0:1, 0:NT], bias, start=True, stop=False)
                            for u in range(G):
                                ins = mm(pb(4 * par + 2, D, u * D)[0:NT, :], ctb[:, par, u * NT:(u + 1) * NT],
                                         sage_w[p - 1][:, :], start=False, stop=u == G - 1)
                            ins.then_inc(S["mm"], 1)
                    elif p == 5:
                        for par in range(2):
                            need("state", par)
                            freed("ct", par)
                            hold(pe)
                            for u in range(G):
                                ins = turn(pb(4 * par + 1, NT, u * NT)[0:D, :], c65[:, par, u, 0:D], ident[0:NT, 0:NT])
                            ins.then_inc(S["tr"], 1)
                        for par in range(2):
                            need("ct", par)
                            freed("out", par)
                            bias = brow["g1"][0:1, :, :].rearrange("p u f -> p (u f)")
                            hold(pe)
                            mm(pb(4 * par + 2)[0:NT, :], ones[0:1, 0:NT], bias[:, 0:512], start=True, stop=False)
                            mm(pb(4 * par + 3, 128)[0:NT, :], ones[0:1, 0:NT], bias[:, 512:640], start=True, stop=False)
                            for u in range(G):
                                ins = mm(pb(4 * par + 2 + u // 4, DH, (u % 4) * DH)[0:NT, :],
                                         ctb[0:D, par, u * NT:(u + 1) * NT], g1t[:, :], start=False, stop=u >= 3)
                            ins.then_inc(S["mm"], 1)
                    elif p == 6:
                        for par in range(2):
                            need("state", par)
                            freed("out", par)
                            for u in range(G):
                                ins = turn(pb(4 * par + 2, NT, u * NT), c128[:, par, u, :], ident[0:NT, 0:NT])
                            ins.then_inc(S["tr"], 1)
                        for par in range(2):
                            need("ct", par)
                            freed("relu", par)
                            mm(pb(4 * par + 3, G * NT), g2t[:, :], ctb[:, par, :], start=True, stop=True).then_inc(S["mm"], 1)
                        for par in range(2):
                            need("relu", par)
                            for u in range(G):
                                ins = mm(pb(4 * par + 2, D, u * D)[0:NT, :], h6T[:, par, u * NT:(u + 1) * NT], g3t[:, :],
                                         start=True, stop=True)
                            ins.then_inc(S["mm2"], 1)
                    elif p == 7:
                        for par in range(2):
                            need("nrm", par)
                            freed("ct", par)
                            hold(pe)
                            for u in range(G):
                                ins = turn(pb(4 * par + 1, NT, u * NT)[0:D, :], w3[:, par, u, :], ident[0:NT, 0:NT])
                            ins.then_inc(S["tr"], 1)
                        for par in range(2):
                            need("ct", par)
                            freed("out", par)
                            hold(pe)
                            for u in range(G):
                                ins = mm(pb(4 * par + 2, D, u * D)[0:NT, :], ctb[0:D, par, u * NT:(u + 1) * NT],
                                         m1w[0:D, 0, :], start=True, stop=True)
                            ins.then_inc(S["mm"], 1)
                    elif p in (3, 4):
                        l = p - 3
                        end = "out" if p == 3 else "xadd"
                        for par in range(2):
                            need("he", par)
                            pe.wait_ge(L["hs"][par], loaded(p, "hs", g))
                            freed("ct", par)
                            for u in range(G):
                                ins = turn(pb(4 * par, NT, u * NT)[0:66, :], hs66[:, par, u, :], ident[0:NT, 0:NT])
                            ins.then_inc(S["tr_h"], 1)
                        for par in range(2):
                            need("oh", par)
                            freed("den", par)
                            freed("state_in", par)
                            turn_onehots(4 * par, oh[:, par, :, :]).then_inc(S["tr_o"], 1)
                        for par in range(2):
                            need("ht", par)
                            freed(end, par)
                            for h in range(2):
                                for u in range(G):
                                    ins = mm(pb(4 * par + h, 65, u * 65)[0:NT, :], hT[:, par, u * NT:(u + 1) * NT],
                                             qk[:, l, h, :], start=True, stop=True)
                            ins.then_inc(S["mm_g"], 1)
                        for par in range(2):
                            need("gt", par)
                            need("oht", par)
                            node_to_edge(4 * par, par).then_inc(S["exp_g"], 1)
                        for par in range(2):
                            need("dot", par)
                            turn(pb(4 * par, W)[0:2 * G, :], al[:, par, :], ident[:, :]).then_inc(S["tr_a"], 1)
                        for par in range(2):
                            need("exp", par)
                            hold(pe)
                            turn(pb(4 * par + 1, 2 * G), rowm[:, par, 3, :], ident[0:2 * G, 0:2 * G]).then_inc(S["tr_p"], 1)
                        for par in range(2):
                            need("wm", par)
                            q = 4 * par
                            weighted_sums(q, par, oh[:, par, :, :]).then_inc(S["agg"], 1)

                            def prepare():
                                pe.wait_ge(baton[p], at(pe, xb, 1))
                                hold(pe)
                                turn_rows(q, par, flags[:, par, 1, :]).then_inc(baton[p], 1)
                                pe.wait_ge(baton[p], at(pe, xb, 4))
                                hold(pe)
                                pick(q, oh[:, par, :, :]).then_inc(baton[p], 1)

                            def body(j):
                                pe.wait_ge(baton[p], at(pe, xb, 8))
                                hold(pe)
                                turn_onehots(q, xoh).then_inc(baton[p], 1)
                                pe.wait_ge(baton[p], at(pe, xb, 10))
                                hold(pe)
                                node_to_edge(q, par).then_inc(baton[p], 1)
                                pe.wait_ge(baton[p], at(pe, xb, 13))
                                hold(pe)
                                turn(pb(q, W)[0:2 * G, :], al[:, par, :], ident[:, :]).then_inc(baton[p], 1)
                                pe.wait_ge(baton[p], at(pe, xb, 18))
                                hold(pe)
                                turn(pb(q + 1, 2 * G), rowm[:, par, 3, :], ident[0:2 * G, 0:2 * G])\
                                    .then_inc(baton[p], 1)
                                pe.wait_ge(baton[p], at(pe, xb, 20))
                                hold(pe)
                                weighted_sums(q, par, xoh).then_inc(baton[p], 1)
                                hold(pe)
                                turn_rows(q, par, xflag[:, 1, :]).then_inc(baton[p], 1)
                                pe.wait_ge(baton[p], at(pe, xb, 24))
                                hold(pe)
                                pick(q, xoh).then_inc(baton[p], 1)
                            further(pe, p, xb, xmaxc, body, prepare)
                        for par in range(2):
                            need("state", par)
                            for u in range(G):
                                ins = turn(pb(4 * par, NT, u * NT), c128[:, par, u, :], ident[0:NT, 0:NT])
                            ins.then_inc(S["tr"], 1)
                        for par in range(2):
                            need("ct", par)
                            for u in range(G):
                                cols = slice(u * NT, (u + 1) * NT)
                                o = pb(4 * par + 1, D, u * D)[0:NT, :]
                                mm(o, ctb[:, par, cols], vw[:, l, :], start=True, stop=False)
                                ins = mm(o, hT[:, par, cols], sw[:, l, :], start=False, stop=True)
                            ins.then_inc(S["mm"], 1)
                    else:
                        for par in range(2):
                            pe.wait_ge(L["hs"][par], loaded(p, "hs", g))
                            freed("pre", par)
                            for u in range(G):
                                ins = turn(pb(4 * par, NT, u * NT)[0:65, :], hs66[:, par, u, 0:65], ident[0:NT, 0:NT])
                            ins.then_inc(S["tr_h"], 1)
                        for par in range(2):
                            need("oh", par)
                            freed("ub", par)
                            turn_onehots(4 * par, oh[:, par, :, :]).then_inc(S["tr_o"], 1)
                        for par in range(2):
                            need("ht", par)
                            for u in range(G):
                                ins = mm(pb(4 * par + 1, D, u * D)[0:NT, :], hT[0:65, par, u * NT:(u + 1) * NT],
                                         m1w[:, 1, :], start=True, stop=True)
                            ins.then_inc(S["mm_y"], 1)
                        for par in range(2):
                            pe.wait_ge(L["ea"][par], 5 * loaded(p, "ea", g))
                            need("oht", par)
                            hold(pe)
                            turn_features(4 * par, ea[:, par, :, :]).then_inc(S["tr_e"], 1)
                        for par in range(2):
                            pe.wait_ge(gathered[par], gathered_at(p, g))
                            need("yt", par)
                            need("et", par)
                            messages(4 * par, par, m65[:, par, :, :]).then_inc(S["mm_z"], 1)
                        for par in range(2):
                            q = 4 * par
                            need("silu", par)
                            message_sums(q, par, oh[:, par, :, :]).then_inc(S["agg"], 1)

                            def body(j):
                                pe.wait_ge(baton[p], at(pe, xb, 5))
                                hold(pe)
                                turn_onehots(q, xoh).then_inc(baton[p], 1)
                                pe.wait_ge(baton[p], at(pe, xb, 7))
                                hold(pe)
                                turn_features(q, xea).then_inc(baton[p], 1)
                                pe.wait_ge(baton[p], at(pe, xb, 9))
                                hold(pe)
                                messages(q, par, xm65).then_inc(baton[p], 1)
                                pe.wait_ge(baton[p], at(pe, xb, 16))
                                hold(pe)
                                message_sums(q, par, xoh).then_inc(baton[p], 1)
                            further(pe, p, xb, xmaxc, body)
                        for par in range(2):
                            need("state", par)
                            for u in range(G):
                                ins = turn(pb(4 * par + 2, NT, u * NT)[0:65, :], c65[:, par, u, :], ident[0:NT, 0:NT])
                            ins.then_inc(S["tr"], 1)
                        for par in range(2):
                            need("ct", par)
                            mm(pb(4 * par + 3, G * NT)[0:D, :], mu[:, :], ctb[0:65, par, :], start=True, stop=True)\
                                .then_inc(S["mm"], 1)
                        for par in range(2):
                            need("usilu", par)
                            for u in range(G):
                                ins = mm(pb(4 * par, D, u * D)[0:NT, :], usT[:, par, u * NT:(u + 1) * NT], u2w[:, :],
                                         start=True, stop=True)
                            ins.then_inc(S["mm2"], 1)

        @block.scalar
        def _(act):
            fn = nc.scalar.activation
            act.preload_act_table_set("natural_log_exp_and_others")
            act.wait_ge(pool_c, POOL_CONSTS)
            for n in "abc":
                for par in range(2):
                    act.dma_start(prime_d[:, :], ident[0:16, 0:16]).then_inc(ST[n][par], 16)
                    act.wait_ge(ST[n][par], 16)
            for n in ACT_STAGES.split():
                act.sem_inc(S[n], 2)
            act.sem_inc(primed, 1)
            act.wait_ge(primed, 4)
            xb = act.alloc_register("xb_act")

            for p in range(NPASS):
                if p:
                    pass_written(act, p - 1)
                    act.reg_mov(xb, 1)
                if p == 2:
                    fn(dinv[:, :], deg[:, :], ACT.Ln, bias=epsc[0:NT, 1:2]).then_inc(s_act, 1)
                    act.wait_ge(s_act, 1)
                    fn(dinv[:, :], dinv[:, :], ACT.Exp, scale=-0.5).then_inc(s_act, 1)
                with act.Fori(0, GROUPS // 2) as i:
                    g = i * 2
                    if p in (3, 4, 8):
                        xmaxc = act.value_load(maxc[0:1, bass.ds(i, 1)], min_val=0, max_val=E)

                    def need(name, par):
                        act.wait_ge(S[name], done(p, name, g, par))

                    def freed(name, par):
                        act.wait_ge(S[name], before(p, name, g, par))

                    def store(name, par, buf, producer, table):
                        need(producer, par)
                        act.dma_start(tiles_of(table)[:, bass.ds(g * G + par * G, G), :], buf).then_inc(ST[name][par], 16)

                    if p in (1, 2, 5, 6):
                        bank, rows = {1: (1, 128), 2: (1, 128), 5: (1, D), 6: (2, 128)}[p]
                        for par in range(2):
                            need("tr", par)
                            freed("mm", par)
                            fn(ctb[0:rows, par, :], pb(4 * par + bank, G * NT)[0:rows, :], ACT.Copy).then_inc(S["ct"], 1)
                    if p == 1:
                        for par in range(2):
                            need("mm", par)
                            act.wait_ge(ST["a"][par], stored_before(p, "a", g))
                            fn(w3[:, par, :, :], tiles(pb(4 * par + 2, G * D)[0:NT, :], D), ACT.Relu).then_inc(S["out"], 1)
                            store("a", par, w3[:, par, :, :], "out", OUTA[p])
                    if p == 5:
                        for par in range(2):
                            store("a", par, w3b[:, par, :, :], "out", OUTA[p])
                    if p == 6:
                        for par in range(2):
                            need("mm", par)
                            freed("mm2", par)
                            fn(h6T[:, par, :], pb(4 * par + 3, G * NT), ACT.Relu, bias=g2b[:, 0:1]).then_inc(S["relu"], 1)
                        for par in range(2):
                            store("a", par, w3[:, par, :, :], "out", OUTA[p])
                    if p == 7:
                        for par in range(2):
                            need("sub", par)
                            fn(w1[:, par, :, :], w1[:, par, :, :], ACT.Exp).then_inc(S["exp"], 1)
                    if p in (3, 4):
                        for par in range(2):
                            need("tr_h", par)
                            fn(hT[:, par, :], pb(4 * par, G * NT)[0:66, :], ACT.Copy).then_inc(S["ht"], 1)
                        for par in range(2):
                            need("tr_o", par)
                            fn(ohT[:, par, :], P[0:NT, (4 * par + 2) * 512:(4 * par + 2) * 512 + G * W], ACT.Copy)\
                                .then_inc(S["oht"], 1)
                        for par in range(2):
                            need("mm_g", par)
                            fn(gS[:, par, :, :], two_banks(4 * par, NT, G * 65), ACT.Copy).then_inc(S["gt"], 1)
                        for par in range(2):
                            need("sub", par)
                            fn(rowm[:, par, 3, :], rowm[:, par, 2, :], ACT.Exp).then_inc(S["exp"], 1)
                        for par in range(2):
                            def body(j):
                                act.wait_ge(baton[p], at(act, xb, 9))
                                fn(ohT[:, par, :], P[0:NT, (4 * par + 2) * 512:(4 * par + 2) * 512 + G * W], ACT.Copy)\
                                    .then_inc(baton[p], 1)
                                act.wait_ge(baton[p], at(act, xb, 17))
                                fn(rowm[:, par, 3, :], rowm[:, par, 2, :], ACT.Exp).then_inc(baton[p], 1)
                                act.wait_ge(baton[p], at(act, xb, 31))
                                fn(xs[:, 3:5, :], xs[:, 3:5, :], ACT.Exp).then_inc(baton[p], 1)
                            further(act, p, xb, xmaxc, body)
                        for par in range(2):
                            need("tr", par)
                            fn(ctb[:, par, :], pb(4 * par, G * NT), ACT.Copy).then_inc(S["ct"], 1)
                        if p == 3:
                            for par in range(2):
                                need("mm", par)
                                act.wait_ge(ST["a"][par], stored_before(p, "a", g))
                                fn(w3[:, par, :, :], tiles(pb(4 * par + 1, G * D)[0:NT, :], D), ACT.Copy)\
                                    .then_inc(S["out"], 1)
                                store("a", par, w3[:, par, :, :], "out", OUTA[p])
                    if p == 8:
                        for par in range(2):
                            need("tr_h", par)
                            fn(hT[0:65, par, :], pb(4 * par, G * NT)[0:65, :], ACT.Copy).then_inc(S["ht"], 1)
                        for par in range(2):
                            need("tr_o", par)
                            fn(ohT[:, par, :], P[0:NT, (4 * par + 2) * 512:(4 * par + 2) * 512 + G * W], ACT.Copy)\
                                .then_inc(S["oht"], 1)
                        for par in range(2):
                            need("mm_y", par)
                            fn(ysb[:, par, :], pb(4 * par + 1, G * D)[0:NT, :], ACT.Copy).then_inc(S["yt"], 1)
                        for par in range(2):
                            need("tr_e", par)
                            fn(eT[:, par, :], P[0:D, (4 * par + 2) * 512:(4 * par + 2) * 512 + G * W], ACT.Copy)\
                                .then_inc(S["et"], 1)
                        for par in range(2):
                            need("mm_z", par)
                            fn(z1[:, par, :], pb(4 * par + 1, G * D), ACT.Abs).then_inc(S["abs"], 1)
                        for par in range(2):
                            need("abs", par)
                            fn(z1[:, par, :], z1[:, par, :], ACT.Exp, scale=-1.0).then_inc(S["e1"], 1)
                        for par in range(2):
                            need("e1", par)
                            fn(z2[:, par, :], z1[:, par, :], ACT.Ln, bias=epsc[:, 1:2]).then_inc(S["e2"], 1)
                        for par in range(2):
                            need("lsig", par)
                            fn(z1[:, par, :], z2[:, par, :], ACT.Exp).then_inc(S["e3"], 1)
                        for par in range(2):
                            def body(j):
                                act.wait_ge(baton[p], at(act, xb, 6))
                                fn(ohT[:, par, :], P[0:NT, (4 * par + 2) * 512:(4 * par + 2) * 512 + G * W], ACT.Copy)\
                                    .then_inc(baton[p], 1)
                                act.wait_ge(baton[p], at(act, xb, 8))
                                fn(eT[:, par, :], P[0:D, (4 * par + 2) * 512:(4 * par + 2) * 512 + G * W], ACT.Copy)\
                                    .then_inc(baton[p], 1)
                                act.wait_ge(baton[p], at(act, xb, 10))
                                fn(z1[:, par, :], pb(4 * par + 1, G * D), ACT.Abs).then_inc(baton[p], 1)
                                act.wait_ge(baton[p], at(act, xb, 11))
                                fn(z1[:, par, :], z1[:, par, :], ACT.Exp, scale=-1.0).then_inc(baton[p], 1)
                                act.wait_ge(baton[p], at(act, xb, 12))
                                fn(z2[:, par, :], z1[:, par, :], ACT.Ln, bias=epsc[:, 1:2]).then_inc(baton[p], 1)
                                act.wait_ge(baton[p], at(act, xb, 14))
                                fn(z1[:, par, :], z2[:, par, :], ACT.Exp).then_inc(baton[p], 1)
                            further(act, p, xb, xmaxc, body)
                        for par in range(2):
                            need("tr", par)
                            fn(ctb[0:65, par, :], pb(4 * par + 2, G * NT)[0:65, :], ACT.Copy).then_inc(S["ct"], 1)
                        for par in range(2):
                            need("ub", par)
                            fn(ue[:, par, :], uz[:, par, :], ACT.Abs).then_inc(S["uabs"], 1)
                        for par in range(2):
                            need("uabs", par)
                            fn(ue[:, par, :], ue[:, par, :], ACT.Exp, scale=-1.0).then_inc(S["u1"], 1)
                        for par in range(2):
                            need("u1", par)
                            fn(ue[:, par, :], ue[:, par, :], ACT.Ln, bias=epsc[0:D, 1:2]).then_inc(S["u2"], 1)
                        for par in range(2):
                            need("ulsig", par)
                            fn(ue[:, par, :], ue[:, par, :], ACT.Exp).then_inc(S["u3"], 1)

                    if p in (2, 4, 7):
                        for par in range(2):
                            store("b", par, w2[:, par, :, :], "xadd", OUTB[p])
                    if p in (0, 2, 4, 7, 8):
                        for par in range(2):
                            need("cen", par)
                            fn(w1[:, par, :, :], w0[:, par, :, :], ACT.Square).then_inc(S["sq"], 1)
                        for par in range(2):
                            need("var", par)
                            fn(small[:, par, 2, 0:G], small[:, par, 1, 0:G], ACT.Ln, bias=epsc[0:NT, 0:1], scale=1.0 / D)\
                                .then_inc(S["ln"], 1)
                        for par in range(2):
                            need("ln", par)
                            fn(small[:, par, 3, 0:G], small[:, par, 2, 0:G], ACT.Exp, scale=-0.5).then_inc(S["rstd"], 1)
                    if p in (0, 2, 4, 7):
                        for par in range(2):
                            store("a", par, w3[:, par, :, :], "nrm", OUTA[p])
                    if p == 7:
                        for par in range(2):
                            need("tr", par)
                            freed("mm", par)
                            fn(ctb[0:D, par, :], pb(4 * par + 1, G * NT)[0:D, :], ACT.Copy).then_inc(S["ct"], 1)
                        for par in range(2):
                            need("mm", par)
                            act.wait_ge(ST["c"][par], stored_before(p, "c", g))
                            fn(wc[:, par, :, :], tiles(pb(4 * par + 2, G * D)[0:NT, :], D), ACT.Copy).then_inc(S["out"], 1)
                            store("c", par, wc[:, par, :, :], "out", OUTC[p])
                    if p == 8:
                        for par in range(2):
                            store("b", par, w3[:, par, :, :], "xadd", OUTB[p])

        @block.vector
        def _(dve):
            v = nc.vector
            k = 0

            def step(ins):
                nonlocal k
                k += 1
                ins.then_inc(s_dve, 1)
                dve.wait_ge(s_dve, k)

            def split(x, q, r, by):
                step(v.tensor_scalar(q[:, :], x[:, :], 1.0 / by, None, ALU.mult))
                step(v.tensor_copy(dwork[:, :], q[:, :]))
                step(v.tensor_copy(q[:, :], dwork[:, :]))
                step(v.scalar_tensor_tensor(r[:, :], q[:, :], -float(by), x[:, :], ALU.mult, ALU.add))
                step(v.tensor_scalar(c1[:, :], r[:, :], 0.0, None, ALU.is_lt))
                step(v.tensor_tensor(q[:, :], q[:, :], c1[:, :], ALU.subtract))
                step(v.scalar_tensor_tensor(r[:, :], c1[:, :], float(by), r[:, :], ALU.mult, ALU.add))
                step(v.tensor_scalar(c1[:, :], r[:, :], float(by), None, ALU.is_ge))
                step(v.tensor_tensor(q[:, :], q[:, :], c1[:, :], ALU.add))
                step(v.scalar_tensor_tensor(r[:, :], c1[:, :], -float(by), r[:, :], ALU.mult, ALU.add))

            dve.wait_ge(pool_c, POOL_CONSTS)
            step(v.tensor_copy(iota_f[:, :], iota_i[:, :]))
            step(v.tensor_scalar(base_f[:, :], iota_f[:, :], float(NT), None, ALU.mult))
            step(v.tensor_copy(tbase[:, :], tbase_i[:, :]))
            dve.wait_ge(s_list, 16)
            x0, x1, x2, c1 = hq
            step(v.tensor_copy(x0[:, :], dlist[:, :]))
            split(x0, x1, x2, NT)
            split(x1, x0, x2, LO)
            hi, lo = x0, x2
            with dve.Fori(0, E // CH // HB // 2) as t2:
                for kk in range(2):
                    cols = bass.ds(t2 * (2 * HB) + kk * HB, HB)
                    dve.wait_ge(q_used, 2 * t2 + (kk + 1))
                    for onehot, digit, n in ((ohh, hi, HI), (ohl, lo, LO)):
                        v.tensor_tensor(onehot[:, kk, :, :], iota_f[0:CH, 0:n].unsqueeze(1).broadcast_to([CH, HB, n]),
                                        digit[:, cols].unsqueeze(2).broadcast_to([CH, HB, n]), ALU.is_equal)\
                            .then_inc(q_ready, 1)
            dve.wait_ge(s_pe, 1)
            step(v.tensor_copy(cnt_s[:, :], pb(0, LO)[0:HI, :]))
            assert k == CNT_DONE
            dve.wait_ge(s_load, 16 * N_WEIGHT_LOADS)
            v.tensor_tensor(swrow[0:1, :, :], bvrow[0:1, :, 0, :], bvrow[0:1, :, 1, :], ALU.add).then_inc(s_sw, 1)
            dve.wait_ge(s_sw, 1)
            v.tensor_scalar(swrow[0:1, :, :], swrow[0:1, :, :], 0.5, None, ALU.mult).then_inc(w_dve, 1)
            dve.wait_ge(w_pe, 1)
            for l in range(2):
                v.tensor_copy(cwT[:, l, :, :, :], pb(6 + l, 260)[0:D, :].rearrange("p (k h f) -> p k h f", k=2, h=2))\
                    .then_inc(w_dve, 1)
            v.tensor_copy(g1t[:, :], pb(5, 128)[0:D, :]).then_inc(w_dve, 1)
            v.tensor_copy(g2t[:, :], pb(5, 128, 128)).then_inc(w_dve, 1)
            v.tensor_copy(g3t[:, :], pb(5, D, 256)).then_inc(w_dve, 1)
            v.tensor_copy(m2T[:, :], pb(5, 65, 320)[0:D, :]).then_inc(w_dve, 1)
            dve.wait_ge(w_pe, 2)
            v.tensor_scalar(qk[0:65, :, :, :], pb(6, 260)[0:65, :].rearrange("p (l h f) -> p l h f", l=2, h=2),
                            float(D) ** -0.5, None, ALU.mult).then_inc(w_dve, 1)
            v.tensor_copy(mu[:, :], pb(5, D)[0:65, :]).then_inc(w_dve, 1)
            v.tensor_scalar(vw[:, :, :], vw[:, :, :], 0.5, None, ALU.mult).then_inc(w_dve, 1)
            v.tensor_copy(sw[0:65, :, :], cw[:, :, 3, 0:D]).then_inc(w_dve, 1)
            dve.wait_ge(s_cnt, 48)
            step(v.reduce_max(maxc_f[:, :], crow[:, :].rearrange("p (i c) -> p i c", c=2 * G), AX))
            step(v.tensor_copy(maxc[:, :], maxc_f[:, :]))
            dve.wait_ge(s_pe, 2)
            step(v.tensor_copy(scol_i[:, :], pb(3, T // CH)[0:CH, :]))
            assert k == SCOL_DONE
            dve.wait_ge(s_win, 16 * 2 * (T // CH))
            step(v.tensor_copy(wsf[:, :, :], wdst[:, :, :]))
            step(v.tensor_tensor(drelw[:, :, 0:W - 1], wsf[:, :, 1:W], wsf[:, :, 0:W - 1], ALU.not_equal))
            step(v.tensor_scalar(flagw[:, :, 0, 1:W], drelw[:, :, 0:W - 1], -BIG, None, ALU.mult))
            step(v.tensor_scalar(flagw[:, :, 1, 0:W - 1], drelw[:, :, 0:W - 1], -BIG, None, ALU.mult))
            assert k == FLAG_DONE
            for c in range(T // CH):
                step(v.tensor_scalar(drelw[:, c, :], wsf[:, c, :], tbase[0:CH, c:c + 1], None, ALU.subtract))
            step(v.tensor_copy(wsf[:, :, :], wsrc[:, :, :]))
            assert k == WSF_DONE
            dve.wait_ge(s_pe, 3)
            step(v.tensor_copy(srcw[:, :], pb(4, T)))
            step(v.tensor_copy(drel[:, 0:T], pb(5, T)))
            dve.sem_inc(tables, 1)
            for n in DVE_STAGES.split():
                dve.sem_inc(S[n], 2)
            dve.sem_inc(primed, 1)
            dve.wait_ge(primed, 4)

            def by_node(table, tile0, f):
                return table[:, tile0].unsqueeze(2).broadcast_to([NT, G, f])

            def bias5(n):
                return bias_b[n][:, :].unsqueeze(1).broadcast_to([NT, G, D])

            def small5(par, row, f):
                return small[:, par, row, 0:G].unsqueeze(2).broadcast_to([NT, G, f])

            def heads(x, rows, f):
                return x.rearrange("p (h u) -> p h u", h=2).unsqueeze(3).broadcast_to([rows, 2, G, f])

            def both(x):
                return x.unsqueeze(1).broadcast_to([128, 2, G, 65])

            def by_head(x):
                return x.rearrange("p h (u f) -> p h u f", f=65)

            def onehots(into, rel):
                return v.tensor_tensor(into, iota_f[:, 0:NT].unsqueeze(1).broadcast_to([128, G, NT]),
                                       rel.unsqueeze(2).broadcast_to([128, G, NT]), ALU.is_equal)

            xb = dve.alloc_register("xb_dve")

            for p in range(NPASS):
                if p:
                    dve.wait_ge(S["oh"], start(p, "oh"))
                    for par in range(2):
                        onehots(oh[:, par, :, :], drel[:, par * G:(par + 1) * G]).then_inc(S["oh"], 1)
                    pass_written(dve, p - 1)
                    dve.reg_mov(xb, 1)
                if p == 2:
                    v.tensor_scalar(hasedge[:, :], deg[:, :], 0.0, None, ALU.is_gt).then_inc(s_sw, 1)
                    dve.wait_ge(s_sw, 2)
                    dve.wait_ge(s_act, 2)
                with dve.Fori(0, GROUPS // 2) as i:
                    g = i * 2
                    if p:
                        xmaxc = dve.value_load(maxc[0:1, bass.ds(i, 1)], min_val=0, max_val=E)

                    def need(name, par):
                        dve.wait_ge(S[name], done(p, name, g, par))

                    def freed(name, par):
                        dve.wait_ge(S[name], before(p, name, g, par))

                    def tile0(par):
                        return bass.ds(g * G + par * G, G)

                    def baton_at(n):
                        dve.wait_ge(baton[p], at(dve, xb, n))

                    def xonehots(par, n):
                        v.tensor_copy(xdf[:, :], xdst[:, :]).then_inc(baton[p], 1)
                        baton_at(n + 1)
                        v.tensor_tensor(xdf[:, :], xdf[:, :], base_f[:, tile0(par)], ALU.subtract).then_inc(baton[p], 1)
                        baton_at(n + 2)
                        onehots(xoh[:, :, :], xdf[:, :]).then_inc(baton[p], 1)

                    def next_onehots():
                        for par in range(2):
                            need("agg", par)
                            onehots(oh[:, par, :, :], drel[:, bass.ds(g * G + (2 + par) * G, G)]).then_inc(S["oh"], 1)

                    if p == 1:
                        for par in range(2):
                            sums = tiles(pb(4 * par, G * 65)[0:NT, :], 65)
                            inv = invdeg[:, tile0(par)]

                            def mean(rows, signal, sem_of):
                                hold(dve)
                                signal(v.tensor_copy(deg[:, tile0(par)], rows[:, :, D]), "deg")
                                signal(v.tensor_scalar(inv, deg[:, tile0(par)], 1.0, None, ALU.max), "max")
                                hold(dve)
                                signal(v.reciprocal(inv, inv), "rec")
                                signal(v.tensor_tensor(c128[:, par, :, 0:D], rows[:, :, 0:D],
                                                       by_node(invdeg, tile0(par), D), ALU.mult), "ev")

                            def main_signal(ins, name):
                                ins.then_inc(S[name], 1)
                                need(name, par)

                            need("agg", par)
                            freed("tr", par)
                            mean(sums, main_signal, None)
                            state = tiles(xstate[:, 0:G * 65], 65)

                            def prepare():
                                v.tensor_copy(state, sums).then_inc(baton[p], 1)
                                baton_at(1)

                            def body(j):
                                baton_at(2)
                                xonehots(par, 2)
                                baton_at(6)
                                v.tensor_tensor(state, state, sums, ALU.add).then_inc(baton[p], 1)
                                baton_at(7)
                                steps = [7]

                                def x_signal(ins, name):
                                    steps[0] += 1
                                    ins.then_inc(baton[p], 1)
                                    baton_at(steps[0])
                                mean(state, x_signal, None)
                            further(dve, p, xb, xmaxc, body, prepare)
                            dve.sem_inc(S["state"], 1)
                        next_onehots()

                    if p in (2, 5, 6, 7):
                        width = DH if p == 6 else D
                        scale = invdeg if p == 2 else dinv
                        for par in range(2):
                            q = 4 * par
                            sums = tiles(P[0:NT, q * 512:q * 512 + G * width], width)
                            into = c65[:, par, :, 0:D] if p in (5, 7) else c128[:, par, :, 0:width]
                            need("agg", par)
                            if p != 7:
                                freed("tr", par)
                            v.tensor_tensor(into, sums, by_node(scale, tile0(par), width), ALU.mult).then_inc(S["ev"], 1)
                            need("ev", par)

                            def body(j):
                                xsum = tiles(xt[:, 0:G * width], width)
                                baton_at(2)
                                xonehots(par, 2)
                                baton_at(6)
                                v.tensor_tensor(xsum, sums, by_node(scale, tile0(par), width), ALU.mult)\
                                    .then_inc(baton[p], 1)
                                baton_at(7)
                                v.tensor_tensor(into, into, xsum, ALU.add).then_inc(baton[p], 1)
                                baton_at(8)
                            further(dve, p, xb, xmaxc, body)
                            dve.sem_inc(S["state"], 1)
                        next_onehots()

                    if p == 5:
                        for par in range(2):
                            need("mm", par)
                            dve.wait_ge(ST["a"][par], stored_before(p, "a", g))
                            wide = tiles(P[0:NT, (4 * par + 2) * 512:(4 * par + 2) * 512 + G * DH], DH)
                            v.scalar_tensor_tensor(w3b[:, par, :, :], wide, 0.0, by_node(dinv, tile0(par), DH),
                                                   ALU.max, ALU.mult).then_inc(S["out"], 1)
                    if p == 6:
                        for par in range(2):
                            need("mm2", par)
                            dve.wait_ge(ST["a"][par], stored_before(p, "a", g))
                            v.tensor_tensor(w3[:, par, :, :], tiles(pb(4 * par + 2, G * D)[0:NT, :], D),
                                            by_node(dinv, tile0(par), D), ALU.mult).then_inc(S["out"], 1)
                    if p == 7:
                        for par in range(2):
                            v.tensor_tensor(w1[:, par, :, :], c65[:, par, :, 0:D], bias5("g3"), ALU.add).then_inc(S["pre"], 1)
                        for par in range(2):
                            need("pre", par)
                            v.reduce_max(small[:, par, 4, 0:G], w1[:, par, :, :], AX).then_inc(S["max"], 1)
                        for par in range(2):
                            need("max", par)
                            v.tensor_tensor(w1[:, par, :, :], w1[:, par, :, :], small5(par, 4, D), ALU.subtract)\
                                .then_inc(S["sub"], 1)
                        for par in range(2):
                            need("exp", par)
                            v.reduce_sum(small[:, par, 5, 0:G], w1[:, par, :, :], AX).then_inc(S["den"], 1)
                        for par in range(2):
                            need("den", par)
                            v.reciprocal(small[:, par, 5, 0:G], small[:, par, 5, 0:G]).then_inc(S["rec"], 1)
                        for par in range(2):
                            need("rec", par)
                            v.tensor_tensor(w0[:, par, :, :], w1[:, par, :, :], small5(par, 5, D), ALU.mult)\
                                .then_inc(S["prob"], 1)
                        for par in range(2):
                            need("prob", par)
                            dve.wait_ge(L["x"][par], loaded(p, "x", g))
                            dve.wait_ge(ST["b"][par], stored_before(p, "b", g))
                            v.tensor_tensor(w2[:, par, :, :], w0[:, par, :, :], xres[:, par, :, :], ALU.add)\
                                .then_inc(S["xadd"], 1)

                    if p in (3, 4):
                        for par in range(2):
                            freed("tr_h", par)
                            v.tensor_copy(hs66[:, par, :, D + 1], hasedge[:, tile0(par)]).then_inc(S["he"], 1)
                        q2 = [by_head(two_banks(4 * par + 2, 128, G * 65)) for par in range(2)]
                        qn = [by_head(two_banks(4 * par + 2, NT, G * 65)) for par in range(2)]

                        for par in range(2):
                            need("exp_g", par)
                            dve.wait_ge(gathered[par], gathered_at(p, g))
                            v.tensor_tensor(pr[:, par, :, :, :], q2[par], both(m65[:, par, :, :]), ALU.mult)\
                                .then_inc(S["prod"], 1)
                        for par in range(2):
                            need("prod", par)
                            v.reduce_sum(al[:, par, :].rearrange("p (h u) -> p h u", h=2), pr[:, par, :, :, :], AX)\
                                .then_inc(S["dot"], 1)
                        for par in range(2):
                            need("tr_a", par)
                            dve.wait_ge(L["flag"][par], 2 * loaded(p, "flag", g))
                            v.tensor_tensor_scan(rowm[:, par, 0, :], flags[:, par, 0, :], pb(4 * par, W)[0:2 * G, :], -BIG,
                                                 ALU.add, ALU.max).then_inc(S["fwd"], 1)
                        for par in range(2):
                            need("fwd", par)
                            v.tensor_tensor_scan(rowm[:, par, 1, W - 1::-1], flags[:, par, 1, W - 1::-1],
                                                 rowm[:, par, 0, W - 1::-1], -BIG, ALU.add, ALU.max).then_inc(S["seg"], 1)
                        for par in range(2):
                            need("seg", par)
                            v.tensor_tensor(rowm[:, par, 2, :], pb(4 * par, W)[0:2 * G, :], rowm[:, par, 1, :],
                                            ALU.subtract).then_inc(S["sub"], 1)
                        for par in range(2):
                            need("tr_p", par)
                            v.tensor_tensor(pr[:, par, :, :, :], both(m65[:, par, :, :]),
                                            heads(pb(4 * par + 1, 2 * G), 128, 65), ALU.mult).then_inc(S["wm"], 1)
                        for par in range(2):
                            q = 4 * par
                            den = small[:, par, 5, :]
                            den2 = den.rearrange("p (h u) -> p h u", h=2)
                            cview = c128[:, par, :, :].rearrange("p u (h f) -> p h u f", h=2)
                            need("agg", par)
                            freed("tr", par)
                            v.tensor_scalar(den2, qn[par][:, :, :, D], 1e-16, None, ALU.add).then_inc(S["den"], 1)
                            need("den", par)
                            v.reciprocal(den, den).then_inc(S["rec"], 1)
                            need("rec", par)
                            v.tensor_tensor(cview, qn[par][:, :, :, 0:D], heads(den, NT, D), ALU.mult)\
                                .then_inc(S["state_in"], 1)
                            need("state_in", par)
                            state = xstate[:, :].rearrange("p (h u f) -> p h u f", h=2, f=65)
                            xsum = xt[:, :].rearrange("p (h u f) -> p h u f", h=2, f=65)
                            mx = xs[:, 5, :]

                            def node_maxima(into, n):
                                v.tensor_scalar(xcol[:, 0, :], pb(q, 2 * G, 16), -1.0, None, ALU.is_lt).then_inc(baton[p], 1)
                                baton_at(n + 1)
                                v.tensor_tensor(xcol[:, 1, :], pb(q, 2 * G), xcol[:, 0, :], ALU.mult).then_inc(baton[p], 1)
                                baton_at(n + 3)
                                v.tensor_scalar(xs[:, 1, :], pb(q, 2 * G, 48)[0:NT, :], -FLOOR, FLOOR, ALU.mult, ALU.add)\
                                    .then_inc(baton[p], 1)
                                baton_at(n + 4)
                                v.tensor_tensor(into, xs[:, 1, :], pb(q, 2 * G, 32)[0:NT, :], ALU.add).then_inc(baton[p], 1)
                                baton_at(n + 5)

                            def prepare():
                                v.tensor_copy(state, qn[par]).then_inc(baton[p], 1)
                                baton_at(2)
                                node_maxima(mx, 2)

                            def body(j):
                                baton_at(2)
                                xonehots(par, 2)
                                baton_at(5)
                                v.tensor_scalar(xrf[:, :], xrow[:, :], -BIG, None, ALU.mult).then_inc(baton[p], 1)
                                baton_at(6)
                                for s in range(2):
                                    v.tensor_tensor(xflag[:, s, 1 - s:W - s], xrf[:, 1:W], xrf[:, 0:W - 1],
                                                    ALU.subtract).then_inc(baton[p], 1)
                                    baton_at(7 + s)
                                baton_at(11)
                                v.tensor_tensor(pr[:, par, :, :, :], q2[par], both(xm65[:, :, :]), ALU.mult)\
                                    .then_inc(baton[p], 1)
                                baton_at(12)
                                v.reduce_sum(al[:, par, :].rearrange("p (h u) -> p h u", h=2), pr[:, par, :, :, :], AX)\
                                    .then_inc(baton[p], 1)
                                baton_at(14)
                                v.tensor_tensor_scan(rowm[:, par, 0, :], xflag[:, 0, :], pb(q, W)[0:2 * G, :], -BIG,
                                                     ALU.add, ALU.max).then_inc(baton[p], 1)
                                baton_at(15)
                                v.tensor_tensor_scan(rowm[:, par, 1, W - 1::-1], xflag[:, 1, W - 1::-1],
                                                     rowm[:, par, 0, W - 1::-1], -BIG, ALU.add, ALU.max)\
                                    .then_inc(baton[p], 1)
                                baton_at(16)
                                v.tensor_tensor(rowm[:, par, 2, :], pb(q, W)[0:2 * G, :], rowm[:, par, 1, :],
                                                ALU.subtract).then_inc(baton[p], 1)
                                baton_at(19)
                                v.tensor_tensor(pr[:, par, :, :, :], both(xm65[:, :, :]), heads(pb(q + 1, 2 * G), 128, 65),
                                                ALU.mult).then_inc(baton[p], 1)
                                baton_at(22)
                                node_maxima(xs[:, 0, :], 22)
                                v.tensor_copy(xsum, qn[par]).then_inc(baton[p], 1)
                                v.tensor_tensor(xs[:, 2, :], mx, xs[:, 0, :], ALU.max).then_inc(baton[p], 1)
                                baton_at(29)
                                v.tensor_tensor(xs[:, 3, :], mx, xs[:, 2, :], ALU.subtract).then_inc(baton[p], 1)
                                v.tensor_tensor(xs[:, 4, :], xs[:, 0, :], xs[:, 2, :], ALU.subtract).then_inc(baton[p], 1)
                                baton_at(32)
                                v.tensor_copy(mx, xs[:, 2, :]).then_inc(baton[p], 1)
                                baton_at(33)
                                v.tensor_tensor(state, state, heads(xs[:, 3, :], NT, 65), ALU.mult).then_inc(baton[p], 1)
                                v.tensor_tensor(xsum, xsum, heads(xs[:, 4, :], NT, 65), ALU.mult).then_inc(baton[p], 1)
                                baton_at(35)
                                v.tensor_tensor(state, state, xsum, ALU.add).then_inc(baton[p], 1)
                                baton_at(36)
                                v.tensor_scalar(den2, state[:, :, :, D], 1e-16, None, ALU.add).then_inc(baton[p], 1)
                                baton_at(37)
                                v.reciprocal(den, den).then_inc(baton[p], 1)
                                baton_at(38)
                                v.tensor_tensor(cview, state[:, :, :, 0:D], heads(den, NT, D), ALU.mult)\
                                    .then_inc(baton[p], 1)
                                baton_at(39)
                            further(dve, p, xb, xmaxc, body, prepare)
                            dve.sem_inc(S["state"], 1)
                        next_onehots()
                        if p == 4:
                            for par in range(2):
                                need("mm", par)
                                dve.wait_ge(L["x"][par], loaded(p, "x", g))
                                dve.wait_ge(ST["b"][par], stored_before(p, "b", g))
                                v.tensor_tensor(w2[:, par, :, :], tiles(pb(4 * par + 1, G * D)[0:NT, :], D),
                                                xres[:, par, :, :], ALU.add).then_inc(S["xadd"], 1)
                    if p == 2:
                        for par in range(2):
                            need("mm", par)
                            dve.wait_ge(L["x"][par], loaded(p, "x", g))
                            dve.wait_ge(ST["b"][par], stored_before(p, "b", g))
                            v.tensor_tensor(w2[:, par, :, :], tiles(pb(4 * par + 2, G * D)[0:NT, :], D),
                                            xres[:, par, :, :], ALU.add).then_inc(S["xadd"], 1)

                    if p == 8:
                        for par in range(2):
                            need("e2", par)
                            v.scalar_tensor_tensor(z2[:, par, :], pb(4 * par + 1, G * D), 0.0, z2[:, par, :],
                                                   ALU.min, ALU.subtract).then_inc(S["lsig"], 1)
                        for par in range(2):
                            need("e3", par)
                            v.tensor_tensor(sg[:, par, :, 0:D], tiles(pb(4 * par + 1, G * D), D), tiles(z1[:, par, :], D),
                                            ALU.mult).then_inc(S["silu"], 1)
                        for par in range(2):
                            q = 4 * par
                            sums = tiles(pb(q, G * 65)[0:NT, :], 65)
                            need("agg", par)
                            freed("tr", par)
                            v.tensor_copy(c65[:, par, :, :], sums).then_inc(S["ev"], 1)
                            need("ev", par)

                            def body(j):
                                baton_at(2)
                                xonehots(par, 2)
                                baton_at(13)
                                v.scalar_tensor_tensor(z2[:, par, :], pb(q + 1, G * D), 0.0, z2[:, par, :],
                                                       ALU.min, ALU.subtract).then_inc(baton[p], 1)
                                baton_at(15)
                                v.tensor_tensor(sg[:, par, :, 0:D], tiles(pb(q + 1, G * D), D), tiles(z1[:, par, :], D),
                                                ALU.mult).then_inc(baton[p], 1)
                                baton_at(17)
                                v.tensor_tensor(c65[:, par, :, :], c65[:, par, :, :], sums, ALU.add)\
                                    .then_inc(baton[p], 1)
                                baton_at(18)
                            further(dve, p, xb, xmaxc, body)
                            dve.sem_inc(S["state"], 1)
                        next_onehots()
                        for par in range(2):
                            need("mm", par)
                            u = pb(4 * par + 3, G * NT)[0:D, :]
                            v.tensor_scalar(uz[:, par, :], u, u1b[:, 0:1], None, ALU.add).then_inc(S["ub"], 1)
                        for par in range(2):
                            need("u2", par)
                            need("ub", par)
                            v.scalar_tensor_tensor(ue[:, par, :], uz[:, par, :], 0.0, ue[:, par, :],
                                                   ALU.min, ALU.subtract).then_inc(S["ulsig"], 1)
                        for par in range(2):
                            need("u3", par)
                            freed("mm2", par)
                            v.tensor_tensor(usT[0:D, par, :], uz[:, par, :], ue[:, par, :], ALU.mult).then_inc(S["usilu"], 1)
                        for par in range(2):
                            need("mm2", par)
                            v.tensor_tensor(w2[:, par, :, :], tiles(pb(4 * par, G * D)[0:NT, :], D),
                                            hs66[:, par, :, 0:D], ALU.add).then_inc(S["pre"], 1)

                    if p in (0, 2, 4, 7, 8):
                        rows = xres if p == 0 else w2
                        for par in range(2):
                            if p == 0:
                                dve.wait_ge(L["x"][par], loaded(p, "x", g))
                            else:
                                need("pre" if p == 8 else "xadd", par)
                            v.reduce_sum(small[:, par, 0, 0:G], rows[:, par, :, :], AX).then_inc(S["red"], 1)
                        for par in range(2):
                            need("red", par)
                            v.scalar_tensor_tensor(w0[:, par, :, :], small5(par, 0, D), -1.0 / D, rows[:, par, :, :],
                                                   ALU.mult, ALU.add).then_inc(S["cen"], 1)
                        for par in range(2):
                            need("sq", par)
                            v.reduce_sum(small[:, par, 1, 0:G], w1[:, par, :, :], AX).then_inc(S["var"], 1)
                        if p == 4:
                            for par in range(2):
                                need("rstd", par)
                                v.tensor_tensor(small[:, par, 3, 0:G], small[:, par, 3, 0:G], dinv[:, tile0(par)],
                                                ALU.mult).then_inc(S["rsc"], 1)
                        for par in range(2):
                            need("rsc" if p == 4 else "rstd", par)
                            if p == 8:
                                v.tensor_tensor(w0[:, par, :, :], w0[:, par, :, :], small5(par, 3, D), ALU.mult)\
                                    .then_inc(S["nrm"], 1)
                            else:
                                dve.wait_ge(ST["a"][par], stored_before(p, "a", g))
                                v.scalar_tensor_tensor(w3[:, par, :, :], w0[:, par, :, :], 0.0, small5(par, 3, D),
                                                       ALU.max, ALU.mult).then_inc(S["nrm"], 1)
                    if p == 8:
                        for par in range(2):
                            need("nrm", par)
                            v.tensor_tensor(w1[:, par, :, :], w0[:, par, :, :], bias5("gamma"), ALU.mult).then_inc(S["gam"], 1)
                        for par in range(2):
                            need("gam", par)
                            v.tensor_tensor(w0[:, par, :, :], w1[:, par, :, :], bias5("beta"), ALU.add).then_inc(S["bet"], 1)
                        for par in range(2):
                            need("bet", par)
                            dve.wait_ge(L["x"][par], loaded(p, "x", g))
                            dve.wait_ge(ST["b"][par], stored_before(p, "b", g))
                            v.tensor_tensor(w3[:, par, :, :], w0[:, par, :, :], xres[:, par, :, :], ALU.add)\
                                .then_inc(S["xadd"], 1)
                    hold(dve)


NPASS = 9
PE_STAGES = "tr mm mm2 agg tr_h tr_o mm_g exp_g tr_a tr_p mm_y tr_e mm_z"
ACT_STAGES = "ct out relu exp ht oht gt yt et abs uabs e1 e2 e3 u1 u2 u3 sq ln rstd"
DVE_STAGES = ("oh he ev state state_in deg max rec den xadd prod dot fwd seg sub wm pre prob rsc red cen var nrm gam bet "
              "lsig silu ub ulsig usilu")
POOL_CONSTS = 22
CNT_DONE, SCOL_DONE, FLAG_DONE, WSF_DONE = 25, 28, 32, 37
W_DVE = 11
N_WEIGHT_LOADS = 46


def kernel(**inputs):
    import numpy as _np
    import concourse.bacc as _bacc
    from concourse import mybir as _mybir
    from concourse.bass_utils import run_bass_kernel_spmd as _run

    nc = _bacc.Bacc("TRN2", target_bir_lowering=False, num_devices=1)
    arrays, args = {}, {}
    for name in sorted(inputs):
        x = _np.ascontiguousarray(inputs[name])
        arrays[f"in_{name}_dram"] = x
        args[name] = nc.dram_tensor(f"in_{name}_dram", x.shape, _mybir.dt.from_np(x.dtype), kind="ExternalInput").ap()
    out = nc.dram_tensor("out_0_dram", (N, D), F32, kind="ExternalOutput").ap()
    build(nc, args, out)
    r = _run(nc, [arrays], core_ids=[0])
    return r.results[0]["out_0_dram"]
```

```python
import concourse.bass as bass
from concourse import mybir
from contextlib import ExitStack

N = 50000
E = 50000
D = 64
DH = 128
NT = 100
W = 128
T = N // NT
G = 5
GROUPS = T // G
HI, LO = 20, 25
HB = 8
CH = 125
EPAD = 391 * W + W
PADDST = 1 << 20
BIG = 1.0e30
FLOOR = -1.0e29

F32 = mybir.dt.float32
BF16 = mybir.dt.bfloat16
I32 = mybir.dt.int32
ALU = mybir.AluOpType
ACT = mybir.ActivationFunctionType
AX = mybir.AxisListType.X

LN = "red cen sq var ln rstd nrm "
CONV = ("oh he tr_h ht tr_o oht mm_g gt exp_g prod dot tr_a fwd seg sub exp tr_p wm agg den rec state_in state tr ct mm ")
PASS_STAGES = {
    0: LN,
    1: "oh agg deg max rec ev state tr ct mm out",
    2: "oh agg ev state tr ct mm xadd " + LN,
    3: CONV + "out",
    4: CONV + "xadd rsc " + LN,
    5: "oh agg ev state tr ct mm out",
    6: "oh agg ev state tr ct mm relu mm2 out",
    7: "oh agg ev state pre max sub exp den rec prob xadd tr ct mm out " + LN,
    8: "oh tr_h ht tr_o oht mm_y yt tr_e et mm_z abs e1 e2 lsig e3 silu agg ev state tr ct mm "
       "ub uabs u1 u2 ulsig u3 usilu mm2 pre gam bet xadd " + LN,
}
NAMES = sorted({n for v in PASS_STAGES.values() for n in v.split()})
LOADS = {0: "x", 1: "idx hs", 2: "idx hs x", 3: "idx hs flag", 4: "idx hs flag x", 5: "idx hs", 6: "idx hs",
         7: "idx hs x", 8: "idx hs ea hr x"}
STORES = {0: "a", 1: "a", 2: "a b", 3: "a", 4: "a b", 5: "a", 6: "a", 7: "a b c", 8: "b"}
EDGE_PASSES = range(1, 9)
SKEWED = (3, 4, 8)


def rank(table, p, name):
    return sum(name in table[q].split() for q in range(p))


def start(p, name):
    return 2 + (GROUPS + 2 * (name == "oh")) * rank(PASS_STAGES, p, name)


def done(p, name, g, par):
    return g + (start(p, name) + par + 1)


def before(p, name, g, par):
    return g + (start(p, name) + par - 1)


def ended(table, p, name, per):
    return per * (GROUPS // 2) * rank(table, p + 1, name)


def loaded(p, name, g):
    return 8 * g + (8 * GROUPS * rank(LOADS, p, name) + 16)


def gathered_at(p, g):
    return 8 * G * g + (8 * G * GROUPS * (p - 1) + 32 * G)


def gathered_before(p, g):
    return 8 * G * g + (8 * G * GROUPS * (p - 1) + 16 * G)


def stored_before(p, name, g):
    return 8 * g + (8 * GROUPS * rank(STORES, p, name) + 16)


def build(nc, a, out):
    ctx = ExitStack()
    with ctx:
        ctx.enter_context(nc.allow_non_contiguous_dma(reason="short index columns and biases"))

        def sb(name, shape, dt=F32):
            return ctx.enter_context(nc.sbuf_tensor(name, shape, dt))

        def sem(name):
            return ctx.enter_context(nc.semaphore(name))

        def dram(name, shape, dt=F32):
            return nc.dram_tensor(name, shape, dt, kind="Internal").ap()

        srcpad = dram("srcpad", (EPAD // W, W), I32)
        dstpad = dram("dstpad", (EPAD // W, W), I32)
        eapad = dram("eapad", (EPAD, D))
        cnt_d = dram("cnt_d", (T,))
        srow_d = dram("srow_d", (T,), I32)
        flag_d = dram("flag_d", (T, 2, W))
        Ht = {n: dram(f"h{n}", (N, DH if n == 5 else D)) for n in range(9)}
        X1 = dram("x1", (N, D))
        X2 = dram("x2", (N, D))
        X3 = dram("x3", (N, D))
        prime_d = dram("prime_d", (16, 16))

        def tiles_of(table):
            return table.rearrange("(t p) f -> p t f", p=NT)

        iota_i = sb("iota_i", [128, T], I32)
        iota_f = sb("iota_f", [128, T])
        base_f = sb("base_f", [128, T])
        pcol_i = sb("pcol_i", [128, 1], I32)
        tbase_i = sb("tbase_i", [128, T // CH], I32)
        tbase = sb("tbase", [128, T // CH])
        ident = sb("ident", [128, 128])
        tri = sb("tri", [128, 128])
        ones = sb("ones", [128, 128])
        epsc = sb("epsc", [128, 2])
        srcw = sb("srcw", [128, T], I32)
        drel = sb("drel", [128, T + 2 * G])
        deg = sb("deg", [NT, T])
        invdeg = sb("invdeg", [NT, T])
        dinv = sb("dinv", [NT, T])
        hasedge = sb("hasedge", [NT, T])
        maxc_f = sb("maxc_f", [1, GROUPS // 2])
        maxc = sb("maxc", [1, GROUPS // 2], I32)
        srow = sb("srow", [1, T], I32)
        sage_w = [sb(f"sage_w{l}", [128, D]) for l in range(2)]
        brow = {n: sb(f"brow_{n}", [1, G, w]) for n, w in (("s0", D), ("s1", D), ("g1", DH))}
        bias_b = {n: sb(f"bias_{n}", [NT, D]) for n in ("g3", "gamma", "beta")}
        cw = sb("cw", [65, 2, 4, 128])
        cwT = sb("cwT", [64, 2, 2, 2, 65])
        qk = sb("qk", [66, 2, 2, 65])
        vw = sb("vw", [128, 2, D])
        sw = sb("sw", [66, 2, D])
        bvrow = sb("bvrow", [1, 2, 2, D])
        swrow = sb("swrow", [1, 2, D])
        g1w = sb("g1w", [128, D])
        g2w = sb("g2w", [128, 128])
        g3w = sb("g3w", [64, 128])
        g1t = sb("g1t", [64, 128])
        g2t = sb("g2t", [128, 128])
        g3t = sb("g3t", [128, D])
        g2b = sb("g2b", [128, 1])
        m1w = sb("m1w", [65, 3, D])
        m2w = sb("m2w", [65, D])
        m2T = sb("m2T", [64, 65])
        u1w = sb("u1w", [64, D])
        u1b = sb("u1b", [64, 1])
        mu = sb("mu", [65, D])
        u2w = sb("u2w", [65, D])

        nidx = sb("nidx", [128, 2, G], I32)
        m65 = sb("m65", [128, 2, G, 65])
        m128 = sb("m128", [128, 2, G, 128])
        oh = sb("oh", [128, 2, G, NT])
        ohT = sb("ohT", [NT, 2, G * W])
        c128 = sb("c128", [NT, 2, G, 128])
        c65 = sb("c65", [NT, 2, G, 65])
        ctb = sb("ctb", [128, 2, G * NT])
        hs66 = sb("hs66", [NT, 2, G, 66])
        hsb = sb("hsb", [NT, 2, G * 128])
        xres = sb("xres", [NT, 2, G, D])
        w0, w1, w2, w3 = (sb(f"w{k}", [NT, 2, G, D]) for k in range(4))
        w3b = sb("w3b", [NT, 2, G, DH])
        wc = sb("wc", [NT, 2, G, D])
        small = sb("small", [NT, 2, 8, 2 * G])
        hT = sb("hT", [66, 2, G * NT])
        gS = sb("gS", [NT, 2, G * 130])
        pr = sb("pr", [128, 2, G, 2, 65])
        al = sb("al", [128, 2, 2 * G])
        rowm = sb("rowm", [2 * G, 2, 4, W])
        flags = sb("flags", [2 * G, 2, 2, W])
        h6T = sb("h6T", [128, 2, G * NT])
        eT = sb("eT", [64, 2, G * W])
        ea = sb("ea", [128, 2, G, D])
        ysb = sb("ysb", [NT, 2, G * D])
        z1, z2 = (sb(f"z{k}", [128, 2, G * D]) for k in (1, 2))
        sg = sb("sg", [128, 2, G, 65])
        uz, ue = (sb(f"u{k}", [64, 2, G * NT]) for k in "ze")
        usT = sb("usT", [65, 2, G * NT])
        xsrc = sb("xsrc", [128, G], I32)
        xdst = sb("xdst", [128, G], I32)
        xdf = sb("xdf", [128, G])
        xrow = sb("xrow", [2 * G, W], I32)
        xrf = sb("xrf", [2 * G, W])
        xflag = sb("xflag", [2 * G, 2, W])
        xm65 = sb("xm65", [128, G, 65])
        xm128 = sb("xm128", [128, G, 128])
        xoh = sb("xoh", [128, G, NT])
        xt = sb("xt", [NT, G * 130])
        xstate = sb("xstate", [NT, G * 130])
        xea = sb("xea", [128, G, D])
        xcol = sb("xcol", [128, 3, 2 * G])
        xs = sb("xs", [NT, 6, 2 * G])
        fillc = sb("fillc", [128, 2, 16], I32)
        fillz = sb("fillz", [128, 2 * D])
        zb = sb("zb", [128, 128], BF16)
        dlist = sb("dlist", [CH, E // CH], I32)
        dwork = sb("dwork", [CH, E // CH], I32)
        scol_i = sb("scol_i", [CH, T // CH], I32)
        wsrc = sb("wsrc", [CH, T // CH, W], I32)
        wdst = sb("wdst", [CH, T // CH, W], I32)
        drelw = sb("drelw", [CH, T // CH, W])
        wsf = sb("wsf", [CH, T // CH, W])
        flagw = sb("flagw", [CH, T // CH, 2, W])
        hq = [sb(f"hq{k}", [CH, E // CH]) for k in range(4)]
        ohh = sb("ohh", [CH, 2, HB, HI], BF16)
        ohl = sb("ohl", [CH, 2, HB, LO], BF16)
        cnt_s = sb("cnt_s", [HI, LO])
        cntc = sb("cntc", [CH, T // CH])
        crow = sb("crow", [1, T])

        P = ctx.enter_context(nc.psum_tensor("psum_all", [128, 8 * 512], F32))

        def pb(k, cols=512, off=0):
            return P[:, k * 512 + off:k * 512 + off + cols]

        def tiles(x, f):
            return x.rearrange("p (u f) -> p u f", f=f)

        IN_BANKS = ((0, 3), (3, G))

        def of_bank(k, part, rows):
            u0, u1 = IN_BANKS[part]
            return pb(k + part, (u1 - u0) * 130)[0:rows, :].rearrange("p (u h f) -> p u h f", h=2, f=65)

        def of_tile(k, u):
            return pb(k + u // 3, 130, (u % 3) * 130)

        S = {n: sem(f"st_{n}") for n in NAMES}
        L = {n: [sem(f"loaded_{n}{par}") for par in range(2)] for n in ("idx", "hs", "hr", "x", "flag", "ea")}
        ST = {n: [sem(f"stored_{n}{par}") for par in range(2)] for n in "abc"}
        gathered = [sem(f"gathered{par}") for par in range(2)]
        s_load = sem("weights_loaded")
        w_pe = sem("weights_pe")
        w_dve = sem("weights_dve")
        s_vrow = sem("mean_bv_moved")
        s_list = sem("edge_list_loaded")
        s_pad = sem("edge_lists_padded")
        s_ea = sem("edge_features_padded")
        s_fill = sem("fill_ready")
        s_sw = sem("small_products")
        pool_c = sem("pool_consts")
        s_dve = sem("dve_setup")
        s_act = sem("act_setup")
        s_pe = sem("pe_setup")
        q_ready = sem("hist_onehots_ready")
        q_used = sem("hist_onehots_used")
        s_cnt = sem("counts_moved")
        s_srow = sem("window_starts_moved")
        s_flag = sem("flags_stored")
        s_win = sem("windows_gathered")
        tables = sem("tables_ready")
        held = sem("held")
        primed = sem("stages_primed")
        x_in = sem("further_inputs")
        x_g = sem("further_gathered")
        baton = {p: sem(f"baton{p}") for p in EDGE_PASSES}

        SELF = {1: Ht[0], 2: Ht[1], 3: Ht[2], 4: Ht[3], 5: Ht[4], 6: Ht[5], 7: Ht[6], 8: Ht[7]}
        TABLE = dict(SELF)
        TABLE[8] = Ht[8]
        XIN = {0: a["x"], 2: a["x"], 4: X1, 7: X2, 8: X3}
        OUTA = {p: Ht[p] for p in range(8)}
        OUTB = {2: X1, 4: X2, 7: X3, 8: out}
        OUTC = {7: Ht[8]}

        def pass_written(eng, p):
            for n in STORES[p].split():
                for par in range(2):
                    eng.wait_ge(ST[n][par], 16 + ended(STORES, p, n, 16))

        def hold(eng):
            eng.sem_inc(held, 1)

        XSTEPS = {1: (1, 11), 2: (0, 8), 3: (7, 39), 4: (7, 39), 5: (0, 8), 6: (0, 8), 7: (0, 8), 8: (0, 18)}

        def further(eng, p, xb, xmaxc, body, prepare=None):
            first, each = XSTEPS[p]
            hold(eng)
            with eng.If(xmaxc > W):
                if prepare is not None:
                    prepare()
                    hold(eng)
                if first:
                    eng.reg_add(xb, xb, first)
                with eng.Fori(W, xmaxc, W) as j:
                    body(j)
                    hold(eng)
                    eng.reg_add(xb, xb, each)

        def skewed(eng, half, tails):
            def job(par, i):
                return par, i, i * 2

            half(job(0, 0), None, None)
            half(job(1, 0), job(0, 0), None)
            with eng.Fori(0, GROUPS // 2 - 1) as i:
                half(job(0, i + 1), job(1, i), job(0, i) if tails else None)
                half(job(1, i + 1), job(0, i + 1), job(1, i) if tails else None)
            last = GROUPS // 2 - 1
            half(None, job(1, last), job(0, last) if tails else None)
            if tails:
                half(None, None, job(1, last))

        def at(eng, xb, k):
            return eng.snap(xb, min_val=1, max_val=1 << 30) + k

        block = ctx.enter_context(nc.Block())

        @block.sync
        def _(sp):
            sp.dma_start(dlist[:, :], a["dst"].rearrange("(p t) -> p t", p=CH)).then_inc(s_list, 16)
            for l in range(2):
                sp.dma_start(sage_w[l][0:D, :], a[f"L0_gnn_W_neigh{l}"]).then_inc(s_load, 16)
                sp.dma_start(sage_w[l][D:128, :], a[f"L0_gnn_W_self{l}"]).then_inc(s_load, 16)
                for k, n in enumerate("qkvs"):
                    wide = D if n == "s" else DH
                    sp.dma_start(cw[0:D, l, k, 0:wide], a[f"L1_gnn_l{l + 1}_w{n}"]).then_inc(s_load, 16)
                    sp.dma_start(cw[D:D + 1, l, k, 0:wide],
                                 a[f"L1_gnn_l{l + 1}_b{n}"].rearrange("(o n) -> o n", o=1)).then_inc(s_load, 16)
                for h in range(2):
                    sp.dma_start(vw[h * D:(h + 1) * D, l, :], a[f"L1_gnn_l{l + 1}_wv"][:, h * D:(h + 1) * D])\
                      .then_inc(s_load, 16)
                sp.dma_start(bvrow[0:1, l, :, :], a[f"L1_gnn_l{l + 1}_bv"].rearrange("(o h n) -> o h n", o=1, h=2))\
                  .then_inc(s_load, 16)
            for n, key in (("s0", "L0_gnn_b0"), ("s1", "L0_gnn_b1"), ("g1", "L2_gnn_b1")):
                wide = DH if n == "g1" else D
                sp.dma_start(brow[n][0:1, :, :], a[key].rearrange("(o u n) -> o u n", o=1, u=1)
                             .broadcast_to([1, G, wide])).then_inc(s_load, 16)
            for n, key in (("g3", "L2_gnn_b3"), ("gamma", "L3_gnn_ln_gamma"), ("beta", "L3_gnn_ln_beta")):
                sp.dma_start(bias_b[n][:, :], a[key].rearrange("(o n) -> o n", o=1).broadcast_to([NT, D]))\
                  .then_inc(s_load, 16)
            sp.dma_start(g1w[:, :], a["L2_gnn_W1"]).then_inc(s_load, 16)
            sp.dma_start(g2w[:, :], a["L2_gnn_W2"]).then_inc(s_load, 16)
            sp.dma_start(g3w[:, :], a["L2_gnn_W3"]).then_inc(s_load, 16)
            sp.dma_start(g2b[:, :], a["L2_gnn_b2"].rearrange("(n o) -> n o", o=1)).then_inc(s_load, 16)
            for k in range(3):
                sp.dma_start(m1w[0:D, k, :], a["L3_gnn_W_m1"][k * D:(k + 1) * D, :]).then_inc(s_load, 16)
            sp.dma_start(m1w[D:D + 1, 1, :], a["L3_gnn_b_m1"].rearrange("(o n) -> o n", o=1)).then_inc(s_load, 16)
            sp.dma_start(m2w[0:D, :], a["L3_gnn_W_m2"]).then_inc(s_load, 16)
            sp.dma_start(m2w[D:D + 1, :], a["L3_gnn_b_m2"].rearrange("(o n) -> o n", o=1)).then_inc(s_load, 16)
            sp.dma_start(u1w[:, :], a["L3_gnn_W_u1"]).then_inc(s_load, 16)
            sp.dma_start(u1b[:, :], a["L3_gnn_b_u1"].rearrange("(n o) -> n o", o=1)).then_inc(s_load, 16)
            sp.dma_start(u2w[0:D, :], a["L3_gnn_W_u2"]).then_inc(s_load, 16)
            sp.dma_start(u2w[D:D + 1, :], a["L3_gnn_b_u2"].rearrange("(o n) -> o n", o=1)).then_inc(s_load, 16)
            for pad, lst in ((srcpad, a["src"]), (dstpad, a["dst"])):
                sp.dma_start(pad.rearrange("a b -> (a b)")[0:E].rearrange("(p t) -> p t", p=80),
                             lst.rearrange("(p t) -> p t", p=80)).then_inc(s_pad, 16)
            sp.wait_ge(s_fill, 3)
            for pad, fill in ((srcpad, 0), (dstpad, 1)):
                sp.dma_start(pad.rearrange("a b -> (a b)")[E:EPAD].rearrange("(p t) -> p t", p=16),
                             fillc[0:16, fill, 0:(EPAD - E) // 16]).then_inc(s_pad, 16)
            sp.dma_start(eapad[E:EPAD, :].rearrange("(p t) f -> p (t f)", p=88), fillz[0:88, :]).then_inc(s_pad, 16)
            sp.wait_ge(w_dve, 1)
            sp.dma_start(sw[D + 1:D + 2, :, :], swrow[0:1, :, :]).then_inc(s_vrow, 16)
            sp.wait_ge(s_dve, CNT_DONE)
            sp.dma_start(cnt_d.rearrange("(h l) -> h l", l=LO), cnt_s[:, :]).then_inc(s_cnt, 16)
            sp.wait_ge(s_cnt, 16)
            sp.dma_start(cntc[:, :], cnt_d.rearrange("(c p) -> p c", p=CH)).then_inc(s_cnt, 16)
            sp.dma_start(crow[:, :], cnt_d.rearrange("(o t) -> o t", o=1)).then_inc(s_cnt, 16)
            sp.wait_ge(s_dve, SCOL_DONE)
            sp.dma_start(srow_d.rearrange("(c p) -> p c", p=CH), scol_i[:, :]).then_inc(s_srow, 16)
            sp.wait_ge(s_srow, 16)
            sp.dma_start(srow[:, :], srow_d.rearrange("(o t) -> o t", o=1)).then_inc(s_srow, 16)
            sp.dma_start(eapad[0:E, :].rearrange("(p t) f -> p (t f)", p=80),
                         a["edge_attr_64"].rearrange("(p t) f -> p (t f)", p=80)).then_inc(s_ea, 16)
            sp.wait_ge(s_dve, FLAG_DONE)
            sp.dma_start(flag_d.rearrange("(c p) s w -> p c s w", p=CH), flagw[:, :, :, :]).then_inc(s_flag, 16)
            sp.wait_ge(s_flag, 16)
            sp.wait_ge(s_srow, 32)
            sp.wait_ge(tables, 1)
            sp.wait_ge(primed, 4)

            xin = sp.alloc_register("xin")
            sp.reg_mov(xin, 0)
            xb = sp.alloc_register("xb_sp")
            st = sp.alloc_register("xstart")
            srcflat = srcpad.rearrange("a (b o) -> (a b) o", o=1)
            dstflat = dstpad.rearrange("a (b o) -> (a b) o", o=1)
            for p in range(NPASS):
                if p:
                    pass_written(sp, p - 1)
                    sp.reg_mov(xb, 1)
                    sp.sem_inc(baton[p], 1)
                if p == 8:
                    sp.wait_ge(s_ea, 16)
                names = LOADS[p].split()
                def early(par, g):
                    tile0 = bass.ds(g * G + par * G, G)
                    if "idx" in names:
                        sp.wait_ge(gathered[par], gathered_before(p, g))
                        sp.dma_start(nidx[:, par, :], srcw[:, tile0]).then_inc(L["idx"][par], 16)
                    if "hs" in names:
                        table = tiles_of(SELF[p])[:, tile0, :]
                        reader = {1: "tr", 2: "tr", 3: "tr_h", 4: "tr_h", 5: "agg", 6: "agg", 7: "agg", 8: "tr_h"}[p]
                        into = {1: c128[:, par, :, D:128], 2: c128[:, par, :, D:128], 3: hs66[:, par, :, 0:D],
                                4: hs66[:, par, :, 0:D], 5: tiles(hsb[:, par, 0:G * D], D),
                                6: tiles(hsb[:, par, :], DH), 7: tiles(hsb[:, par, 0:G * D], D),
                                8: hs66[:, par, :, 0:D]}[p]
                        sp.wait_ge(S[reader], before(p, reader, g, par))
                        sp.dma_start(into, table).then_inc(L["hs"][par], 16)
                    if "ea" in names:
                        sp.wait_ge(S["tr_e"], before(p, "tr_e", g, par))
                        hold(sp)
                        for u in range(G):
                            s0 = sp.value_load(srow[0:1, bass.ds(g * G + (par * G + u), 1)], min_val=0, max_val=E)
                            sp.dma_start(ea[:, par, u, :], eapad[bass.ds(s0, W), :]).then_inc(L["ea"][par], 16)
                    if "flag" in names:
                        sp.wait_ge(S["seg"], before(p, "seg", g, par))
                        for h in range(2):
                            sp.dma_start(flags[h * G:(h + 1) * G, par, :, :], flag_d[tile0, :, :])\
                              .then_inc(L["flag"][par], 16)

                def late(par, g):
                    tile0 = bass.ds(g * G + par * G, G)
                    if "hr" in names:
                        sp.wait_ge(S["pre"], before(p, "pre", g, par))
                        sp.dma_start(tiles(hsb[:, par, 0:G * D], D), tiles_of(SELF[p])[:, tile0, :]).then_inc(L["hr"][par], 16)
                    if "x" in names:
                        reader = "cen" if p == 0 else "xadd"
                        sp.wait_ge(S[reader], before(p, reader, g, par))
                        sp.dma_start(xres[:, par, :, :], tiles_of(XIN[p])[:, tile0, :]).then_inc(L["x"][par], 16)

                def windows(par, i):
                    g = i * 2
                    xmaxc = sp.value_load(maxc[0:1, bass.ds(i, 1)], min_val=0, max_val=E)
                    def body(j):
                        sp.wait_ge(baton[p], at(sp, xb, 0))
                        hold(sp)
                        loads = 0
                        for u in range(G):
                            s0 = sp.value_load(srow[0:1, bass.ds(g * G + (par * G + u), 1)], min_val=0, max_val=E)
                            sp.reg_alu(st, s0 + j, E, ALU.min)
                            s1 = sp.snap(st, min_val=0, max_val=E)
                            sp.dma_start(xsrc[:, u:u + 1], srcflat[bass.ds(s1, W), :]).then_inc(x_in, 16)
                            sp.dma_start(xdst[:, u:u + 1], dstflat[bass.ds(s1, W), :]).then_inc(x_in, 16)
                            loads += 2
                            if p in (3, 4):
                                for h in range(2):
                                    sp.dma_start(xrow[h * G + u:h * G + u + 1, :],
                                                 dstpad.rearrange("(o a) b -> o (a b)", o=1)[:, bass.ds(s1, W)])\
                                      .then_inc(x_in, 16)
                                loads += 2
                            if p == 8:
                                sp.dma_start(xea[:, u, :], eapad[bass.ds(s1, W), :]).then_inc(x_in, 16)
                                loads += 1
                        sp.reg_add(xin, xin, 16 * loads)
                        sp.wait_ge(x_in, sp.snap(xin, min_val=1, max_val=1 << 30))
                        sp.sem_inc(baton[p], 1)
                    further(sp, p, xb, xmaxc, body)

                if p in SKEWED:
                    early(0, 0)
                    late(0, 0)
                    early(1, 0)
                    with sp.Fori(0, GROUPS // 2 - 1) as i:
                        windows(0, i)
                        early(0, i * 2 + 2)
                        late(1, i * 2)
                        windows(1, i)
                        early(1, i * 2 + 2)
                        late(0, i * 2 + 2)
                    windows(0, GROUPS // 2 - 1)
                    late(1, GROUPS - 2)
                    windows(1, GROUPS // 2 - 1)
                else:
                    with sp.Fori(0, GROUPS // 2) as i:
                        for par in range(2):
                            early(par, i * 2)
                        for par in range(2):
                            late(par, i * 2)
                        if p:
                            for par in range(2):
                                windows(par, i)
            pass_written(sp, NPASS - 1)

        @block.gpsimd
        def _(pool):
            k = 0

            def const(ins):
                nonlocal k
                k += 1
                ins.then_inc(pool_c, 1)
                pool.wait_ge(pool_c, k)

            const(nc.gpsimd.memset(fillc[:, 0, :], 0))
            const(nc.gpsimd.memset(fillc[:, 1, :], PADDST))
            const(nc.gpsimd.memset(fillz[:, :], 0.0))
            pool.sem_inc(s_fill, 3)
            const(nc.gpsimd.iota(iota_i[:, :], pattern=[[1, T]], base=0, channel_multiplier=0))
            const(nc.gpsimd.iota(pcol_i[:, :], pattern=[[0, 1]], base=0, channel_multiplier=1))
            const(nc.gpsimd.iota(tbase_i[:, :], pattern=[[NT * CH, T // CH]], base=0, channel_multiplier=NT))
            const(nc.gpsimd.memset(ident[:, :], 0.0))
            const(nc.gpsimd.affine_select(out=ident[:, :], in_=ident[:, :], compare_op=ALU.not_equal, fill=1.0, base=0,
                                          pattern=[[-1, 128]], channel_multiplier=1))
            const(nc.gpsimd.memset(ones[:, :], 1.0))
            const(nc.gpsimd.affine_select(out=tri[:, :], in_=ones[:, :], compare_op=ALU.is_gt, fill=0.0, base=0,
                                          pattern=[[1, 128]], channel_multiplier=-1))
            const(nc.gpsimd.memset(epsc[:, 0:1], 1e-5))
            const(nc.gpsimd.memset(epsc[:, 1:2], 1.0))
            const(nc.gpsimd.memset(zb[:, :], 0.0))
            const(nc.gpsimd.memset(m65[:, :, :, :], 1.0))
            const(nc.gpsimd.memset(xm65[:, :, :], 1.0))
            const(nc.gpsimd.memset(hs66[:, :, :, :], 1.0))
            const(nc.gpsimd.memset(sg[:, :, :, :], 1.0))
            const(nc.gpsimd.memset(usT[:, :, :], 1.0))
            const(nc.gpsimd.memset(qk[:, :, :, :], 0.0))
            const(nc.gpsimd.memset(xflag[:, :, :], -BIG))
            const(nc.gpsimd.memset(flagw[:, :, :, :], -BIG))
            const(nc.gpsimd.memset(drel[:, T:T + 2 * G], 0.0))
            assert k == POOL_CONSTS
            pool.wait_ge(s_pad, 80)
            pool.wait_ge(s_dve, SCOL_DONE)
            for c in range(T // CH):
                for into, pad in ((wsrc, srcpad), (wdst, dstpad)):
                    pool.indirect_dma_start(into[:, c, :], None, pad,
                                            bass.IndirectOffsetOnAxis(ap=scol_i[:, c:c + 1], axis=1)).then_inc(s_win, 16)
            pool.wait_ge(tables, 1)
            for par in range(2):
                for u in range(G):
                    pool.indirect_dma_start(m65[:, par, u, 0:D], None, a["x"],
                                            bass.IndirectOffsetOnAxis(ap=pcol_i[:, 0:1], axis=0)).then_inc(gathered[par], 16)
                pool.wait_ge(gathered[par], 16 * G)
            pool.sem_inc(primed, 1)
            pool.wait_ge(primed, 4)
            xg = pool.alloc_register("xg")
            pool.reg_mov(xg, 0)
            xb = pool.alloc_register("xb_pool")
            for p in range(1, NPASS):
                pass_written(pool, p - 1)
                pool.reg_mov(xb, 1)
                table, width = TABLE[p], (DH if p == 6 else D)
                rows, xrows = (m128, xm128) if p == 6 else (m65, xm65)
                reader = "mm_z" if p == 8 else "wm" if p in (3, 4) else "agg"
                def gather(par, g):
                    pool.wait_ge(L["idx"][par], loaded(p, "idx", g))
                    pool.wait_ge(S[reader], before(p, reader, g, par))
                    hold(pool)
                    for u in range(G):
                        pool.indirect_dma_start(rows[:, par, u, 0:width], None, table,
                                                bass.IndirectOffsetOnAxis(ap=nidx[:, par, u:u + 1], axis=0))\
                            .then_inc(gathered[par], 16)

                def windows(par, i):
                    xmaxc = pool.value_load(maxc[0:1, bass.ds(i, 1)], min_val=0, max_val=E)

                    def body(j):
                        pool.wait_ge(baton[p], at(pool, xb, 1))
                        hold(pool)
                        for u in range(G):
                            pool.indirect_dma_start(xrows[:, u, 0:width], None, table,
                                                    bass.IndirectOffsetOnAxis(ap=xsrc[:, u:u + 1], axis=0))\
                                .then_inc(x_g, 16)
                        pool.reg_add(xg, xg, 16 * G)
                        pool.wait_ge(x_g, pool.snap(xg, min_val=1, max_val=1 << 30))
                        pool.sem_inc(baton[p], 1)
                    further(pool, p, xb, xmaxc, body)

                if p in SKEWED:
                    gather(0, 0)
                    gather(1, 0)
                    with pool.Fori(0, GROUPS // 2 - 1) as i:
                        for par in range(2):
                            windows(par, i)
                            gather(par, i * 2 + 2)
                    for par in range(2):
                        windows(par, GROUPS // 2 - 1)
                else:
                    with pool.Fori(0, GROUPS // 2) as i:
                        for par in range(2):
                            gather(par, i * 2)
                        for par in range(2):
                            windows(par, i)

        @block.tensor
        def _(pe):
            mm, turn = nc.tensor.matmul, nc.tensor.transpose

            pe.wait_ge(pool_c, POOL_CONSTS)
            mm(pb(0, LO)[0:HI, :], zb[0:CH, 0:HI], zb[0:CH, 0:LO], start=True, stop=False)
            pe.sem_inc(q_used, 2)
            with pe.Fori(0, E // CH // HB // 2) as t2:
                for k in range(2):
                    pe.wait_ge(q_ready, 4 * t2 + (2 * k + 2))
                    for n in range(HB):
                        ins = mm(pb(0, LO)[0:HI, :], ohh[:, k, n, :], ohl[:, k, n, :], start=False, stop=False)
                    ins.then_inc(q_used, 1)
            mm(pb(0, LO)[0:HI, :], zb[0:CH, 0:HI], zb[0:CH, 0:LO], start=False, stop=True).then_inc(s_pe, 1)

            pe.wait_ge(s_load, 16 * N_WEIGHT_LOADS)
            for l in range(2):
                for k in range(2):
                    for h in range(2):
                        turn(pb(6 + l, 65, (k * 2 + h) * 65)[0:D, :], cw[:, l, k, h * D:(h + 1) * D], ident[0:65, 0:65])
            turn(pb(5, 128)[0:D, :], g1w[:, :], ident[:, :])
            turn(pb(5, 128, 128), g2w[:, :], ident[:, :])
            turn(pb(5, D, 256), g3w[:, :], ident[0:D, 0:D])
            turn(pb(5, 65, 320)[0:D, :], m2w[:, :], ident[0:65, 0:65]).then_inc(w_pe, 1)
            pe.wait_ge(w_dve, 7)
            for l in range(2):
                for h in range(2):
                    mm(pb(6, 65, (l * 2 + h) * 65)[0:65, :], cwT[:, l, 0, h, :], cwT[:, l, 1, h, :], start=True, stop=True)
            mm(pb(5, D)[0:65, :], m2T[:, :], u1w[:, :], start=True, stop=True).then_inc(w_pe, 1)

            pe.wait_ge(s_cnt, 48)
            for c in range(T // CH):
                ins = mm(pb(3, 1, c)[0:CH, :], tri[0:CH, 0:CH], cntc[:, c:c + 1], start=True, stop=c == 0)
                for d in range(c):
                    ins = mm(pb(3, 1, c)[0:CH, :], ones[0:CH, 0:CH], cntc[:, d:d + 1], start=False, stop=d == c - 1)
            ins.then_inc(s_pe, 1)
            pe.wait_ge(s_dve, WSF_DONE)
            for c in range(T // CH):
                turn(pb(4, CH, c * CH), wsf[:, c, :], ident[0:CH, 0:CH])
                ins = turn(pb(5, CH, c * CH), drelw[:, c, :], ident[0:CH, 0:CH])
            ins.then_inc(s_pe, 1)
            for n in PE_STAGES.split():
                pe.sem_inc(S[n], 2)
            pe.sem_inc(primed, 1)
            pe.wait_ge(primed, 4)
            pe.wait_ge(w_dve, W_DVE)
            pe.wait_ge(s_vrow, 16)

            xb = pe.alloc_register("xb_pe")

            def turn_onehots(q, onehot):
                for u in range(G):
                    ins = turn(pb(q + 2 + u // 4, W, (u % 4) * W)[0:NT, :], onehot[:, u, :], ident[:, :])
                return ins

            def node_to_edge(q, par):
                for u in range(G):
                    ins = mm(of_tile(q + 2, u), ohT[:, par, u * W:(u + 1) * W],
                             gS[:, par, u * 130:(u + 1) * 130], start=True, stop=True)
                return ins

            def weighted_sums(q, par, onehot):
                for u in range(G):
                    ins = mm(of_tile(q + 2, u)[0:NT, :], onehot[:, u, :], pr[:, par, u, :, :].rearrange("p h f -> p (h f)"),
                             start=True, stop=True)
                return ins

            def turn_rows(q, par, flag_rows):
                turn(pb(q, 2 * G), rowm[:, par, 1, :], ident[0:2 * G, 0:2 * G])
                return turn(pb(q, 2 * G, 16), flag_rows, ident[0:2 * G, 0:2 * G])

            def pick(q, onehot):
                for k in range(2):
                    for h in range(2):
                        for u in range(G):
                            c = h * G + u
                            ins = mm(pb(q, 1, 32 + 16 * k + c)[0:NT, :], onehot[:, u, :], xcol[:, 1 - k, c:c + 1],
                                     start=True, stop=True)
                return ins

            def turn_features(q, e):
                for u in range(G):
                    ins = turn(pb(q + 2 + u // 4, W, (u % 4) * W)[0:D, :], e[:, u, :], ident[:, :])
                return ins

            def messages(q, par, rows):
                mm(pb(q + 1, G * D), ident[:, :], rows[:, :, 0:D], start=True, stop=False)
                for u in range(G):
                    o = pb(q + 1, D, u * D)
                    mm(o, ohT[:, par, u * W:(u + 1) * W], ysb[:, par, u * D:(u + 1) * D], start=False, stop=False)
                    ins = mm(o, eT[:, par, u * W:(u + 1) * W], m1w[0:D, 2, :], start=False, stop=u == G - 1)
                return ins

            def message_sums(q, par, onehot):
                for u in range(G):
                    ins = mm(pb(q, 65, u * 65)[0:NT, :], onehot[:, u, :], sg[:, par, u, :], start=True, stop=True)
                return ins

            def conv_half(p, front, back, tail):
                l = p - 3
                end = "out" if p == 3 else "xadd"

                def need(name, job):
                    pe.wait_ge(S[name], done(p, name, job[2], job[0]))

                def freed(name, job):
                    pe.wait_ge(S[name], before(p, name, job[2], job[0]))

                f = 4 * front[0] if front else None
                if front:
                    par = front[0]
                    need("he", front)
                    pe.wait_ge(L["hs"][par], loaded(p, "hs", front[2]))
                    freed("ct", front)
                    freed(end, front)
                    hold(pe)
                    for u in range(G):
                        ins = turn(pb(f, NT, u * NT)[0:66, :], hs66[:, par, u, :], ident[0:NT, 0:NT])
                    ins.then_inc(S["tr_h"], 1)
                if front:
                    par = front[0]
                    need("oh", front)
                    freed("den", front)
                    freed("state_in", front)
                    turn_onehots(f, oh[:, par, :, :]).then_inc(S["tr_o"], 1)
                if back:
                    par = back[0]
                    need("exp", back)
                    hold(pe)
                    turn(pb(4 * par + 1, 2 * G), rowm[:, par, 3, :], ident[0:2 * G, 0:2 * G]).then_inc(S["tr_p"], 1)
                if front:
                    par = front[0]
                    need("ht", front)
                    for u in range(G):
                        ins = mm(of_tile(f, u)[0:NT, :], hT[:, par, u * NT:(u + 1) * NT],
                                 qk[:, l, :, :].rearrange("p h f -> p (h f)"), start=True, stop=True)
                    ins.then_inc(S["mm_g"], 1)
                if back:
                    par, i, g = back
                    q = 4 * par
                    xmaxc = pe.value_load(maxc[0:1, bass.ds(i, 1)], min_val=0, max_val=E)
                    need("wm", back)
                    weighted_sums(q, par, oh[:, par, :, :]).then_inc(S["agg"], 1)

                    def prepare():
                        pe.wait_ge(baton[p], at(pe, xb, 1))
                        hold(pe)
                        turn_rows(q, par, flags[:, par, 1, :]).then_inc(baton[p], 1)
                        pe.wait_ge(baton[p], at(pe, xb, 4))
                        hold(pe)
                        pick(q, oh[:, par, :, :]).then_inc(baton[p], 1)

                    def body(j):
                        pe.wait_ge(baton[p], at(pe, xb, 8))
                        hold(pe)
                        turn_onehots(q, xoh).then_inc(baton[p], 1)
                        pe.wait_ge(baton[p], at(pe, xb, 10))
                        hold(pe)
                        node_to_edge(q, par).then_inc(baton[p], 1)
                        pe.wait_ge(baton[p], at(pe, xb, 13))
                        hold(pe)
                        turn(pb(q, W)[0:2 * G, :], al[:, par, :], ident[:, :]).then_inc(baton[p], 1)
                        pe.wait_ge(baton[p], at(pe, xb, 18))
                        hold(pe)
                        turn(pb(q + 1, 2 * G), rowm[:, par, 3, :], ident[0:2 * G, 0:2 * G])\
                            .then_inc(baton[p], 1)
                        pe.wait_ge(baton[p], at(pe, xb, 20))
                        hold(pe)
                        weighted_sums(q, par, xoh).then_inc(baton[p], 1)
                        hold(pe)
                        turn_rows(q, par, xflag[:, 1, :]).then_inc(baton[p], 1)
                        pe.wait_ge(baton[p], at(pe, xb, 24))
                        hold(pe)
                        pick(q, xoh).then_inc(baton[p], 1)
                    further(pe, p, xb, xmaxc, body, prepare)
                if front:
                    need("gt", front)
                    need("oht", front)
                    node_to_edge(f, front[0]).then_inc(S["exp_g"], 1)
                if back:
                    need("state", back)
                    for u in range(G):
                        ins = turn(pb(q, NT, u * NT), c128[:, par, u, :], ident[0:NT, 0:NT])
                    ins.then_inc(S["tr"], 1)
                    need("ct", back)
                    for u in range(G):
                        cols = slice(u * NT, (u + 1) * NT)
                        o = pb(q + 1, D, u * D)[0:NT, :]
                        mm(o, ctb[:, par, cols], vw[:, l, :], start=True, stop=False)
                        ins = mm(o, hT[:, par, cols], sw[:, l, :], start=False, stop=True)
                    ins.then_inc(S["mm"], 1)
                if front:
                    need("dot", front)
                    turn(pb(f, W)[0:2 * G, :], al[:, front[0], :], ident[:, :]).then_inc(S["tr_a"], 1)

            def message_half(p, front, back, tail):
                def need(name, job):
                    pe.wait_ge(S[name], done(p, name, job[2], job[0]))

                def freed(name, job):
                    pe.wait_ge(S[name], before(p, name, job[2], job[0]))

                if front:
                    par = front[0]
                    f = 4 * par
                    pe.wait_ge(L["hs"][par], loaded(p, "hs", front[2]))
                    freed("pre", front)
                    for u in range(G):
                        ins = turn(pb(f, NT, u * NT)[0:65, :], hs66[:, par, u, 0:65], ident[0:NT, 0:NT])
                    ins.then_inc(S["tr_h"], 1)
                if front:
                    par = front[0]
                    need("oh", front)
                    freed("ub", front)
                    turn_onehots(f, oh[:, par, :, :]).then_inc(S["tr_o"], 1)
                if back:
                    par, i, g = back
                    q = 4 * par
                    xmaxc = pe.value_load(maxc[0:1, bass.ds(i, 1)], min_val=0, max_val=E)
                    need("silu", back)
                    message_sums(q, par, oh[:, par, :, :]).then_inc(S["agg"], 1)

                    def body(j):
                        pe.wait_ge(baton[p], at(pe, xb, 5))
                        hold(pe)
                        turn_onehots(q, xoh).then_inc(baton[p], 1)
                        pe.wait_ge(baton[p], at(pe, xb, 7))
                        hold(pe)
                        turn_features(q, xea).then_inc(baton[p], 1)
                        pe.wait_ge(baton[p], at(pe, xb, 9))
                        hold(pe)
                        messages(q, par, xm65).then_inc(baton[p], 1)
                        pe.wait_ge(baton[p], at(pe, xb, 16))
                        hold(pe)
                        message_sums(q, par, xoh).then_inc(baton[p], 1)
                    further(pe, p, xb, xmaxc, body)
                if front:
                    par = front[0]
                    need("ht", front)
                    for u in range(G):
                        ins = mm(pb(f + 1, D, u * D)[0:NT, :], hT[0:65, par, u * NT:(u + 1) * NT],
                                 m1w[:, 1, :], start=True, stop=True)
                    ins.then_inc(S["mm_y"], 1)
                if back:
                    par = back[0]
                    need("state", back)
                    for u in range(G):
                        ins = turn(pb(4 * par + 2, NT, u * NT)[0:65, :], c65[:, par, u, :], ident[0:NT, 0:NT])
                    ins.then_inc(S["tr"], 1)
                if front:
                    par = front[0]
                    pe.wait_ge(L["ea"][par], 5 * loaded(p, "ea", front[2]))
                    need("oht", front)
                    hold(pe)
                    turn_features(f, ea[:, par, :, :]).then_inc(S["tr_e"], 1)
                if back:
                    par = back[0]
                    need("ct", back)
                    mm(pb(4 * par + 3, G * NT)[0:D, :], mu[:, :], ctb[0:65, par, :], start=True, stop=True)\
                        .then_inc(S["mm"], 1)
                if front:
                    par = front[0]
                    pe.wait_ge(gathered[par], gathered_at(p, front[2]))
                    need("yt", front)
                    need("et", front)
                    messages(f, par, m65[:, par, :, :]).then_inc(S["mm_z"], 1)
                if back:
                    par = back[0]
                    need("usilu", back)
                    for u in range(G):
                        ins = mm(pb(4 * par, D, u * D)[0:NT, :], usT[:, par, u * NT:(u + 1) * NT], u2w[:, :],
                                 start=True, stop=True)
                    ins.then_inc(S["mm2"], 1)

            for p in range(1, NPASS):
                pass_written(pe, p - 1)
                pe.reg_mov(xb, 1)
                if p in SKEWED:
                    half = message_half if p == 8 else conv_half
                    skewed(pe, lambda front, back, tail: half(p, front, back, tail), p != 3)
                    continue
                with pe.Fori(0, GROUPS // 2) as i:
                    g = i * 2
                    xmaxc = pe.value_load(maxc[0:1, bass.ds(i, 1)], min_val=0, max_val=E)

                    def need(name, par):
                        pe.wait_ge(S[name], done(p, name, g, par))

                    def freed(name, par):
                        pe.wait_ge(S[name], before(p, name, g, par))

                    if p in (1, 2, 5, 6, 7):
                        width = {1: 65, 6: DH}.get(p, D)
                        rows, xrows = (m128, xm128) if p == 6 else (m65, xm65)

                        def sums_of(par, onehot, m, add):
                            q = 4 * par
                            for u in range(G):
                                c = u * width
                                ins = mm(pb(q + c // 512, width, c % 512)[0:NT, :], onehot[:, u, :], m[:, u, 0:width],
                                         start=not add, stop=not add or u == G - 1 or (c + width) % 512 == 0)
                            return ins

                        for par in range(2):
                            q = 4 * par
                            need("oh", par)
                            freed("ev", par)
                            if p >= 5:
                                pe.wait_ge(L["hs"][par], loaded(p, "hs", g))
                                for c in range(0, G * width, 512):
                                    cols = min(512, G * width - c)
                                    mm(pb(q + c // 512, cols)[0:NT, :], ident[0:NT, 0:NT], hsb[:, par, c:c + cols],
                                       start=True, stop=False)
                            pe.wait_ge(gathered[par], gathered_at(p, g))
                            sums_of(par, oh[:, par, :, :], rows[:, par, :, :], p >= 5).then_inc(S["agg"], 1)

                            def body(j):
                                pe.wait_ge(baton[p], at(pe, xb, 5))
                                hold(pe)
                                sums_of(par, xoh, xrows, False).then_inc(baton[p], 1)
                            further(pe, p, xb, xmaxc, body)

                    if p in (1, 2):
                        for par in range(2):
                            need("state", par)
                            pe.wait_ge(L["hs"][par], loaded(p, "hs", g))
                            freed("ct", par)
                            for u in range(G):
                                ins = turn(pb(4 * par + 1, NT, u * NT), c128[:, par, u, :], ident[0:NT, 0:NT])
                            ins.then_inc(S["tr"], 1)
                        for par in range(2):
                            need("ct", par)
                            freed("out" if p == 1 else "xadd", par)
                            bias = brow[f"s{p - 1}"][0:1, :, :].rearrange("p u f -> p (u f)")
                            hold(pe)
                            mm(pb(4 * par + 2, G * D)[0:NT, :], ones[0:1, 0:NT], bias, start=True, stop=False)
                            for u in range(G):
                                ins = mm(pb(4 * par + 2, D, u * D)[0:NT, :], ctb[:, par, u * NT:(u + 1) * NT],
                                         sage_w[p - 1][:, :], start=False, stop=u == G - 1)
                            ins.then_inc(S["mm"], 1)
                    elif p == 5:
                        for par in range(2):
                            need("state", par)
                            freed("ct", par)
                            hold(pe)
                            for u in range(G):
                                ins = turn(pb(4 * par + 1, NT, u * NT)[0:D, :], c65[:, par, u, 0:D], ident[0:NT, 0:NT])
                            ins.then_inc(S["tr"], 1)
                        for par in range(2):
                            need("ct", par)
                            freed("out", par)
                            bias = brow["g1"][0:1, :, :].rearrange("p u f -> p (u f)")
                            hold(pe)
                            mm(pb(4 * par + 2)[0:NT, :], ones[0:1, 0:NT], bias[:, 0:512], start=True, stop=False)
                            mm(pb(4 * par + 3, 128)[0:NT, :], ones[0:1, 0:NT], bias[:, 512:640], start=True, stop=False)
                            for u in range(G):
                                ins = mm(pb(4 * par + 2 + u // 4, DH, (u % 4) * DH)[0:NT, :],
                                         ctb[0:D, par, u * NT:(u + 1) * NT], g1t[:, :], start=False, stop=u >= 3)
                            ins.then_inc(S["mm"], 1)
                    elif p == 6:
                        for par in range(2):
                            need("state", par)
                            freed("out", par)
                            for u in range(G):
                                ins = turn(pb(4 * par + 2, NT, u * NT), c128[:, par, u, :], ident[0:NT, 0:NT])
                            ins.then_inc(S["tr"], 1)
                        for par in range(2):
                            need("ct", par)
                            freed("relu", par)
                            mm(pb(4 * par + 3, G * NT), g2t[:, :], ctb[:, par, :], start=True, stop=True).then_inc(S["mm"], 1)
                        for par in range(2):
                            need("relu", par)
                            for u in range(G):
                                ins = mm(pb(4 * par + 2, D, u * D)[0:NT, :], h6T[:, par, u * NT:(u + 1) * NT], g3t[:, :],
                                         start=True, stop=True)
                            ins.then_inc(S["mm2"], 1)
                    elif p == 7:
                        for par in range(2):
                            need("nrm", par)
                            freed("ct", par)
                            hold(pe)
                            for u in range(G):
                                ins = turn(pb(4 * par + 1, NT, u * NT)[0:D, :], w3[:, par, u, :], ident[0:NT, 0:NT])
                            ins.then_inc(S["tr"], 1)
                        for par in range(2):
                            need("ct", par)
                            freed("out", par)
                            hold(pe)
                            for u in range(G):
                                ins = mm(pb(4 * par + 2, D, u * D)[0:NT, :], ctb[0:D, par, u * NT:(u + 1) * NT],
                                         m1w[0:D, 0, :], start=True, stop=True)
                            ins.then_inc(S["mm"], 1)

        @block.scalar
        def _(act):
            fn = nc.scalar.activation
            act.preload_act_table_set("natural_log_exp_and_others")
            act.wait_ge(pool_c, POOL_CONSTS)
            for n in "abc":
                for par in range(2):
                    act.dma_start(prime_d[:, :], ident[0:16, 0:16]).then_inc(ST[n][par], 16)
                    act.wait_ge(ST[n][par], 16)
            for n in ACT_STAGES.split():
                act.sem_inc(S[n], 2)
            act.sem_inc(primed, 1)
            act.wait_ge(primed, 4)
            xb = act.alloc_register("xb_act")

            def conv_half(p, front, back, tail):
                def need(name, job):
                    act.wait_ge(S[name], done(p, name, job[2], job[0]))

                def store(name, job, buf, producer, table):
                    need(producer, job)
                    act.dma_start(tiles_of(table)[:, bass.ds(job[2] * G + job[0] * G, G), :], buf).then_inc(ST[name][job[0]], 16)

                if front:
                    par = front[0]
                    need("tr_h", front)
                    fn(hT[:, par, :], pb(4 * par, G * NT)[0:66, :], ACT.Copy).then_inc(S["ht"], 1)
                if tail:
                    par = tail[0]
                    need("cen", tail)
                    fn(w1[:, par, :, :], w0[:, par, :, :], ACT.Square).then_inc(S["sq"], 1)
                if front:
                    par = front[0]
                    need("tr_o", front)
                    fn(ohT[:, par, :], P[0:NT, (4 * par + 2) * 512:(4 * par + 2) * 512 + G * W], ACT.Copy).then_inc(S["oht"], 1)
                if front:
                    par = front[0]
                    need("mm_g", front)
                    fn(gS[:, par, 0:390], pb(4 * par, 390)[0:NT, :], ACT.Copy)
                    fn(gS[:, par, 390:650], pb(4 * par + 1, 260)[0:NT, :], ACT.Copy).then_inc(S["gt"], 1)
                if tail:
                    par = tail[0]
                    need("var", tail)
                    fn(small[:, par, 2, 0:G], small[:, par, 1, 0:G], ACT.Ln, bias=epsc[0:NT, 0:1], scale=1.0 / D)\
                        .then_inc(S["ln"], 1)
                    need("ln", tail)
                    fn(small[:, par, 3, 0:G], small[:, par, 2, 0:G], ACT.Exp, scale=-0.5).then_inc(S["rstd"], 1)
                if back:
                    par, i, g = back
                    xmaxc = act.value_load(maxc[0:1, bass.ds(i, 1)], min_val=0, max_val=E)
                    def body(j):
                        act.wait_ge(baton[p], at(act, xb, 9))
                        fn(ohT[:, par, :], P[0:NT, (4 * par + 2) * 512:(4 * par + 2) * 512 + G * W], ACT.Copy)\
                            .then_inc(baton[p], 1)
                        act.wait_ge(baton[p], at(act, xb, 17))
                        fn(rowm[:, par, 3, :], rowm[:, par, 2, :], ACT.Exp).then_inc(baton[p], 1)
                        act.wait_ge(baton[p], at(act, xb, 31))
                        fn(xs[:, 3:5, :], xs[:, 3:5, :], ACT.Exp).then_inc(baton[p], 1)
                    further(act, p, xb, xmaxc, body)
                    need("tr", back)
                    fn(ctb[:, par, :], pb(4 * par, G * NT), ACT.Copy).then_inc(S["ct"], 1)
                if front:
                    par = front[0]
                    need("sub", front)
                    fn(rowm[:, par, 3, :], rowm[:, par, 2, :], ACT.Exp).then_inc(S["exp"], 1)
                if tail:
                    store("a", tail, w3[:, tail[0], :, :], "nrm", OUTA[p])
                if back and p == 3:
                    par, i, g = back
                    need("mm", back)
                    act.wait_ge(ST["a"][par], stored_before(p, "a", g))
                    fn(w3[:, par, :, :], tiles(pb(4 * par + 1, G * D)[0:NT, :], D), ACT.Copy).then_inc(S["out"], 1)
                    store("a", back, w3[:, par, :, :], "out", OUTA[p])
                if back and p == 4:
                    store("b", back, w2[:, back[0], :, :], "xadd", OUTB[p])

            def message_half(p, front, back, tail):
                def need(name, job):
                    act.wait_ge(S[name], done(p, name, job[2], job[0]))

                if front:
                    par = front[0]
                    need("tr_h", front)
                    fn(hT[0:65, par, :], pb(4 * par, G * NT)[0:65, :], ACT.Copy).then_inc(S["ht"], 1)
                if tail:
                    par = tail[0]
                    need("cen", tail)
                    fn(w1[:, par, :, :], w0[:, par, :, :], ACT.Square).then_inc(S["sq"], 1)
                if back:
                    par, i, g = back
                    xmaxc = act.value_load(maxc[0:1, bass.ds(i, 1)], min_val=0, max_val=E)
                    def body(j):
                        act.wait_ge(baton[p], at(act, xb, 6))
                        fn(ohT[:, par, :], P[0:NT, (4 * par + 2) * 512:(4 * par + 2) * 512 + G * W], ACT.Copy)\
                            .then_inc(baton[p], 1)
                        act.wait_ge(baton[p], at(act, xb, 8))
                        fn(eT[:, par, :], P[0:D, (4 * par + 2) * 512:(4 * par + 2) * 512 + G * W], ACT.Copy)\
                            .then_inc(baton[p], 1)
                        act.wait_ge(baton[p], at(act, xb, 10))
                        fn(z1[:, par, :], pb(4 * par + 1, G * D), ACT.Abs).then_inc(baton[p], 1)
                        act.wait_ge(baton[p], at(act, xb, 11))
                        fn(z1[:, par, :], z1[:, par, :], ACT.Exp, scale=-1.0).then_inc(baton[p], 1)
                        act.wait_ge(baton[p], at(act, xb, 12))
                        fn(z2[:, par, :], z1[:, par, :], ACT.Ln, bias=epsc[:, 1:2]).then_inc(baton[p], 1)
                        act.wait_ge(baton[p], at(act, xb, 14))
                        fn(z1[:, par, :], z2[:, par, :], ACT.Exp).then_inc(baton[p], 1)
                    further(act, p, xb, xmaxc, body)
                if front:
                    par = front[0]
                    need("tr_o", front)
                    fn(ohT[:, par, :], P[0:NT, (4 * par + 2) * 512:(4 * par + 2) * 512 + G * W], ACT.Copy).then_inc(S["oht"], 1)
                if back:
                    par = back[0]
                    need("tr", back)
                    fn(ctb[0:65, par, :], pb(4 * par + 2, G * NT)[0:65, :], ACT.Copy).then_inc(S["ct"], 1)
                if front:
                    par = front[0]
                    need("mm_y", front)
                    fn(ysb[:, par, :], pb(4 * par + 1, G * D)[0:NT, :], ACT.Copy).then_inc(S["yt"], 1)
                if tail:
                    par = tail[0]
                    need("var", tail)
                    fn(small[:, par, 2, 0:G], small[:, par, 1, 0:G], ACT.Ln, bias=epsc[0:NT, 0:1], scale=1.0 / D)\
                        .then_inc(S["ln"], 1)
                    need("ln", tail)
                    fn(small[:, par, 3, 0:G], small[:, par, 2, 0:G], ACT.Exp, scale=-0.5).then_inc(S["rstd"], 1)
                if front:
                    par = front[0]
                    need("tr_e", front)
                    fn(eT[:, par, :], P[0:D, (4 * par + 2) * 512:(4 * par + 2) * 512 + G * W], ACT.Copy).then_inc(S["et"], 1)
                if back:
                    par = back[0]
                    need("ub", back)
                    fn(ue[:, par, :], uz[:, par, :], ACT.Abs).then_inc(S["uabs"], 1)
                    need("uabs", back)
                    fn(ue[:, par, :], ue[:, par, :], ACT.Exp, scale=-1.0).then_inc(S["u1"], 1)
                    need("u1", back)
                    fn(ue[:, par, :], ue[:, par, :], ACT.Ln, bias=epsc[0:D, 1:2]).then_inc(S["u2"], 1)
                if back:
                    par = back[0]
                    need("ulsig", back)
                    fn(ue[:, par, :], ue[:, par, :], ACT.Exp).then_inc(S["u3"], 1)
                if front:
                    par = front[0]
                    need("mm_z", front)
                    fn(z1[:, par, :], pb(4 * par + 1, G * D), ACT.Abs).then_inc(S["abs"], 1)
                if front:
                    par = front[0]
                    need("abs", front)
                    fn(z1[:, par, :], z1[:, par, :], ACT.Exp, scale=-1.0).then_inc(S["e1"], 1)
                    need("e1", front)
                    fn(z2[:, par, :], z1[:, par, :], ACT.Ln, bias=epsc[:, 1:2]).then_inc(S["e2"], 1)
                if tail:
                    par = tail[0]
                    need("xadd", tail)
                    act.dma_start(tiles_of(OUTB[p])[:, bass.ds(tail[2] * G + par * G, G), :], w3[:, par, :, :])\
                       .then_inc(ST["b"][par], 16)
                if front:
                    par = front[0]
                    need("lsig", front)
                    fn(z1[:, par, :], z2[:, par, :], ACT.Exp).then_inc(S["e3"], 1)

            for p in range(NPASS):
                if p:
                    pass_written(act, p - 1)
                    act.reg_mov(xb, 1)
                if p == 2:
                    fn(dinv[:, :], deg[:, :], ACT.Ln, bias=epsc[0:NT, 1:2]).then_inc(s_act, 1)
                    act.wait_ge(s_act, 1)
                    fn(dinv[:, :], dinv[:, :], ACT.Exp, scale=-0.5).then_inc(s_act, 1)
                if p in SKEWED:
                    half = message_half if p == 8 else conv_half
                    skewed(act, lambda front, back, tail: half(p, front, back, tail), p != 3)
                    continue
                with act.Fori(0, GROUPS // 2) as i:
                    g = i * 2
                    def need(name, par):
                        act.wait_ge(S[name], done(p, name, g, par))

                    def freed(name, par):
                        act.wait_ge(S[name], before(p, name, g, par))

                    def store(name, par, buf, producer, table):
                        need(producer, par)
                        act.dma_start(tiles_of(table)[:, bass.ds(g * G + par * G, G), :], buf).then_inc(ST[name][par], 16)

                    if p in (1, 2, 5, 6):
                        bank, rows = {1: (1, 128), 2: (1, 128), 5: (1, D), 6: (2, 128)}[p]
                        for par in range(2):
                            need("tr", par)
                            freed("mm", par)
                            fn(ctb[0:rows, par, :], pb(4 * par + bank, G * NT)[0:rows, :], ACT.Copy).then_inc(S["ct"], 1)
                    if p == 1:
                        for par in range(2):
                            need("mm", par)
                            act.wait_ge(ST["a"][par], stored_before(p, "a", g))
                            fn(w3[:, par, :, :], tiles(pb(4 * par + 2, G * D)[0:NT, :], D), ACT.Relu).then_inc(S["out"], 1)
                            store("a", par, w3[:, par, :, :], "out", OUTA[p])
                    if p == 5:
                        for par in range(2):
                            store("a", par, w3b[:, par, :, :], "out", OUTA[p])
                    if p == 6:
                        for par in range(2):
                            need("mm", par)
                            freed("mm2", par)
                            fn(h6T[:, par, :], pb(4 * par + 3, G * NT), ACT.Relu, bias=g2b[:, 0:1]).then_inc(S["relu"], 1)
                        for par in range(2):
                            store("a", par, w3[:, par, :, :], "out", OUTA[p])
                    if p == 7:
                        for par in range(2):
                            need("sub", par)
                            fn(w1[:, par, :, :], w1[:, par, :, :], ACT.Exp).then_inc(S["exp"], 1)
                    if p in (2, 4, 7):
                        for par in range(2):
                            store("b", par, w2[:, par, :, :], "xadd", OUTB[p])
                    if p in (0, 2, 4, 7, 8):
                        for par in range(2):
                            need("cen", par)
                            fn(w1[:, par, :, :], w0[:, par, :, :], ACT.Square).then_inc(S["sq"], 1)
                        for par in range(2):
                            need("var", par)
                            fn(small[:, par, 2, 0:G], small[:, par, 1, 0:G], ACT.Ln, bias=epsc[0:NT, 0:1], scale=1.0 / D)\
                                .then_inc(S["ln"], 1)
                        for par in range(2):
                            need("ln", par)
                            fn(small[:, par, 3, 0:G], small[:, par, 2, 0:G], ACT.Exp, scale=-0.5).then_inc(S["rstd"], 1)
                    if p in (0, 2, 4, 7):
                        for par in range(2):
                            store("a", par, w3[:, par, :, :], "nrm", OUTA[p])
                    if p == 7:
                        for par in range(2):
                            need("tr", par)
                            freed("mm", par)
                            fn(ctb[0:D, par, :], pb(4 * par + 1, G * NT)[0:D, :], ACT.Copy).then_inc(S["ct"], 1)
                        for par in range(2):
                            need("mm", par)
                            act.wait_ge(ST["c"][par], stored_before(p, "c", g))
                            fn(wc[:, par, :, :], tiles(pb(4 * par + 2, G * D)[0:NT, :], D), ACT.Copy).then_inc(S["out"], 1)
                            store("c", par, wc[:, par, :, :], "out", OUTC[p])

        @block.vector
        def _(dve):
            v = nc.vector
            k = 0

            def step(ins):
                nonlocal k
                k += 1
                ins.then_inc(s_dve, 1)
                dve.wait_ge(s_dve, k)

            def split(x, q, r, by):
                step(v.tensor_scalar(q[:, :], x[:, :], 1.0 / by, None, ALU.mult))
                step(v.tensor_copy(dwork[:, :], q[:, :]))
                step(v.tensor_copy(q[:, :], dwork[:, :]))
                step(v.scalar_tensor_tensor(r[:, :], q[:, :], -float(by), x[:, :], ALU.mult, ALU.add))
                step(v.tensor_scalar(c1[:, :], r[:, :], 0.0, None, ALU.is_lt))
                step(v.tensor_tensor(q[:, :], q[:, :], c1[:, :], ALU.subtract))
                step(v.scalar_tensor_tensor(r[:, :], c1[:, :], float(by), r[:, :], ALU.mult, ALU.add))
                step(v.tensor_scalar(c1[:, :], r[:, :], float(by), None, ALU.is_ge))
                step(v.tensor_tensor(q[:, :], q[:, :], c1[:, :], ALU.add))
                step(v.scalar_tensor_tensor(r[:, :], c1[:, :], -float(by), r[:, :], ALU.mult, ALU.add))

            dve.wait_ge(pool_c, POOL_CONSTS)
            step(v.tensor_copy(iota_f[:, :], iota_i[:, :]))
            step(v.tensor_scalar(base_f[:, :], iota_f[:, :], float(NT), None, ALU.mult))
            step(v.tensor_copy(tbase[:, :], tbase_i[:, :]))
            dve.wait_ge(s_list, 16)
            x0, x1, x2, c1 = hq
            step(v.tensor_copy(x0[:, :], dlist[:, :]))
            split(x0, x1, x2, NT)
            split(x1, x0, x2, LO)
            hi, lo = x0, x2
            with dve.Fori(0, E // CH // HB // 2) as t2:
                for kk in range(2):
                    cols = bass.ds(t2 * (2 * HB) + kk * HB, HB)
                    dve.wait_ge(q_used, 2 * t2 + (kk + 1))
                    for onehot, digit, n in ((ohh, hi, HI), (ohl, lo, LO)):
                        v.tensor_tensor(onehot[:, kk, :, :], iota_f[0:CH, 0:n].unsqueeze(1).broadcast_to([CH, HB, n]),
                                        digit[:, cols].unsqueeze(2).broadcast_to([CH, HB, n]), ALU.is_equal)\
                            .then_inc(q_ready, 1)
            dve.wait_ge(s_pe, 1)
            step(v.tensor_copy(cnt_s[:, :], pb(0, LO)[0:HI, :]))
            assert k == CNT_DONE
            dve.wait_ge(s_load, 16 * N_WEIGHT_LOADS)
            v.tensor_tensor(swrow[0:1, :, :], bvrow[0:1, :, 0, :], bvrow[0:1, :, 1, :], ALU.add).then_inc(s_sw, 1)
            dve.wait_ge(s_sw, 1)
            v.tensor_scalar(swrow[0:1, :, :], swrow[0:1, :, :], 0.5, None, ALU.mult).then_inc(w_dve, 1)
            dve.wait_ge(w_pe, 1)
            for l in range(2):
                v.tensor_copy(cwT[:, l, :, :, :], pb(6 + l, 260)[0:D, :].rearrange("p (k h f) -> p k h f", k=2, h=2))\
                    .then_inc(w_dve, 1)
            v.tensor_copy(g1t[:, :], pb(5, 128)[0:D, :]).then_inc(w_dve, 1)
            v.tensor_copy(g2t[:, :], pb(5, 128, 128)).then_inc(w_dve, 1)
            v.tensor_copy(g3t[:, :], pb(5, D, 256)).then_inc(w_dve, 1)
            v.tensor_copy(m2T[:, :], pb(5, 65, 320)[0:D, :]).then_inc(w_dve, 1)
            dve.wait_ge(w_pe, 2)
            v.tensor_scalar(qk[0:65, :, :, :], pb(6, 260)[0:65, :].rearrange("p (l h f) -> p l h f", l=2, h=2),
                            float(D) ** -0.5, None, ALU.mult).then_inc(w_dve, 1)
            v.tensor_copy(mu[:, :], pb(5, D)[0:65, :]).then_inc(w_dve, 1)
            v.tensor_scalar(vw[:, :, :], vw[:, :, :], 0.5, None, ALU.mult).then_inc(w_dve, 1)
            v.tensor_copy(sw[0:65, :, :], cw[:, :, 3, 0:D]).then_inc(w_dve, 1)
            dve.wait_ge(s_cnt, 48)
            step(v.reduce_max(maxc_f[:, :], crow[:, :].rearrange("p (i c) -> p i c", c=2 * G), AX))
            step(v.tensor_copy(maxc[:, :], maxc_f[:, :]))
            dve.wait_ge(s_pe, 2)
            step(v.tensor_copy(scol_i[:, :], pb(3, T // CH)[0:CH, :]))
            assert k == SCOL_DONE
            dve.wait_ge(s_win, 16 * 2 * (T // CH))
            step(v.tensor_copy(wsf[:, :, :], wdst[:, :, :]))
            step(v.tensor_tensor(drelw[:, :, 0:W - 1], wsf[:, :, 1:W], wsf[:, :, 0:W - 1], ALU.not_equal))
            step(v.tensor_scalar(flagw[:, :, 0, 1:W], drelw[:, :, 0:W - 1], -BIG, None, ALU.mult))
            step(v.tensor_scalar(flagw[:, :, 1, 0:W - 1], drelw[:, :, 0:W - 1], -BIG, None, ALU.mult))
            assert k == FLAG_DONE
            for c in range(T // CH):
                step(v.tensor_scalar(drelw[:, c, :], wsf[:, c, :], tbase[0:CH, c:c + 1], None, ALU.subtract))
            step(v.tensor_copy(wsf[:, :, :], wsrc[:, :, :]))
            assert k == WSF_DONE
            dve.wait_ge(s_pe, 3)
            step(v.tensor_copy(srcw[:, :], pb(4, T)))
            step(v.tensor_copy(drel[:, 0:T], pb(5, T)))
            dve.sem_inc(tables, 1)
            for n in DVE_STAGES.split():
                dve.sem_inc(S[n], 2)
            dve.sem_inc(primed, 1)
            dve.wait_ge(primed, 4)

            def by_node(table, tile0, f):
                return table[:, tile0].unsqueeze(2).broadcast_to([NT, G, f])

            def bias5(n):
                return bias_b[n][:, :].unsqueeze(1).broadcast_to([NT, G, D])

            def small5(par, row, f):
                return small[:, par, row, 0:G].unsqueeze(2).broadcast_to([NT, G, f])

            def heads(x, rows, f):
                return x.rearrange("p (h u) -> p u h", h=2).unsqueeze(3).broadcast_to([rows, G, 2, f])

            def both(x):
                return x.unsqueeze(2).broadcast_to([128, G, 2, 65])

            def onehots(into, rel):
                return v.tensor_tensor(into, iota_f[:, 0:NT].unsqueeze(1).broadcast_to([128, G, NT]),
                                       rel.unsqueeze(2).broadcast_to([128, G, NT]), ALU.is_equal)

            xb = dve.alloc_register("xb_dve")

            def job_helpers(p, job):
                par, i, g = job

                def baton_at(n):
                    dve.wait_ge(baton[p], at(dve, xb, n))

                def xonehots(par, n):
                    v.tensor_copy(xdf[:, :], xdst[:, :]).then_inc(baton[p], 1)
                    baton_at(n + 1)
                    v.tensor_tensor(xdf[:, :], xdf[:, :], base_f[:, bass.ds(g * G + par * G, G)], ALU.subtract)\
                        .then_inc(baton[p], 1)
                    baton_at(n + 2)
                    onehots(xoh[:, :, :], xdf[:, :]).then_inc(baton[p], 1)

                return baton_at, xonehots

            def conv_half(p, front, back, tail):
                def need(name, job):
                    dve.wait_ge(S[name], done(p, name, job[2], job[0]))

                def freed(name, job):
                    dve.wait_ge(S[name], before(p, name, job[2], job[0]))

                if front:
                    par, i, g = front
                    freed("tr_h", front)
                    v.tensor_copy(hs66[:, par, :, D + 1], hasedge[:, bass.ds(g * G + par * G, G)]).then_inc(S["he"], 1)
                if tail:
                    par = tail[0]
                    need("xadd", tail)
                    v.reduce_sum(small[:, par, 0, 0:G], w2[:, par, :, :], AX).then_inc(S["red"], 1)
                    need("red", tail)
                    v.scalar_tensor_tensor(w0[:, par, :, :], small5(par, 0, D), -1.0 / D, w2[:, par, :, :],
                                           ALU.mult, ALU.add).then_inc(S["cen"], 1)
                if back:
                    par = back[0]
                    q = 4 * par
                    need("tr_p", back)
                    v.tensor_tensor(pr[:, par, :, :, :], both(m65[:, par, :, :]),
                                    heads(pb(q + 1, 2 * G), 128, 65), ALU.mult).then_inc(S["wm"], 1)
                if tail:
                    par = tail[0]
                    need("sq", tail)
                    v.reduce_sum(small[:, par, 1, 0:G], w1[:, par, :, :], AX).then_inc(S["var"], 1)
                if back:
                    par, i, g = back
                    xmaxc = dve.value_load(maxc[0:1, bass.ds(i, 1)], min_val=0, max_val=E)
                    sums = [of_bank(q + 2, part, NT) for part in range(2)]
                    den = small[:, par, 5, :]
                    den2 = den.rearrange("p (h u) -> p u h", h=2)
                    cview = c128[:, par, :, :].rearrange("p u (h f) -> p u h f", h=2)
                    baton_at, xonehots = job_helpers(p, back)
                    need("agg", back)
                    freed("tr", back)
                    for part, (u0, u1) in enumerate(IN_BANKS):
                        ins = v.tensor_scalar(den2[:, u0:u1], sums[part][:, :, :, D], 1e-16, None, ALU.add)
                    ins.then_inc(S["den"], 1)
                    need("den", back)
                    v.reciprocal(den, den).then_inc(S["rec"], 1)
                    need("rec", back)
                    for part, (u0, u1) in enumerate(IN_BANKS):
                        ins = v.tensor_tensor(cview[:, u0:u1], sums[part][:, :, :, 0:D], heads(den, NT, D)[:, u0:u1], ALU.mult)
                    ins.then_inc(S["state_in"], 1)
                    need("state_in", back)
                    state = xstate[:, :].rearrange("p (u h f) -> p u h f", h=2, f=65)
                    xsum = xt[:, :].rearrange("p (u h f) -> p u h f", h=2, f=65)
                    mx = xs[:, 5, :]

                    def node_maxima(into, n):
                        v.tensor_scalar(xcol[:, 0, :], pb(q, 2 * G, 16), -1.0, None, ALU.is_lt).then_inc(baton[p], 1)
                        baton_at(n + 1)
                        v.tensor_tensor(xcol[:, 1, :], pb(q, 2 * G), xcol[:, 0, :], ALU.mult).then_inc(baton[p], 1)
                        baton_at(n + 3)
                        v.tensor_scalar(xs[:, 1, :], pb(q, 2 * G, 48)[0:NT, :], -FLOOR, FLOOR, ALU.mult, ALU.add)\
                            .then_inc(baton[p], 1)
                        baton_at(n + 4)
                        v.tensor_tensor(into, xs[:, 1, :], pb(q, 2 * G, 32)[0:NT, :], ALU.add).then_inc(baton[p], 1)
                        baton_at(n + 5)

                    def prepare():
                        for part, (u0, u1) in enumerate(IN_BANKS):
                            ins = v.tensor_copy(state[:, u0:u1], sums[part])
                        ins.then_inc(baton[p], 1)
                        baton_at(2)
                        node_maxima(mx, 2)

                    def body(j):
                        baton_at(2)
                        xonehots(par, 2)
                        baton_at(5)
                        v.tensor_scalar(xrf[:, :], xrow[:, :], -BIG, None, ALU.mult).then_inc(baton[p], 1)
                        baton_at(6)
                        for s in range(2):
                            v.tensor_tensor(xflag[:, s, 1 - s:W - s], xrf[:, 1:W], xrf[:, 0:W - 1],
                                            ALU.subtract).then_inc(baton[p], 1)
                            baton_at(7 + s)
                        baton_at(11)
                        for part, (u0, u1) in enumerate(IN_BANKS):
                            ins = v.tensor_tensor(pr[:, par, u0:u1, :, :], of_bank(q + 2, part, 128),
                                                  both(xm65[:, :, :])[:, u0:u1], ALU.mult)
                        ins.then_inc(baton[p], 1)
                        baton_at(12)
                        v.reduce_sum(al[:, par, :].rearrange("p (h u) -> p u h", h=2), pr[:, par, :, :, :], AX)\
                            .then_inc(baton[p], 1)
                        baton_at(14)
                        v.tensor_tensor_scan(rowm[:, par, 0, :], xflag[:, 0, :], pb(q, W)[0:2 * G, :], -BIG,
                                             ALU.add, ALU.max).then_inc(baton[p], 1)
                        baton_at(15)
                        v.tensor_tensor_scan(rowm[:, par, 1, W - 1::-1], xflag[:, 1, W - 1::-1],
                                             rowm[:, par, 0, W - 1::-1], -BIG, ALU.add, ALU.max)\
                            .then_inc(baton[p], 1)
                        baton_at(16)
                        v.tensor_tensor(rowm[:, par, 2, :], pb(q, W)[0:2 * G, :], rowm[:, par, 1, :],
                                        ALU.subtract).then_inc(baton[p], 1)
                        baton_at(19)
                        v.tensor_tensor(pr[:, par, :, :, :], both(xm65[:, :, :]), heads(pb(q + 1, 2 * G), 128, 65),
                                        ALU.mult).then_inc(baton[p], 1)
                        baton_at(22)
                        node_maxima(xs[:, 0, :], 22)
                        for part, (u0, u1) in enumerate(IN_BANKS):
                            ins = v.tensor_copy(xsum[:, u0:u1], sums[part])
                        ins.then_inc(baton[p], 1)
                        v.tensor_tensor(xs[:, 2, :], mx, xs[:, 0, :], ALU.max).then_inc(baton[p], 1)
                        baton_at(29)
                        v.tensor_tensor(xs[:, 3, :], mx, xs[:, 2, :], ALU.subtract).then_inc(baton[p], 1)
                        v.tensor_tensor(xs[:, 4, :], xs[:, 0, :], xs[:, 2, :], ALU.subtract).then_inc(baton[p], 1)
                        baton_at(32)
                        v.tensor_copy(mx, xs[:, 2, :]).then_inc(baton[p], 1)
                        baton_at(33)
                        v.tensor_tensor(state, state, heads(xs[:, 3, :], NT, 65), ALU.mult).then_inc(baton[p], 1)
                        v.tensor_tensor(xsum, xsum, heads(xs[:, 4, :], NT, 65), ALU.mult).then_inc(baton[p], 1)
                        baton_at(35)
                        v.tensor_tensor(state, state, xsum, ALU.add).then_inc(baton[p], 1)
                        baton_at(36)
                        v.tensor_scalar(den2, state[:, :, :, D], 1e-16, None, ALU.add).then_inc(baton[p], 1)
                        baton_at(37)
                        v.reciprocal(den, den).then_inc(baton[p], 1)
                        baton_at(38)
                        v.tensor_tensor(cview, state[:, :, :, 0:D], heads(den, NT, D), ALU.mult)\
                            .then_inc(baton[p], 1)
                        baton_at(39)
                    further(dve, p, xb, xmaxc, body, prepare)
                    dve.sem_inc(S["state"], 1)
                if front:
                    par = front[0]
                    need("exp_g", front)
                    dve.wait_ge(gathered[par], gathered_at(p, front[2]))
                    for part, (u0, u1) in enumerate(IN_BANKS):
                        ins = v.tensor_tensor(pr[:, par, u0:u1, :, :], of_bank(4 * par + 2, part, 128),
                                              both(m65[:, par, :, :])[:, u0:u1], ALU.mult)
                    ins.then_inc(S["prod"], 1)
                if front:
                    par = front[0]
                    need("prod", front)
                    v.reduce_sum(al[:, par, :].rearrange("p (h u) -> p u h", h=2), pr[:, par, :, :, :], AX)\
                        .then_inc(S["dot"], 1)
                if front:
                    par, i, g = front
                    f = 4 * par
                    need("tr_a", front)
                    dve.wait_ge(L["flag"][par], 2 * loaded(p, "flag", g))
                    v.tensor_tensor_scan(rowm[:, par, 0, :], flags[:, par, 0, :], pb(f, W)[0:2 * G, :], -BIG,
                                         ALU.add, ALU.max).then_inc(S["fwd"], 1)
                    need("fwd", front)
                    v.tensor_tensor_scan(rowm[:, par, 1, W - 1::-1], flags[:, par, 1, W - 1::-1],
                                         rowm[:, par, 0, W - 1::-1], -BIG, ALU.add, ALU.max).then_inc(S["seg"], 1)
                    need("seg", front)
                    v.tensor_tensor(rowm[:, par, 2, :], pb(f, W)[0:2 * G, :], rowm[:, par, 1, :],
                                    ALU.subtract).then_inc(S["sub"], 1)
                if tail:
                    par, i, g = tail
                    need("rstd", tail)
                    v.tensor_tensor(small[:, par, 3, 0:G], small[:, par, 3, 0:G], dinv[:, bass.ds(g * G + par * G, G)],
                                    ALU.mult).then_inc(S["rsc"], 1)
                    need("rsc", tail)
                    dve.wait_ge(ST["a"][par], stored_before(p, "a", g))
                    v.scalar_tensor_tensor(w3[:, par, :, :], w0[:, par, :, :], 0.0, small5(par, 3, D),
                                           ALU.max, ALU.mult).then_inc(S["nrm"], 1)
                if back:
                    par, i, g = back
                    onehots(oh[:, par, :, :], drel[:, bass.ds(g * G + (2 + par) * G, G)]).then_inc(S["oh"], 1)
                    if p == 4:
                        need("mm", back)
                        dve.wait_ge(L["x"][par], loaded(p, "x", g))
                        dve.wait_ge(ST["b"][par], stored_before(p, "b", g))
                        v.tensor_tensor(w2[:, par, :, :], tiles(pb(q + 1, G * D)[0:NT, :], D),
                                        xres[:, par, :, :], ALU.add).then_inc(S["xadd"], 1)
                hold(dve)

            def message_half(p, front, back, tail):
                def need(name, job):
                    dve.wait_ge(S[name], done(p, name, job[2], job[0]))

                def freed(name, job):
                    dve.wait_ge(S[name], before(p, name, job[2], job[0]))

                if tail:
                    par = tail[0]
                    need("pre", tail)
                    v.reduce_sum(small[:, par, 0, 0:G], w2[:, par, :, :], AX).then_inc(S["red"], 1)
                    need("red", tail)
                    v.scalar_tensor_tensor(w0[:, par, :, :], small5(par, 0, D), -1.0 / D, w2[:, par, :, :],
                                           ALU.mult, ALU.add).then_inc(S["cen"], 1)
                if back:
                    par, i, g = back
                    q = 4 * par
                    xmaxc = dve.value_load(maxc[0:1, bass.ds(i, 1)], min_val=0, max_val=E)
                    sums = tiles(pb(q, G * 65)[0:NT, :], 65)
                    baton_at, xonehots = job_helpers(p, back)
                    need("agg", back)
                    freed("tr", back)
                    v.tensor_copy(c65[:, par, :, :], sums).then_inc(S["ev"], 1)
                    need("ev", back)
                    def body(j):
                        baton_at(2)
                        xonehots(par, 2)
                        baton_at(13)
                        v.scalar_tensor_tensor(z2[:, par, :], pb(q + 1, G * D), 0.0, z2[:, par, :],
                                               ALU.min, ALU.subtract).then_inc(baton[p], 1)
                        baton_at(15)
                        v.tensor_tensor(sg[:, par, :, 0:D], tiles(pb(q + 1, G * D), D), tiles(z1[:, par, :], D),
                                        ALU.mult).then_inc(baton[p], 1)
                        baton_at(17)
                        v.tensor_tensor(c65[:, par, :, :], c65[:, par, :, :], sums, ALU.add)\
                            .then_inc(baton[p], 1)
                        baton_at(18)
                    further(dve, p, xb, xmaxc, body)
                    dve.sem_inc(S["state"], 1)
                    onehots(oh[:, par, :, :], drel[:, bass.ds(g * G + (2 + par) * G, G)]).then_inc(S["oh"], 1)
                if tail:
                    par = tail[0]
                    need("sq", tail)
                    v.reduce_sum(small[:, par, 1, 0:G], w1[:, par, :, :], AX).then_inc(S["var"], 1)
                if back:
                    par = back[0]
                    need("mm", back)
                    v.tensor_scalar(uz[:, par, :], pb(q + 3, G * NT)[0:D, :], u1b[:, 0:1], None, ALU.add).then_inc(S["ub"], 1)
                if tail:
                    par, i, g = tail
                    need("rstd", tail)
                    v.tensor_tensor(w0[:, par, :, :], w0[:, par, :, :], small5(par, 3, D), ALU.mult).then_inc(S["nrm"], 1)
                    need("nrm", tail)
                    v.tensor_tensor(w1[:, par, :, :], w0[:, par, :, :], bias5("gamma"), ALU.mult).then_inc(S["gam"], 1)
                if back:
                    par = back[0]
                    need("u2", back)
                    v.scalar_tensor_tensor(ue[:, par, :], uz[:, par, :], 0.0, ue[:, par, :],
                                           ALU.min, ALU.subtract).then_inc(S["ulsig"], 1)
                if tail:
                    par, i, g = tail
                    need("gam", tail)
                    v.tensor_tensor(w0[:, par, :, :], w1[:, par, :, :], bias5("beta"), ALU.add).then_inc(S["bet"], 1)
                    need("bet", tail)
                    dve.wait_ge(L["x"][par], loaded(p, "x", g))
                    dve.wait_ge(ST["b"][par], stored_before(p, "b", g))
                    v.tensor_tensor(w3[:, par, :, :], w0[:, par, :, :], xres[:, par, :, :], ALU.add).then_inc(S["xadd"], 1)
                if back:
                    par = back[0]
                    need("u3", back)
                    freed("mm2", back)
                    v.tensor_tensor(usT[0:D, par, :], uz[:, par, :], ue[:, par, :], ALU.mult).then_inc(S["usilu"], 1)
                if front:
                    par = front[0]
                    need("e2", front)
                    v.scalar_tensor_tensor(z2[:, par, :], pb(4 * par + 1, G * D), 0.0, z2[:, par, :],
                                           ALU.min, ALU.subtract).then_inc(S["lsig"], 1)
                if back:
                    par, i, g = back
                    need("mm2", back)
                    dve.wait_ge(L["hr"][par], loaded(p, "hr", g))
                    v.tensor_tensor(w2[:, par, :, :], tiles(pb(q, G * D)[0:NT, :], D),
                                    tiles(hsb[:, par, 0:G * D], D), ALU.add).then_inc(S["pre"], 1)
                if front:
                    par = front[0]
                    need("e3", front)
                    v.tensor_tensor(sg[:, par, :, 0:D], tiles(pb(4 * par + 1, G * D), D), tiles(z1[:, par, :], D),
                                    ALU.mult).then_inc(S["silu"], 1)
                hold(dve)

            for p in range(NPASS):
                if p:
                    dve.wait_ge(S["oh"], start(p, "oh"))
                    for par in range(2):
                        onehots(oh[:, par, :, :], drel[:, par * G:(par + 1) * G]).then_inc(S["oh"], 1)
                    pass_written(dve, p - 1)
                    dve.reg_mov(xb, 1)
                if p == 2:
                    v.tensor_scalar(hasedge[:, :], deg[:, :], 0.0, None, ALU.is_gt).then_inc(s_sw, 1)
                    dve.wait_ge(s_sw, 2)
                    dve.wait_ge(s_act, 2)
                if p in SKEWED:
                    half = message_half if p == 8 else conv_half
                    skewed(dve, lambda front, back, tail: half(p, front, back, tail), p != 3)
                    continue
                with dve.Fori(0, GROUPS // 2) as i:
                    g = i * 2
                    if p:
                        xmaxc = dve.value_load(maxc[0:1, bass.ds(i, 1)], min_val=0, max_val=E)

                    def need(name, par):
                        dve.wait_ge(S[name], done(p, name, g, par))

                    def freed(name, par):
                        dve.wait_ge(S[name], before(p, name, g, par))

                    def tile0(par):
                        return bass.ds(g * G + par * G, G)

                    def baton_at(n):
                        dve.wait_ge(baton[p], at(dve, xb, n))

                    def xonehots(par, n):
                        v.tensor_copy(xdf[:, :], xdst[:, :]).then_inc(baton[p], 1)
                        baton_at(n + 1)
                        v.tensor_tensor(xdf[:, :], xdf[:, :], base_f[:, tile0(par)], ALU.subtract).then_inc(baton[p], 1)
                        baton_at(n + 2)
                        onehots(xoh[:, :, :], xdf[:, :]).then_inc(baton[p], 1)

                    def next_onehots():
                        for par in range(2):
                            need("agg", par)
                            onehots(oh[:, par, :, :], drel[:, bass.ds(g * G + (2 + par) * G, G)]).then_inc(S["oh"], 1)

                    if p == 1:
                        for par in range(2):
                            sums = tiles(pb(4 * par, G * 65)[0:NT, :], 65)
                            inv = invdeg[:, tile0(par)]

                            def mean(rows, signal, sem_of):
                                hold(dve)
                                signal(v.tensor_copy(deg[:, tile0(par)], rows[:, :, D]), "deg")
                                signal(v.tensor_scalar(inv, deg[:, tile0(par)], 1.0, None, ALU.max), "max")
                                hold(dve)
                                signal(v.reciprocal(inv, inv), "rec")
                                signal(v.tensor_tensor(c128[:, par, :, 0:D], rows[:, :, 0:D],
                                                       by_node(invdeg, tile0(par), D), ALU.mult), "ev")

                            def main_signal(ins, name):
                                ins.then_inc(S[name], 1)
                                need(name, par)

                            need("agg", par)
                            freed("tr", par)
                            mean(sums, main_signal, None)
                            state = tiles(xstate[:, 0:G * 65], 65)

                            def prepare():
                                v.tensor_copy(state, sums).then_inc(baton[p], 1)
                                baton_at(1)

                            def body(j):
                                baton_at(2)
                                xonehots(par, 2)
                                baton_at(6)
                                v.tensor_tensor(state, state, sums, ALU.add).then_inc(baton[p], 1)
                                baton_at(7)
                                steps = [7]

                                def x_signal(ins, name):
                                    steps[0] += 1
                                    ins.then_inc(baton[p], 1)
                                    baton_at(steps[0])
                                mean(state, x_signal, None)
                            further(dve, p, xb, xmaxc, body, prepare)
                            dve.sem_inc(S["state"], 1)
                        next_onehots()

                    if p in (2, 5, 6, 7):
                        width = DH if p == 6 else D
                        scale = invdeg if p == 2 else dinv
                        for par in range(2):
                            q = 4 * par
                            sums = tiles(P[0:NT, q * 512:q * 512 + G * width], width)
                            into = c65[:, par, :, 0:D] if p in (5, 7) else c128[:, par, :, 0:width]
                            need("agg", par)
                            if p != 7:
                                freed("tr", par)
                            v.tensor_tensor(into, sums, by_node(scale, tile0(par), width), ALU.mult).then_inc(S["ev"], 1)
                            need("ev", par)

                            def body(j):
                                xsum = tiles(xt[:, 0:G * width], width)
                                baton_at(2)
                                xonehots(par, 2)
                                baton_at(6)
                                v.tensor_tensor(xsum, sums, by_node(scale, tile0(par), width), ALU.mult)\
                                    .then_inc(baton[p], 1)
                                baton_at(7)
                                v.tensor_tensor(into, into, xsum, ALU.add).then_inc(baton[p], 1)
                                baton_at(8)
                            further(dve, p, xb, xmaxc, body)
                            dve.sem_inc(S["state"], 1)
                        next_onehots()

                    if p == 5:
                        for par in range(2):
                            need("mm", par)
                            dve.wait_ge(ST["a"][par], stored_before(p, "a", g))
                            wide = tiles(P[0:NT, (4 * par + 2) * 512:(4 * par + 2) * 512 + G * DH], DH)
                            v.scalar_tensor_tensor(w3b[:, par, :, :], wide, 0.0, by_node(dinv, tile0(par), DH),
                                                   ALU.max, ALU.mult).then_inc(S["out"], 1)
                    if p == 6:
                        for par in range(2):
                            need("mm2", par)
                            dve.wait_ge(ST["a"][par], stored_before(p, "a", g))
                            v.tensor_tensor(w3[:, par, :, :], tiles(pb(4 * par + 2, G * D)[0:NT, :], D),
                                            by_node(dinv, tile0(par), D), ALU.mult).then_inc(S["out"], 1)
                    if p == 7:
                        for par in range(2):
                            v.tensor_tensor(w1[:, par, :, :], c65[:, par, :, 0:D], bias5("g3"), ALU.add).then_inc(S["pre"], 1)
                        for par in range(2):
                            need("pre", par)
                            v.reduce_max(small[:, par, 4, 0:G], w1[:, par, :, :], AX).then_inc(S["max"], 1)
                        for par in range(2):
                            need("max", par)
                            v.tensor_tensor(w1[:, par, :, :], w1[:, par, :, :], small5(par, 4, D), ALU.subtract)\
                                .then_inc(S["sub"], 1)
                        for par in range(2):
                            need("exp", par)
                            v.reduce_sum(small[:, par, 5, 0:G], w1[:, par, :, :], AX).then_inc(S["den"], 1)
                        for par in range(2):
                            need("den", par)
                            v.reciprocal(small[:, par, 5, 0:G], small[:, par, 5, 0:G]).then_inc(S["rec"], 1)
                        for par in range(2):
                            need("rec", par)
                            v.tensor_tensor(w0[:, par, :, :], w1[:, par, :, :], small5(par, 5, D), ALU.mult)\
                                .then_inc(S["prob"], 1)
                        for par in range(2):
                            need("prob", par)
                            dve.wait_ge(L["x"][par], loaded(p, "x", g))
                            dve.wait_ge(ST["b"][par], stored_before(p, "b", g))
                            v.tensor_tensor(w2[:, par, :, :], w0[:, par, :, :], xres[:, par, :, :], ALU.add)\
                                .then_inc(S["xadd"], 1)

                    if p == 2:
                        for par in range(2):
                            need("mm", par)
                            dve.wait_ge(L["x"][par], loaded(p, "x", g))
                            dve.wait_ge(ST["b"][par], stored_before(p, "b", g))
                            v.tensor_tensor(w2[:, par, :, :], tiles(pb(4 * par + 2, G * D)[0:NT, :], D),
                                            xres[:, par, :, :], ALU.add).then_inc(S["xadd"], 1)

                    if p in (0, 2, 4, 7, 8):
                        rows = xres if p == 0 else w2
                        for par in range(2):
                            if p == 0:
                                dve.wait_ge(L["x"][par], loaded(p, "x", g))
                            else:
                                need("pre" if p == 8 else "xadd", par)
                            v.reduce_sum(small[:, par, 0, 0:G], rows[:, par, :, :], AX).then_inc(S["red"], 1)
                        for par in range(2):
                            need("red", par)
                            v.scalar_tensor_tensor(w0[:, par, :, :], small5(par, 0, D), -1.0 / D, rows[:, par, :, :],
                                                   ALU.mult, ALU.add).then_inc(S["cen"], 1)
                        for par in range(2):
                            need("sq", par)
                            v.reduce_sum(small[:, par, 1, 0:G], w1[:, par, :, :], AX).then_inc(S["var"], 1)
                        if p == 4:
                            for par in range(2):
                                need("rstd", par)
                                v.tensor_tensor(small[:, par, 3, 0:G], small[:, par, 3, 0:G], dinv[:, tile0(par)],
                                                ALU.mult).then_inc(S["rsc"], 1)
                        for par in range(2):
                            need("rsc" if p == 4 else "rstd", par)
                            if p == 8:
                                v.tensor_tensor(w0[:, par, :, :], w0[:, par, :, :], small5(par, 3, D), ALU.mult)\
                                    .then_inc(S["nrm"], 1)
                            else:
                                dve.wait_ge(ST["a"][par], stored_before(p, "a", g))
                                v.scalar_tensor_tensor(w3[:, par, :, :], w0[:, par, :, :], 0.0, small5(par, 3, D),
                                                       ALU.max, ALU.mult).then_inc(S["nrm"], 1)
                    hold(dve)


NPASS = 9
PE_STAGES = "tr mm mm2 agg tr_h tr_o mm_g exp_g tr_a tr_p mm_y tr_e mm_z"
ACT_STAGES = "ct out relu exp ht oht gt yt et abs uabs e1 e2 e3 u1 u2 u3 sq ln rstd"
DVE_STAGES = ("oh he ev state state_in deg max rec den xadd prod dot fwd seg sub wm pre prob rsc red cen var nrm gam bet "
              "lsig silu ub ulsig usilu")
POOL_CONSTS = 22
CNT_DONE, SCOL_DONE, FLAG_DONE, WSF_DONE = 25, 28, 32, 37
W_DVE = 11
N_WEIGHT_LOADS = 46


def kernel(**inputs):
    import numpy as _np
    import concourse.bacc as _bacc
    from concourse import mybir as _mybir
    from concourse.bass_utils import run_bass_kernel_spmd as _run

    nc = _bacc.Bacc("TRN2", target_bir_lowering=False, num_devices=1)
    arrays, args = {}, {}
    for name in sorted(inputs):
        x = _np.ascontiguousarray(inputs[name])
        arrays[f"in_{name}_dram"] = x
        args[name] = nc.dram_tensor(f"in_{name}_dram", x.shape, _mybir.dt.from_np(x.dtype), kind="ExternalInput").ap()
    out = nc.dram_tensor("out_0_dram", (N, D), F32, kind="ExternalOutput").ap()
    build(nc, args, out)
    r = _run(nc, [arrays], core_ids=[0])
    return r.results[0]["out_0_dram"]
```
